# Optimizing a Trainium2 kernel written in Bass

```python
import numpy as np
import jax
import jax.numpy as jnp

def _softmax(x, axis=-1):
    return jax.nn.softmax(x, axis=axis)
def _gelu(x):
    return jax.nn.gelu(x, approximate=True)
def _silu(x):
    return jax.nn.silu(x)
def _sigmoid(x):
    return jax.nn.sigmoid(x)
def _layernorm(x, axis=-1, eps=1e-5):
    m = jnp.mean(x, axis=axis, keepdims=True)
    v = jnp.var(x, axis=axis, keepdims=True)
    return (x - m) / jnp.sqrt(v + eps)
def _scatter_add(tgt, idx, src, axis=0):
    return tgt.at[idx].add(src)
def _segment_sum(src, seg, n):
    return jax.ops.segment_sum(src, seg, n)

kernel_name = 'mk_adj_ffn_d2_adj_256_33987d'

def setup_inputs(seed: int = 0):
    np.random.seed(seed)
    _w = jnp.asarray
    def _rec_inputs():
        import jax
        import jax.numpy as jnp
        _gk = jax.random.key(seed)
        x = -0.0002928 + 1 * jax.random.normal(jax.random.fold_in(_gk, 1), (64, 256, 256), jnp.float32)
        _a = jax.random.bernoulli(jax.random.fold_in(_gk, 2), 0.03125, (64, 256, 256))
        _af = _a.astype(jnp.float32)
        adj = _af
        return x, adj
    x, adj = _rec_inputs()
    def _L0_gnn_setup():
        import jax, jax.numpy as jnp
        import numpy as np
        B, N, D = (4, 4096, 256)
        DENSITY = 32.0 / N
        key = jax.random.key(seed)
        kx, ka, k1, k2, k3, k4 = jax.random.split(key, 6)
        x = jax.random.normal(kx, (B, N, D), dtype=jnp.float32)
        adj = (jax.random.uniform(ka, (B, N, N)) < DENSITY).astype(jnp.float32)
        scale = 0.02
        theta = scale * jax.random.normal(k1, (D, D), dtype=jnp.float32)
        W_h = scale * jax.random.normal(k2, (D, D), dtype=jnp.float32)
        W_t = scale * jax.random.normal(k3, (D, D), dtype=jnp.float32)
        b_t = scale * jax.random.normal(k4, (D,), dtype=jnp.float32)
        return {'x': x, 'adj': adj, 'theta': theta, 'W_h': W_h, 'W_t': W_t, 'b_t': b_t}
    _L0_gnn_all = _L0_gnn_setup()
    _L0_gnn_in = {k: v for k, v in _L0_gnn_all.items() if k in ('theta', 'W_h', 'W_t', 'b_t', )}
    del _L0_gnn_all

    def _L0_ffn_setup():
        import jax, jax.numpy as jnp
        import numpy as np
        B, T, D, H, L = (16, 4096, 256, 256, 2)

        def _lstm(x, W_ih, W_hh, b_ih, b_hh):
            x_proj = jnp.einsum('btd,gd->btg', x, W_ih) + b_ih + b_hh
            h0 = jnp.zeros((x.shape[0], W_hh.shape[1]), x.dtype)
            c0 = jnp.zeros_like(h0)

            def step(carry, xp):
                h, c = carry
                gates = xp + h @ W_hh.T
                i, f, g, o = jnp.split(gates, 4, axis=-1)
                c = jax.nn.sigmoid(f) * c + jax.nn.sigmoid(i) * jnp.tanh(g)
                h = jax.nn.sigmoid(o) * jnp.tanh(c)
                return ((h, c), h)
            _, hs = jax.lax.scan(step, (h0, c0), jnp.swapaxes(x_proj, 0, 1))
            return jnp.swapaxes(hs, 0, 1)
        key = jax.random.key(seed)
        ks = jax.random.split(key, 9)
        s = 1.0 / np.sqrt(H)
        u = lambda k, shape: jax.random.uniform(k, shape, jnp.float32, -s, s)
        return {'x': jax.random.normal(ks[0], (B, T, D), jnp.float32), 'W_ih': u(ks[1], (4 * H, D)), 'W_hh': u(ks[2], (4 * H, H)), 'b_ih': u(ks[3], (4 * H,)), 'b_hh': u(ks[4], (4 * H,)), 'W_lin': u(ks[5], (L, H)), 'b_lin': u(ks[6], (L,)), 'fw_att': jnp.full((1, H), 0.001, jnp.float32), 'bw_att': jnp.full((1, H), 0.001, jnp.float32)}
    _L0_ffn_all = _L0_ffn_setup()
    _L0_ffn_in = {k: v for k, v in _L0_ffn_all.items() if k in ('W_ih', 'W_hh', 'b_ih', 'b_hh', 'W_lin', 'b_lin', 'fw_att', 'bw_att', )}
    del _L0_ffn_all

    def _L1_gnn_setup():
        import jax, jax.numpy as jnp
        import numpy as np
        B, N, F_IN, F_OUT = (8, 2048, 256, 256)
        key = jax.random.key(seed)
        k1, k2, k3, k4 = jax.random.split(key, 4)
        x = jax.random.normal(k1, (B, N, F_IN), dtype=jnp.float32)
        adj = jax.random.uniform(k2, (B, N, N), dtype=jnp.float32)
        W = jax.random.normal(k3, (F_IN, F_OUT), dtype=jnp.float32) * (1.0 / np.sqrt(F_IN))
        b = jax.random.normal(k4, (F_OUT,), dtype=jnp.float32)
        return {'x': x, 'adj': adj, 'W': W, 'b': b}
    _L1_gnn_all = _L1_gnn_setup()
    _L1_gnn_in = {k: v for k, v in _L1_gnn_all.items() if k in ('W', 'b', )}
    del _L1_gnn_all

    def _L1_ffn_setup():
        import jax, jax.numpy as jnp
        import numpy as np
        B, S, D_MODEL, FFN, P = (8, 4096, 256, 1024, 8)
        BLK = 256
        key = jax.random.key(seed)
        ks = jax.random.split(key, 12)
        x = jax.random.normal(ks[0], (B, S, D_MODEL), jnp.float32)
        Wt = 0.05 * jax.random.normal(ks[1], (FFN, D_MODEL), jnp.float32)
        bt = 0.05 * jax.random.normal(ks[2], (FFN,), jnp.float32)
        sl_cvx = 1.0 + 0.1 * jax.random.normal(ks[3], (FFN, P), jnp.float32)
        of_cvx = 0.1 * jax.random.normal(ks[4], (FFN, P), jnp.float32)
        sl_ccv = 1.0 + 0.1 * jax.random.normal(ks[5], (FFN, P), jnp.float32)
        of_ccv = 0.1 * jax.random.normal(ks[6], (FFN, P), jnp.float32)
        alpha = jnp.zeros((FFN,), jnp.float32)
        Wc = jax.random.normal(ks[7], (D_MODEL, FFN), jnp.float32) / np.sqrt(D_MODEL)
        bc = jnp.zeros((FFN,), jnp.float32)
        Wg = 0.01 * jax.random.normal(ks[8], (D_MODEL, FFN), jnp.float32)
        bg = 2.0 * jnp.ones((FFN,), jnp.float32)
        Wd = jax.random.normal(ks[9], (FFN, D_MODEL), jnp.float32) / np.sqrt(FFN)
        bd = jnp.zeros((D_MODEL,), jnp.float32)
        return {'x': x, 'Wt': Wt, 'bt': bt, 'sl_cvx': sl_cvx, 'of_cvx': of_cvx, 'sl_ccv': sl_ccv, 'of_ccv': of_ccv, 'alpha': alpha, 'Wc': Wc, 'bc': bc, 'Wg': Wg, 'bg': bg, 'Wd': Wd, 'bd': bd}
    _L1_ffn_all = _L1_ffn_setup()
    _L1_ffn_in = {k: v for k, v in _L1_ffn_all.items() if k in ('Wt', 'bt', 'sl_cvx', 'of_cvx', 'sl_ccv', 'of_ccv', 'alpha', 'Wc', 'bc', 'Wg', 'bg', 'Wd', 'bd', )}
    del _L1_ffn_all

    return {
        "x": x,
        "adj": adj,
        "L0_gnn_theta": _L0_gnn_in["theta"],
        "L0_gnn_W_h": _L0_gnn_in["W_h"],
        "L0_gnn_W_t": _L0_gnn_in["W_t"],
        "L0_gnn_b_t": _L0_gnn_in["b_t"],
        "L0_ffn_W_ih": _L0_ffn_in["W_ih"],
        "L0_ffn_W_hh": _L0_ffn_in["W_hh"],
        "L0_ffn_b_ih": _L0_ffn_in["b_ih"],
        "L0_ffn_b_hh": _L0_ffn_in["b_hh"],
        "L0_ffn_W_lin": _L0_ffn_in["W_lin"],
        "L0_ffn_b_lin": _L0_ffn_in["b_lin"],
        "L0_ffn_fw_att": _L0_ffn_in["fw_att"],
        "L0_ffn_bw_att": _L0_ffn_in["bw_att"],
        "L1_gnn_W": _L1_gnn_in["W"],
        "L1_gnn_b": _L1_gnn_in["b"],
        "L1_ffn_Wt": _L1_ffn_in["Wt"],
        "L1_ffn_bt": _L1_ffn_in["bt"],
        "L1_ffn_sl_cvx": _L1_ffn_in["sl_cvx"],
        "L1_ffn_of_cvx": _L1_ffn_in["of_cvx"],
        "L1_ffn_sl_ccv": _L1_ffn_in["sl_ccv"],
        "L1_ffn_of_ccv": _L1_ffn_in["of_ccv"],
        "L1_ffn_alpha": _L1_ffn_in["alpha"],
        "L1_ffn_Wc": _L1_ffn_in["Wc"],
        "L1_ffn_bc": _L1_ffn_in["bc"],
        "L1_ffn_Wg": _L1_ffn_in["Wg"],
        "L1_ffn_bg": _L1_ffn_in["bg"],
        "L1_ffn_Wd": _L1_ffn_in["Wd"],
        "L1_ffn_bd": _L1_ffn_in["bd"],
    }

def reference(x, adj, L0_gnn_theta, L0_gnn_W_h, L0_gnn_W_t, L0_gnn_b_t, L0_ffn_W_ih, L0_ffn_W_hh, L0_ffn_b_ih, L0_ffn_b_hh, L0_ffn_W_lin, L0_ffn_b_lin, L0_ffn_fw_att, L0_ffn_bw_att, L1_gnn_W, L1_gnn_b, L1_ffn_Wt, L1_ffn_bt, L1_ffn_sl_cvx, L1_ffn_of_cvx, L1_ffn_sl_ccv, L1_ffn_of_ccv, L1_ffn_alpha, L1_ffn_Wc, L1_ffn_bc, L1_ffn_Wg, L1_ffn_bg, L1_ffn_Wd, L1_ffn_bd):
    import jax
    import jax.numpy as jnp
    def _L0_gnn_ref(x, adj, theta, W_h, W_t, b_t):
        import jax, jax.numpy as jnp
        import numpy as np
        B, N, D = (4, 4096, 256)
        DENSITY = 32.0 / N
        in_degrees = jnp.sum(jnp.abs(adj), axis=-1)
        norm = ((in_degrees + 1e-06) ** (-0.5))[..., None]
        f_hom = jnp.einsum('bnd,de->bne', x, theta) * norm
        f_hom = jnp.einsum('bnm,bmd->bnd', adj, f_hom) * norm
        f_het = jnp.einsum('bnd,de->bne', x, W_h)
        gate = jax.nn.sigmoid(jnp.einsum('bnd,de->bne', x, W_t) + b_t)
        out = gate * f_hom + (1.0 - gate) * f_het
        return jax.nn.elu(out)

    def _L0_ffn_ref(x, W_ih, W_hh, b_ih, b_hh, W_lin, b_lin, fw_att, bw_att):
        import jax, jax.numpy as jnp
        import numpy as np
        B, T, D, H, L = (16, 4096, 256, 256, 2)

        def _lstm(x, W_ih, W_hh, b_ih, b_hh):
            x_proj = jnp.einsum('btd,gd->btg', x, W_ih) + b_ih + b_hh
            h0 = jnp.zeros((x.shape[0], W_hh.shape[1]), x.dtype)
            c0 = jnp.zeros_like(h0)

            def step(carry, xp):
                h, c = carry
                gates = xp + h @ W_hh.T
                i, f, g, o = jnp.split(gates, 4, axis=-1)
                c = jax.nn.sigmoid(f) * c + jax.nn.sigmoid(i) * jnp.tanh(g)
                h = jax.nn.sigmoid(o) * jnp.tanh(c)
                return ((h, c), h)
            _, hs = jax.lax.scan(step, (h0, c0), jnp.swapaxes(x_proj, 0, 1))
            return jnp.swapaxes(hs, 0, 1)
        lstm_out = _lstm(x, W_ih, W_hh, b_ih, b_hh)
        logits = jnp.einsum('bth,lh->btl', lstm_out, W_lin) + b_lin
        g = jax.lax.stop_gradient(jnp.argmax(logits, axis=-1).astype(lstm_out.dtype))[..., None]
        w = g * lstm_out
        inc = jnp.cumsum(w, axis=1)
        prefix = inc - w
        suffix = inc[:, -1:, :] - inc
        return 2.0 * lstm_out + prefix * fw_att + suffix * bw_att

    def _L1_gnn_ref(x, adj, W, b):
        import jax, jax.numpy as jnp
        import numpy as np
        B, N, F_IN, F_OUT = (8, 2048, 256, 256)
        n = adj.shape[-1]
        adj = adj + jnp.eye(n, dtype=adj.dtype)[None, :, :]
        deg = adj.sum(axis=-1)
        deg_inv_sqrt = deg ** (-0.5)
        deg_inv_sqrt = jnp.where(jnp.isinf(deg_inv_sqrt), 0.0, deg_inv_sqrt)
        adj_norm = deg_inv_sqrt[:, :, None] * adj * deg_inv_sqrt[:, None, :]
        h = jnp.einsum('bnf,fo->bno', x, W)
        out = jnp.einsum('bnm,bmo->bno', adj_norm, h)
        return out + b

    def _L1_ffn_ref(x, Wt, bt, sl_cvx, of_cvx, sl_ccv, of_ccv, alpha, Wc, bc, Wg, bg, Wd, bd):
        import jax, jax.numpy as jnp
        import numpy as np
        B, S, D_MODEL, FFN, P = (8, 4096, 256, 1024, 8)
        BLK = 256
        Bx, Sx, D = x.shape
        T = Bx * Sx
        xf = x.reshape(T, D)
        xb = xf.reshape(T // BLK, BLK, D)
        s = jax.nn.sigmoid(alpha)

        def blk_fn(xx):
            t = jnp.max(xx[:, None, :] + Wt[None, :, :], axis=-1) + bt
            z = t[:, :, None]
            cvx = jnp.max(z * sl_cvx[None] + of_cvx[None], axis=-1)
            ccv = jnp.min(z * sl_ccv[None] + of_ccv[None], axis=-1)
            return s * cvx + (1.0 - s) * ccv
        trop = jax.lax.map(blk_fn, xb).reshape(T, FFN)
        classical = jax.nn.gelu(xf @ Wc + bc, approximate=False)
        g = jax.nn.sigmoid(xf @ Wg + bg)
        fused = g * trop + (1.0 - g) * classical
        out = fused @ Wd + bd
        return out.reshape(Bx, Sx, D)

    x = x + _L0_gnn_ref(_layernorm(x, axis=-1), adj, L0_gnn_theta, L0_gnn_W_h, L0_gnn_W_t, L0_gnn_b_t)
    x = x + _L0_ffn_ref(_layernorm(x, axis=-1), L0_ffn_W_ih, L0_ffn_W_hh, L0_ffn_b_ih, L0_ffn_b_hh, L0_ffn_W_lin, L0_ffn_b_lin, L0_ffn_fw_att, L0_ffn_bw_att)
    x = x + _L1_gnn_ref(_layernorm(x, axis=-1), adj, L1_gnn_W, L1_gnn_b)
    x = x + _L1_ffn_ref(_layernorm(x, axis=-1), L1_ffn_Wt, L1_ffn_bt, L1_ffn_sl_cvx, L1_ffn_of_cvx, L1_ffn_sl_ccv, L1_ffn_of_ccv, L1_ffn_alpha, L1_ffn_Wc, L1_ffn_bc, L1_ffn_Wg, L1_ffn_bg, L1_ffn_Wd, L1_ffn_bd)
    return x


_drawn_inputs = setup_inputs


def setup_inputs(seed=0):
    import zlib

    import numpy as np

    out = dict(_drawn_inputs(seed))
    spreads = {'L0_ffn_fw_att': (0.0010000000474974513, 0.6),
     'L0_ffn_bw_att': (0.0010000000474974513, 0.6),
     'L1_ffn_alpha': (0.0, 0.8),
     'L1_ffn_bc': (0.0, 2.0),
     'L1_ffn_bg': (2.0, 0.2),
     'L1_ffn_bd': (0.0, 0.268)}
    factors = {'L0_gnn_b_t': 8.0,
     'L0_ffn_W_hh': 3.139,
     'L0_ffn_b_ih': 4.158,
     'L0_ffn_b_hh': 4.153,
     'L0_ffn_W_lin': 64.0,
     'L0_ffn_b_lin': 64.0,
     'L1_ffn_Wt': 4.628,
     'L1_ffn_bt': 4.478,
     'L1_ffn_of_cvx': 5.195,
     'L1_ffn_of_ccv': 4.777,
     'L1_ffn_Wg': 4.225}
    for name, (base, spread) in spreads.items():
        noise = np.random.default_rng([zlib.crc32(name.encode()), seed]).standard_normal(out[name].shape)
        drawn = base * np.exp(spread * noise) if base else spread * noise
        out[name] = jnp.asarray(drawn.astype(out[name].dtype))
    for name, factor in factors.items():
        out[name] = (out[name] * factor).astype(out[name].dtype)
    return out
```

```python
from contextlib import ExitStack
import numpy as np
import concourse.bass as bass
from concourse import mybir

F32 = mybir.dt.float32
BF16 = mybir.dt.bfloat16
ALU = mybir.AluOpType
ACT = mybir.ActivationFunctionType
AX = mybir.AxisListType
ds = bass.ds

P = 128
B, N, D = 64, 256, 256
KD = D // P
NT = N // P
TOK = B * N
H = 256
GATES = 4
FFN, PIECES = 1024, 8
FT = FFN // P
LN_EPS = 1e-5


def wait_past(eng, sem, value):
    if not isinstance(value, int) or value > 0:
        eng.wait_ge(sem, value)


def graph_rounds(eng, body):
    for j in range(2):
        body(0, j, j)
    with eng.Fori(1, B // 2) as i:
        for j in range(2):
            body(i, j, 2 * i + j)


class Steps:

    def __init__(self, sem, per):
        self.sem, self.per = sem, per

    def begin(self, round_):
        self.base, self.k = round_ * self.per, 0

    def done(self, instruction):
        instruction.then_inc(self.sem, 1)
        self.k += 1
        return self.base + self.k

    def end(self):
        assert self.k == self.per, (self.k, self.per)


def stage_gnn0(nc, a, hx, x1_dram):
    with ExitStack() as ctx:
        def sb(name, shape, dt=F32):
            return ctx.enter_context(nc.sbuf_tensor(name, shape, dt))

        def ps(name, shape):
            return ctx.enter_context(nc.psum_tensor(name, shape, F32))

        def sem(name):
            return ctx.enter_context(nc.semaphore(name))

        w_cat = sb("g0_w", [P, KD, 3 * D])
        bt_row = sb("g0_bt", [1, D])
        ones_row = sb("g0_ones", [1, P])
        pause = sb("g0_pause", [1, 1])
        ident = sb("g0_ident", [P, P])
        x_in = [sb(f"g0_x{j}", [P, NT, D]) for j in range(2)]
        adj_in = [sb(f"g0_adj{j}", [P, NT, N]) for j in range(2)]
        adjt_in = [sb(f"g0_adjt{j}", [P, NT, N]) for j in range(2)]
        x1_out = [sb(f"g0_x1{j}", [P, NT, D]) for j in range(2)]
        stats = sb("g0_stats", [P, NT, 6])
        mv = sb("g0_mv", [P, NT, 2])
        rstd = sb("g0_rstd", [P, NT])
        mv1 = sb("g0_mv1", [P, NT, 2])
        rstd1 = sb("g0_rstd1", [P, NT])
        half = sb("g0_half", [P, NT])
        eps_ln = sb("g0_eps_ln", [P, NT])
        eps_deg = sb("g0_eps_deg", [P, NT])
        vare = sb("g0_vare", [P, NT])
        dege = sb("g0_dege", [P, NT])
        deg = sb("g0_deg", [P, NT])
        norm = sb("g0_norm", [P, NT])
        junk = sb("g0_junk", [P, NT, N])
        xn = sb("g0_xn", [P, NT, D])
        xn_t = sb("g0_xnt", [P, KD, N])
        f_hom = sb("g0_fhom", [P, NT, D])
        f_het = sb("g0_fhet", [P, NT, D])
        tanh_z = sb("g0_tanh_z", [P, NT, D])
        gate = sb("g0_gate", [P, NT, D])
        u = sb("g0_u", [P, NT, D])
        o = sb("g0_o", [P, NT, D])
        neg = sb("g0_neg", [P, NT, D])
        y = sb("g0_y", [P, NT, D])
        ps_t = ps("g0_pst", [P, KD, N])
        ps_hom_het = [ps(f"g0_psa{t}", [P, 2 * D]) for t in range(NT)]
        ps_gate = ps("g0_psg", [P, NT, D])
        ps_agg = ps("g0_psf", [P, NT, D])
        ps_t1 = ps("g0_pst1", [P, KD, N])

        const_in = sem("g0_const_in")
        graph_in = [sem(f"g0_graph_in{j}") for j in range(2)]
        x1_stored = [sem(f"g0_x1_stored{j}") for j in range(2)]
        half_set = sem("g0_half_set")
        ones_set = sem("g0_ones_set")
        dve_steps = Steps(sem("g0_dve_steps"), 7)
        pool_steps = Steps(sem("g0_pool_steps"), 3)
        mv_ready = sem("g0_mv_ready")
        rstd_ready = sem("g0_rstd_ready")
        xn_ready = sem("g0_xn_ready")
        xt_done = sem("g0_xt_done")
        xn_t_ready = sem("g0_xn_t_ready")
        proj_done = sem("g0_proj_done")
        gate_done = sem("g0_gate_done")
        deg_ready = sem("g0_deg_ready")
        norm_ready = sem("g0_norm_ready")
        f_hom_ready = sem("g0_f_hom_ready")
        f_het_ready = sem("g0_f_het_ready")
        tanh_z_ready = sem("g0_tanh_z_ready")
        agg_done = sem("g0_agg_done")
        neg_ready = sem("g0_neg_ready")
        exp_ready = sem("g0_exp_ready")
        x1_ready = sem("g0_x1_ready")
        mv1_ready = sem("g0_mv1_ready")
        rstd1_ready = sem("g0_rstd1_ready")
        xn1_ready = sem("g0_xn1_ready")
        xt1_done = sem("g0_xt1_done")
        hx_written = sem("g0_hx_written")
        CONST_DMAS = 5

        block = ctx.enter_context(nc.Block())

        @block.sync
        def _(sp):
            sp.dma_start(w_cat[:, :, 0:D], a["theta"].rearrange("(k p) e -> p k e", p=P)).then_inc(const_in, 16)
            sp.dma_start(w_cat[:, :, D:2 * D], a["W_h"].rearrange("(k p) e -> p k e", p=P)).then_inc(const_in, 16)
            sp.dma_start(w_cat[:, :, 2 * D:3 * D], a["W_t"].rearrange("(k p) e -> p k e", p=P)).then_inc(const_in, 16)
            sp.dma_start(bt_row[:, :], a["b_t"]).then_inc(const_in, 16)
            sp.dma_start(ident[:, :], a["ident"]).then_inc(const_in, 16)

            def load(n, j):
                for dst, src in ((x_in, "x"), (adj_in, "adj"), (adjt_in, "adjt")):
                    sp.dma_start(dst[j][:, :, :], a[src][ds(n, 1)].rearrange("o (t p) e -> p (o t) e", p=P))\
                      .then_inc(graph_in[j], 16)

            def store(n, j):
                sp.wait_ge(x1_ready, n + 1)
                sp.dma_start(x1_dram[ds(n, 1)].rearrange("o (t p) e -> p (o t) e", p=P), x1_out[j][:, :, :])\
                  .then_inc(x1_stored[j], 16)

            for j in range(2):
                load(j, j)
            with sp.Fori(0, B // 2 - 1) as i:
                for j in range(2):
                    store(2 * i + j, j)
                    load(2 * i + j + 2, j)
            for j in range(2):
                store(B - 2 + j, j)
            for j in range(2):
                sp.wait_ge(x1_stored[j], 16 * (B // 2))

        @block.gpsimd
        def _(pool):
            pool.memset(half[:, :], -0.5).then_inc(half_set, 1)
            pool.memset(eps_ln[:, :], LN_EPS).then_inc(half_set, 1)
            pool.memset(eps_deg[:, :], 1e-6).then_inc(half_set, 1)
            pool.wait_ge(half_set, 3)

            def body(i, j, n):
                pool_steps.begin(n)
                pool.wait_ge(mv_ready, n + 1)
                t = pool_steps.done(pool.tensor_tensor(vare[:, :], mv[:, :, 1], eps_ln[:, :], ALU.add))
                pool.wait_ge(pool_steps.sem, t)
                pool.tensor_tensor(rstd[:, :], vare[:, :], half[:, :], ALU.pow).then_inc(rstd_ready, 1)
                pool.wait_ge(deg_ready, n + 1)
                t = pool_steps.done(pool.tensor_tensor(dege[:, :], deg[:, :], eps_deg[:, :], ALU.add))
                pool.wait_ge(pool_steps.sem, t)
                pool.tensor_tensor(norm[:, :], dege[:, :], half[:, :], ALU.pow).then_inc(norm_ready, 1)
                pool.wait_ge(mv1_ready, n + 1)
                t = pool_steps.done(pool.tensor_tensor(vare[:, :], mv1[:, :, 1], eps_ln[:, :], ALU.add))
                pool.wait_ge(pool_steps.sem, t)
                pool.tensor_tensor(rstd1[:, :], vare[:, :], half[:, :], ALU.pow).then_inc(rstd1_ready, 1)
                pool_steps.end()

            graph_rounds(pool, body)

        @block.scalar
        def _(act):
            def body(i, j, n):
                act.wait_ge(graph_in[j], 48 * (i + 1))
                wait_past(act, x1_ready, n)
                for t in range(NT):
                    last = act.activation(junk[:, t, :], adj_in[j][:, t, :], ACT.Abs, accum_out=deg[:, t:t + 1])
                last.then_inc(deg_ready, 1)
                act.wait_ge(xt_done, n + 1)
                act.activation(xn_t[:, :, :], ps_t[:, :, :], ACT.Copy).then_inc(xn_t_ready, 1)
                act.wait_ge(norm_ready, n + 1)
                act.wait_ge(proj_done, n + 1)
                for t in range(NT):
                    last = act.activation(f_hom[:, t, :], ps_hom_het[t][:, 0:D], ACT.Copy, scale=norm[:, t:t + 1])
                last.then_inc(f_hom_ready, 1)
                for t in range(NT):
                    last = act.activation(f_het[:, t, :], ps_hom_het[t][:, D:2 * D], ACT.Copy)
                last.then_inc(f_het_ready, 1)
                act.wait_ge(gate_done, n + 1)
                act.activation(tanh_z[:, :, :], ps_gate[:, :, :], ACT.Tanh, scale=0.5).then_inc(tanh_z_ready, 1)
                act.wait_ge(neg_ready, n + 1)
                act.activation(neg[:, :, :], neg[:, :, :], ACT.Exp).then_inc(exp_ready, 1)
                act.wait_ge(xt1_done, n + 1)
                act.activation(hx[:, :, 1:1 + N, ds(n, 1)].rearrange("p k t o -> p k (t o)"), ps_t1[:, :, :], ACT.Copy)\
                   .then_inc(hx_written, 1)

            graph_rounds(act, body)

        @block.tensor
        def _(pe):
            pe.wait_ge(const_in, 16 * CONST_DMAS)
            pe.wait_ge(ones_set, 1)

            def turn(dst, src):
                for k in range(KD):
                    for t in range(NT):
                        last = pe.transpose(dst[:, k, t * P:(t + 1) * P], src[:, t, k * P:(k + 1) * P], ident[:, :])
                return last

            def body(i, j, n):
                pe.wait_ge(xn_ready, n + 1)
                turn(ps_t, xn).then_inc(xt_done, 1)
                pe.wait_ge(xn_t_ready, n + 1)
                for t in range(NT):
                    for k in range(KD):
                        last = pe.matmul(ps_hom_het[t][:, :], xn_t[:, k, t * P:(t + 1) * P], w_cat[:, k, 0:2 * D],
                                         start=(k == 0), stop=(k == KD - 1))
                last.then_inc(proj_done, 1)
                for t in range(NT):
                    for k in range(KD):
                        pe.matmul(ps_gate[:, t, :], xn_t[:, k, t * P:(t + 1) * P], w_cat[:, k, 2 * D:3 * D],
                                  start=(k == 0), stop=False)
                    last = pe.matmul(ps_gate[:, t, :], ones_row[:, :], bt_row[:, :], start=False, stop=True)
                last.then_inc(gate_done, 1)
                pe.wait_ge(graph_in[j], 48 * (i + 1))
                pe.wait_ge(f_hom_ready, n + 1)
                for t in range(NT):
                    for m in range(NT):
                        last = pe.matmul(ps_agg[:, t, :], adjt_in[j][:, m, t * P:(t + 1) * P], f_hom[:, m, :],
                                         start=(m == 0), stop=(m == NT - 1))
                last.then_inc(agg_done, 1)
                pe.wait_ge(xn1_ready, n + 1)
                turn(ps_t1, xn).then_inc(xt1_done, 1)

            graph_rounds(pe, body)

        @block.vector
        def _(dve):
            dve.memset(ones_row[:, :], 1.0).then_inc(ones_set, 1)

            def normalise(src, mv_, mv_sem, rstd_, rstd_sem, xn_sem, n):
                for t in range(NT):
                    last = dve.bn_stats(stats[:, t, :], src[:, t, :])
                v = dve_steps.done(last)
                dve.wait_ge(dve_steps.sem, v)
                dve.memset(pause[:, :], 0.0)
                for t in range(NT):
                    last = dve.bn_aggr(mv_[:, t, :], stats[:, t, :])
                last.then_inc(mv_sem, 1)
                dve.wait_ge(rstd_sem, n + 1)
                for t in range(NT):
                    last = dve.tensor_scalar(xn[:, t, :], src[:, t, :], mv_[:, t, 0:1], rstd_[:, t:t + 1],
                                             ALU.subtract, ALU.mult)
                last.then_inc(xn_sem, 1)

            def body(i, j, n):
                dve_steps.begin(n)
                dve.wait_ge(graph_in[j], 48 * (i + 1))
                wait_past(dve, xt1_done, n)
                normalise(x_in[j], mv, mv_ready, rstd, rstd_ready, xn_ready, n)
                dve.wait_ge(tanh_z_ready, n + 1)
                v = dve_steps.done(dve.tensor_scalar(gate[:, :, :], tanh_z[:, :, :], 0.5, 0.5, ALU.mult, ALU.add))
                dve.wait_ge(agg_done, n + 1)
                dve.wait_ge(f_het_ready, n + 1)
                for t in range(NT):
                    last = dve.scalar_tensor_tensor(u[:, t, :], ps_agg[:, t, :], norm[:, t:t + 1], f_het[:, t, :],
                                                    ALU.mult, ALU.subtract)
                v = dve_steps.done(last)
                dve.wait_ge(dve_steps.sem, v)
                v = dve_steps.done(dve.tensor_tensor(u[:, :, :], u[:, :, :], gate[:, :, :], ALU.mult))
                dve.wait_ge(dve_steps.sem, v)
                v = dve_steps.done(dve.tensor_tensor(o[:, :, :], u[:, :, :], f_het[:, :, :], ALU.add))
                dve.wait_ge(dve_steps.sem, v)
                dve.tensor_scalar(neg[:, :, :], o[:, :, :], 0.0, None, ALU.min).then_inc(neg_ready, 1)
                v = dve_steps.done(dve.scalar_tensor_tensor(y[:, :, :], o[:, :, :], 0.0, x_in[j][:, :, :],
                                                            ALU.max, ALU.add))
                dve.wait_ge(dve_steps.sem, v)
                dve.wait_ge(exp_ready, n + 1)
                wait_past(dve, x1_stored[j], 16 * i)
                dve.scalar_tensor_tensor(x1_out[j][:, :, :], neg[:, :, :], -1.0, y[:, :, :],
                                         ALU.add, ALU.add).then_inc(x1_ready, 1)
                dve.wait_ge(x1_ready, n + 1)
                normalise(x1_out[j], mv1, mv1_ready, rstd1, rstd1_ready, xn1_ready, n)
                dve_steps.end()

            graph_rounds(dve, body)


def stage_lstm(nc, a, hx):
    T, S = N, 4
    ROWS = GATES * H // P
    with ExitStack() as ctx:
        def sb(name, shape, dt=F32):
            return ctx.enter_context(nc.sbuf_tensor(name, shape, dt))

        def sem(name):
            return ctx.enter_context(nc.semaphore(name))

        w_ih = sb("l_wih", [P, KD, GATES * H])
        w_hh = sb("l_whh", [P, KD, GATES * H])
        bias = sb("l_bias", [4, GATES, P])
        which = sb("l_which", [4, 2 * S * B])
        act_g = [sb(f"l_act{q}", [P, 2, B]) for q in range(GATES)]
        c = sb("l_c", [P, 2, B])
        ig = sb("l_ig", [P, 2, B])
        tc_ = sb("l_tc", [P, 2, B])
        ps_g = [[ctx.enter_context(nc.psum_tensor(f"l_ps{s}{q}", [P, 2, S, B], F32)) for q in range(GATES)]
                for s in range(2)]

        const_in = sem("l_const_in")
        zero_set = sem("l_zero_set")
        gate_done = [sem(f"l_gate_done{q}") for q in range(GATES)]
        act_ready = [sem(f"l_act_ready{q}") for q in range(GATES)]
        ig_ready = sem("l_ig_ready")
        fc_ready = sem("l_fc_ready")
        c_ready = sem("l_c_ready")
        tanh_c_ready = sem("l_tanh_c_ready")
        h_ready = sem("l_h_ready")
        block = ctx.enter_context(nc.Block())

        @block.sync
        def _(sp):
            sp.dma_start(w_ih[:, :, :], a["w_ih_t"].rearrange("(k p) g -> p k g", p=P)).then_inc(const_in, 16)
            sp.dma_start(w_hh[:, :, :], a["w_hh_t"].rearrange("(k p) g -> p k g", p=P)).then_inc(const_in, 16)
            sp.dma_start(bias[0:2, :, :], a["b_ih"].rearrange("(q c m) -> c q m", q=GATES, c=2)).then_inc(const_in, 16)
            sp.dma_start(bias[2:4, :, :], a["b_hh"].rearrange("(q c m) -> c q m", q=GATES, c=2)).then_inc(const_in, 16)
            sp.dma_start(which[:, :], a["which"]).then_inc(const_in, 16)

        @block.vector
        def _(dve):
            dve.memset(hx[:, :, 0:1, :], 0.0).then_inc(zero_set, 1)
            dve.memset(c[:, :, :], 0.0).then_inc(zero_set, 1)
            dve.wait_ge(zero_set, 2)

            def step(t):
                dve.wait_ge(act_ready[0], t + 1)
                dve.wait_ge(act_ready[1], t + 1)
                dve.tensor_tensor(ig[:, :, :], act_g[0][:, :, :], act_g[1][:, :, :], ALU.mult).then_inc(ig_ready, 1)
                dve.wait_ge(act_ready[2], t + 1)
                wait_past(dve, c_ready, t)
                dve.tensor_tensor(c[:, :, :], c[:, :, :], act_g[2][:, :, :], ALU.mult).then_inc(fc_ready, 1)
                dve.wait_ge(ig_ready, t + 1)
                dve.wait_ge(fc_ready, t + 1)
                dve.tensor_tensor(c[:, :, :], c[:, :, :], ig[:, :, :], ALU.add).then_inc(c_ready, 1)
                dve.wait_ge(act_ready[3], t + 1)
                dve.wait_ge(tanh_c_ready, t + 1)
                dve.tensor_tensor(hx[:, :, ds(t + 1, 1), :].rearrange("p k o b -> p k (o b)"), act_g[3][:, :, :],
                                  tc_[:, :, :], ALU.mult).then_inc(h_ready, 1)

            step(0)
            with dve.Fori(1, T) as t:
                step(t)

        @block.scalar
        def _(act):
            def step(t, s, r):
                for q in range(GATES):
                    act.wait_ge(gate_done[q], t + 1)
                    if q == 0:
                        wait_past(act, h_ready, t)
                    act.activation(act_g[q][:, :, :], ps_g[s][q][:, :, r, :], ACT.Tanh if q == 0 else ACT.Sigmoid)\
                       .then_inc(act_ready[q], 1)
                act.wait_ge(c_ready, t + 1)
                act.activation(tc_[:, :, :], c[:, :, :], ACT.Tanh).then_inc(tanh_c_ready, 1)

            def groups(i):
                for s in range(2):
                    for r in range(S):
                        step(2 * S * i + S * s + r, s, r)

            groups(0)
            with act.Fori(1, T // (2 * S)) as i:
                groups(i)

        @block.tensor
        def _(pe):
            def input_part(group, s, q):
                pe.matmul(ps_g[s][q][:, :, :, :], bias[:, q, :], which[:, :], start=True, stop=False,
                          skip_group_check=True)
                for c2 in range(2):
                    row = (2 * q + c2) * P
                    for k in range(KD):
                        pe.matmul(ps_g[s][q][:, c2, :, :], w_ih[:, k, row:row + P],
                                  hx[:, k, ds(S * group + 1, S), :], start=False, stop=False,
                                  skip_group_check=True)

            def steps(i, s, last):
                group = 2 * i + s
                for r in range(S):
                    t = S * group + r
                    wait_past(pe, h_ready, t)
                    for q in range(GATES):
                        for c2 in range(2):
                            row = (2 * q + c2) * P
                            for k in range(KD):
                                mm = pe.matmul(ps_g[s][q][:, c2, r, :], w_hh[:, k, row:row + P],
                                               hx[:, k, ds(t, 1), :].rearrange("p o b -> p (o b)"), start=False,
                                               stop=(r == S - 1 and c2 == 1 and k == KD - 1), skip_group_check=True)
                        mm.then_inc(gate_done[q], 1)
                    if not last:
                        input_part(group + 1, 1 - s, r)

            pe.wait_ge(const_in, 16 * 5)
            pe.wait_ge(zero_set, 2)
            for q in range(GATES):
                input_part(0, 0, q)
            for s in range(2):
                steps(0, s, False)
            with pe.Fori(1, T // (2 * S) - 1) as i:
                for s in range(2):
                    steps(i, s, False)
            for s in range(2):
                steps(T // (2 * S) - 1, s, s == 1)


def stage_gnn1(nc, a, hx, x1_dram, x3t_dram, xn3t_dram):
    with ExitStack() as ctx:
        def sb(name, shape, dt=F32):
            return ctx.enter_context(nc.sbuf_tensor(name, shape, dt))

        def ps(name, shape):
            return ctx.enter_context(nc.psum_tensor(name, shape, F32))

        def sem(name):
            return ctx.enter_context(nc.semaphore(name))

        w = sb("g1_w", [P, KD, D])
        w_lin = sb("g1_wlin", [P, KD, 2])
        b_lin = sb("g1_blin", [1, 2])
        ones_row = sb("g1_ones_row", [1, P])
        ones_sq = sb("g1_ones_sq", [P, P])
        before = sb("g1_before", [P, P])
        after = sb("g1_after", [P, P])
        ident = sb("g1_ident", [P, P])
        fw = sb("g1_fw", [P, NT, D])
        bw = sb("g1_bw", [P, NT, D])
        b_all = sb("g1_b", [P, NT, D])
        x1_in = [sb(f"g1_x1{j}", [P, NT, D]) for j in range(2)]
        adj_in = [sb(f"g1_adj{j}", [P, NT, N]) for j in range(2)]
        adjt_in = [sb(f"g1_adjt{j}", [P, NT, N]) for j in range(2)]
        x3t_out = [sb(f"g1_x3t{j}", [P, KD, N]) for j in range(2)]
        xn3t_out = [sb(f"g1_xn3t{j}", [P, KD, N]) for j in range(2)]
        mv3 = sb("g1_mv3", [P, NT, 2])
        rstd3 = sb("g1_rstd3", [P, NT])
        h_t = sb("g1_ht", [P, KD, N])
        h = sb("g1_h", [P, NT, D])
        logit = sb("g1_logit", [P, NT, 2])
        picked = sb("g1_picked", [P, NT])
        wh = sb("g1_wh", [P, NT, D])
        y = sb("g1_y", [P, NT, D])
        z = sb("g1_z", [P, NT, D])
        x2 = sb("g1_x2", [P, NT, D])
        x2b = sb("g1_x2b", [P, NT, D])
        x3 = sb("g1_x3", [P, NT, D])
        pause = sb("g1_pause", [1, 1])
        stats = sb("g1_stats", [P, NT, 6])
        mv = sb("g1_mv", [P, NT, 2])
        rstd = sb("g1_rstd", [P, NT])
        half = sb("g1_half", [P, NT])
        eps = sb("g1_eps", [P, NT])
        one = sb("g1_one", [P, NT])
        vare = sb("g1_vare", [P, NT])
        row_sum = sb("g1_row_sum", [P, NT])
        is_zero = sb("g1_is_zero", [P, NT])
        deg_safe = sb("g1_deg_safe", [P, NT])
        keep = sb("g1_keep", [P, NT])
        power = sb("g1_power", [P, NT])
        dinv = sb("g1_dinv", [P, NT])
        junk = sb("g1_junk", [P, NT, N])
        xn = sb("g1_xn", [P, NT, D])
        xn_t = sb("g1_xnt", [P, KD, N])
        hs = sb("g1_hs", [P, NT, D])
        ps_logit = ps("g1_ps_logit", [P, NT, 2])
        ps_h = ps("g1_ps_h", [P, NT, D])
        ps_pre = ps("g1_ps_pre", [P, NT, D])
        ps_suf = ps("g1_ps_suf", [P, NT, D])
        ps_t = ps("g1_ps_t", [P, KD, N])
        ps_w = ps("g1_ps_w", [P, NT, D])
        ps_agg = ps("g1_ps_agg", [P, NT, D])
        ps_x3t = ps("g1_ps_x3t", [P, KD, N])

        const_in = sem("g1_const_in")
        graph_in = [sem(f"g1_graph_in{j}") for j in range(2)]
        x3t_stored = [sem(f"g1_x3t_stored{j}") for j in range(2)]
        consts_set = sem("g1_consts_set")
        ones_set = sem("g1_ones_set")
        dve_steps = Steps(sem("g1_dve_steps"), 8)
        pool_steps = Steps(sem("g1_pool_steps"), 3)
        h_t_ready = sem("g1_h_t_ready")
        logit_done = sem("g1_logit_done")
        logit_ready = sem("g1_logit_ready")
        h_done = sem("g1_h_done")
        h_ready = sem("g1_h_ready")
        picked_ready = sem("g1_picked_ready")
        wh_ready = sem("g1_wh_ready")
        sums_done = sem("g1_sums_done")
        mv_ready = sem("g1_mv_ready")
        rstd_ready = sem("g1_rstd_ready")
        xn_ready = sem("g1_xn_ready")
        xt_done = sem("g1_xt_done")
        xn_t_ready = sem("g1_xn_t_ready")
        proj_done = sem("g1_proj_done")
        row_sum_ready = sem("g1_row_sum_ready")
        deg_ready = sem("g1_deg_ready")
        dinv_ready = sem("g1_dinv_ready")
        hs_ready = sem("g1_hs_ready")
        agg_done = sem("g1_agg_done")
        x3_ready = sem("g1_x3_ready")
        x3t_done = sem("g1_x3t_done")
        mv3_ready = sem("g1_mv3_ready")
        rstd3_ready = sem("g1_rstd3_ready")
        xn3_ready = sem("g1_xn3_ready")
        xn3t_done = sem("g1_xn3t_done")
        xn3t_ready = sem("g1_xn3t_ready")
        CONSTS = ("w", "w_lin", "b_lin", "ident", "before", "after", "fw", "bw", "b")

        block = ctx.enter_context(nc.Block())

        @block.sync
        def _(sp):
            sp.dma_start(w[:, :, :], a["W1"].rearrange("(k p) e -> p k e", p=P)).then_inc(const_in, 16)
            sp.dma_start(w_lin[:, :, :], a["w_lin_t"].rearrange("(k p) c -> p k c", p=P)).then_inc(const_in, 16)
            sp.dma_start(b_lin[:, :], a["b_lin"]).then_inc(const_in, 16)
            sp.dma_start(ident[:, :], a["ident"]).then_inc(const_in, 16)
            sp.dma_start(before[:, :], a["before"]).then_inc(const_in, 16)
            sp.dma_start(after[:, :], a["after"]).then_inc(const_in, 16)
            for t in range(NT):
                for dst, src in ((fw, "fw_att"), (bw, "bw_att"), (b_all, "b1")):
                    sp.dma_start(dst[:, t, :], a[src].to_broadcast([P, D])).then_inc(const_in, 16)

            def load(n, j):
                for dst, src in ((x1_in, x1_dram), (adj_in, a["adj"]), (adjt_in, a["adjt"])):
                    sp.dma_start(dst[j][:, :, :], src[ds(n, 1)].rearrange("o (t p) e -> p (o t) e", p=P))\
                      .then_inc(graph_in[j], 16)

            def store(n, j):
                sp.wait_ge(xn3t_ready, n + 1)
                for dst, src in ((x3t_dram, x3t_out), (xn3t_dram, xn3t_out)):
                    sp.dma_start(dst[:, :, ds(n * N, N)].rearrange("k p t -> p k t"), src[j][:, :, :])\
                      .then_inc(x3t_stored[j], 16)

            for j in range(2):
                load(j, j)
            with sp.Fori(0, B // 2 - 1) as i:
                for j in range(2):
                    store(2 * i + j, j)
                    load(2 * i + j + 2, j)
            for j in range(2):
                store(B - 2 + j, j)
            for j in range(2):
                sp.wait_ge(x3t_stored[j], 32 * (B // 2))

        @block.gpsimd
        def _(pool):
            pool.memset(half[:, :], -0.5).then_inc(consts_set, 1)
            pool.memset(eps[:, :], LN_EPS).then_inc(consts_set, 1)
            pool.memset(one[:, :], 1.0).then_inc(consts_set, 1)
            pool.wait_ge(consts_set, 3)

            def body(i, j, n):
                pool_steps.begin(n)
                pool.wait_ge(deg_ready, n + 1)
                pool.tensor_tensor(power[:, :], deg_safe[:, :], half[:, :], ALU.pow)
                t = pool_steps.done(pool.tensor_tensor(keep[:, :], one[:, :], is_zero[:, :], ALU.subtract))
                pool.wait_ge(pool_steps.sem, t)
                pool.tensor_tensor(dinv[:, :], power[:, :], keep[:, :], ALU.mult).then_inc(dinv_ready, 1)
                pool.wait_ge(mv_ready, n + 1)
                t = pool_steps.done(pool.tensor_tensor(vare[:, :], mv[:, :, 1], eps[:, :], ALU.add))
                pool.wait_ge(pool_steps.sem, t)
                pool.tensor_tensor(rstd[:, :], vare[:, :], half[:, :], ALU.pow).then_inc(rstd_ready, 1)
                pool.wait_ge(mv3_ready, n + 1)
                t = pool_steps.done(pool.tensor_tensor(vare[:, :], mv3[:, :, 1], eps[:, :], ALU.add))
                pool.wait_ge(pool_steps.sem, t)
                pool.tensor_tensor(rstd3[:, :], vare[:, :], half[:, :], ALU.pow).then_inc(rstd3_ready, 1)
                pool_steps.end()

            graph_rounds(pool, body)

        @block.scalar
        def _(act):
            def body(i, j, n):
                wait_past(act, x3_ready, n)
                act.activation(h_t[:, :, :], hx[:, :, 1:1 + N, ds(n, 1)].rearrange("p k t o -> p k (t o)"), ACT.Copy)\
                   .then_inc(h_t_ready, 1)
                act.wait_ge(logit_done, n + 1)
                act.activation(logit[:, :, :], ps_logit[:, :, :], ACT.Copy).then_inc(logit_ready, 1)
                act.wait_ge(h_done, n + 1)
                act.activation(h[:, :, :], ps_h[:, :, :], ACT.Copy).then_inc(h_ready, 1)
                act.wait_ge(graph_in[j], 48 * (i + 1))
                for t in range(NT):
                    last = act.activation(junk[:, t, :], adj_in[j][:, t, :], ACT.Copy, accum_out=row_sum[:, t:t + 1])
                last.then_inc(row_sum_ready, 1)
                act.wait_ge(xt_done, n + 1)
                act.activation(xn_t[:, :, :], ps_t[:, :, :], ACT.Copy).then_inc(xn_t_ready, 1)
                act.wait_ge(dinv_ready, n + 1)
                act.wait_ge(proj_done, n + 1)
                for t in range(NT):
                    last = act.activation(hs[:, t, :], ps_w[:, t, :], ACT.Copy, scale=dinv[:, t:t + 1])
                last.then_inc(hs_ready, 1)
                act.wait_ge(x3t_done, n + 1)
                wait_past(act, x3t_stored[j], 32 * i)
                act.activation(x3t_out[j][:, :, :], ps_x3t[:, :, :], ACT.Copy)
                act.wait_ge(xn3t_done, n + 1)
                act.activation(xn3t_out[j][:, :, :], ps_t[:, :, :], ACT.Copy).then_inc(xn3t_ready, 1)

            graph_rounds(act, body)

        @block.tensor
        def _(pe):
            pe.wait_ge(const_in, 16 * (len(CONSTS) + 3))
            pe.wait_ge(ones_set, 2)

            def turn(dst, src):
                for k in range(2):
                    for t in range(2):
                        last = pe.transpose(dst[:, k, t * P:(t + 1) * P], src[:, t, k * P:(k + 1) * P], ident[:, :])
                return last

            def body(i, j, n):
                pe.wait_ge(h_t_ready, n + 1)
                for t in range(NT):
                    for k in range(KD):
                        pe.matmul(ps_logit[:, t, :], h_t[:, k, t * P:(t + 1) * P], w_lin[:, k, :],
                                  start=(k == 0), stop=False)
                    last = pe.matmul(ps_logit[:, t, :], ones_row[:, :], b_lin[:, :], start=False, stop=True)
                last.then_inc(logit_done, 1)
                turn(ps_h, h_t).then_inc(h_done, 1)
                pe.wait_ge(wh_ready, n + 1)
                pe.matmul(ps_pre[:, 0, :], before[:, :], wh[:, 0, :], start=True, stop=True)
                pe.matmul(ps_pre[:, 1, :], ones_sq[:, :], wh[:, 0, :], start=True, stop=False)
                pe.matmul(ps_pre[:, 1, :], before[:, :], wh[:, 1, :], start=False, stop=True)
                pe.matmul(ps_suf[:, 0, :], after[:, :], wh[:, 0, :], start=True, stop=False)
                pe.matmul(ps_suf[:, 0, :], ones_sq[:, :], wh[:, 1, :], start=False, stop=True)
                pe.matmul(ps_suf[:, 1, :], after[:, :], wh[:, 1, :], start=True, stop=True).then_inc(sums_done, 1)
                pe.wait_ge(xn_ready, n + 1)
                turn(ps_t, xn).then_inc(xt_done, 1)
                pe.wait_ge(xn_t_ready, n + 1)
                for t in range(NT):
                    for k in range(KD):
                        last = pe.matmul(ps_w[:, t, :], xn_t[:, k, t * P:(t + 1) * P], w[:, k, :],
                                         start=(k == 0), stop=(k == KD - 1))
                last.then_inc(proj_done, 1)
                pe.wait_ge(graph_in[j], 48 * (i + 1))
                pe.wait_ge(hs_ready, n + 1)
                for t in range(NT):
                    for m in range(NT):
                        last = pe.matmul(ps_agg[:, t, :], adjt_in[j][:, m, t * P:(t + 1) * P], hs[:, m, :],
                                         start=(m == 0), stop=(m == NT - 1))
                last.then_inc(agg_done, 1)
                pe.wait_ge(x3_ready, n + 1)
                turn(ps_x3t, x3).then_inc(x3t_done, 1)
                pe.wait_ge(xn3_ready, n + 1)
                turn(ps_t, xn).then_inc(xn3t_done, 1)

            graph_rounds(pe, body)

        @block.vector
        def _(dve):
            dve.memset(ones_row[:, :], 1.0).then_inc(ones_set, 1)
            dve.memset(ones_sq[:, :], 1.0).then_inc(ones_set, 1)
            dve.wait_ge(const_in, 16 * (len(CONSTS) + 3))

            def normalise(src, mv_, mv_sem, rstd_, rstd_sem, xn_sem, n):
                for t in range(NT):
                    last = dve.bn_stats(stats[:, t, :], src[:, t, :])
                v = dve_steps.done(last)
                dve.wait_ge(dve_steps.sem, v)
                dve.memset(pause[:, :], 0.0)
                for t in range(NT):
                    last = dve.bn_aggr(mv_[:, t, :], stats[:, t, :])
                last.then_inc(mv_sem, 1)
                if src is x2:
                    dve.tensor_tensor(x2b[:, :, :], x2[:, :, :], b_all[:, :, :], ALU.add)
                dve.wait_ge(rstd_sem, n + 1)
                for t in range(NT):
                    last = dve.tensor_scalar(xn[:, t, :], src[:, t, :], mv_[:, t, 0:1], rstd_[:, t:t + 1],
                                             ALU.subtract, ALU.mult)
                last.then_inc(xn_sem, 1)

            def body(i, j, n):
                dve_steps.begin(n)
                dve.wait_ge(logit_ready, n + 1)
                dve.tensor_tensor(picked[:, :], logit[:, :, 1], logit[:, :, 0], ALU.is_gt).then_inc(picked_ready, 1)
                dve.wait_ge(picked_ready, n + 1)
                dve.wait_ge(h_ready, n + 1)
                for t in range(NT):
                    last = dve.tensor_scalar(wh[:, t, :], h[:, t, :], picked[:, t:t + 1], None, ALU.mult)
                last.then_inc(wh_ready, 1)
                dve.wait_ge(row_sum_ready, n + 1)
                v = dve_steps.done(dve.tensor_scalar(is_zero[:, :], row_sum[:, :], 1.0, 0.0, ALU.add, ALU.is_equal))
                dve.wait_ge(dve_steps.sem, v)
                dve.scalar_tensor_tensor(deg_safe[:, :], row_sum[:, :], 1.0, is_zero[:, :], ALU.add, ALU.add)\
                   .then_inc(deg_ready, 1)
                dve.wait_ge(sums_done, n + 1)
                dve.tensor_tensor(y[:, :, :], ps_pre[:, :, :], fw[:, :, :], ALU.mult)
                v = dve_steps.done(dve.tensor_tensor(z[:, :, :], ps_suf[:, :, :], bw[:, :, :], ALU.mult))
                dve.wait_ge(dve_steps.sem, v)
                v = dve_steps.done(dve.scalar_tensor_tensor(y[:, :, :], h[:, :, :], 2.0, y[:, :, :],
                                                            ALU.mult, ALU.add))
                dve.wait_ge(dve_steps.sem, v)
                v = dve_steps.done(dve.tensor_tensor(y[:, :, :], y[:, :, :], z[:, :, :], ALU.add))
                dve.wait_ge(dve_steps.sem, v)
                dve.wait_ge(graph_in[j], 48 * (i + 1))
                v = dve_steps.done(dve.tensor_tensor(x2[:, :, :], x1_in[j][:, :, :], y[:, :, :], ALU.add))
                dve.wait_ge(dve_steps.sem, v)
                normalise(x2, mv, mv_ready, rstd, rstd_ready, xn_ready, n)
                dve.wait_ge(agg_done, n + 1)
                v = dve_steps.done(dve.tensor_tensor(z[:, :, :], ps_agg[:, :, :], hs[:, :, :], ALU.add))
                dve.wait_ge(dve_steps.sem, v)
                for t in range(NT):
                    last = dve.scalar_tensor_tensor(x3[:, t, :], z[:, t, :], dinv[:, t:t + 1], x2b[:, t, :],
                                                    ALU.mult, ALU.add)
                last.then_inc(x3_ready, 1)
                dve.wait_ge(x3_ready, n + 1)
                normalise(x3, mv3, mv3_ready, rstd3, rstd3_ready, xn3_ready, n)
                dve_steps.end()

            graph_rounds(dve, body)


def stage_tropical(nc, a, xn3t_dram, t_dram):
    TB = 1024
    BLOCKS = TOK // TB
    CH = 512
    with ExitStack() as ctx:
        def sb(name, shape, dt=F32):
            return ctx.enter_context(nc.sbuf_tensor(name, shape, dt))

        def sem(name):
            return ctx.enter_context(nc.semaphore(name))

        w_t = sb("t_w", [P, FT, D])
        ident = sb("t_ident", [P, P])
        ident_b = sb("t_identb", [P, P], BF16)
        x_f = [sb(f"t_x{j}", [P, KD, TB]) for j in range(2)]
        part = [[sb(f"t_part{j}{s}", [P, KD, TB], BF16) for s in range(3)] for j in range(2)]
        rest = sb("t_rest", [P, KD, TB])
        rest2 = sb("t_rest2", [P, KD, TB])
        acc = [sb(f"t_acc{j}", [P, FT, TB]) for j in range(2)]
        row = [ctx.enter_context(nc.psum_tensor(f"t_row{r}", [P, TB], F32)) for r in range(2)]

        const_in = sem("t_const_in")
        x_in = [sem(f"t_x_in{j}") for j in range(2)]
        stored = [sem(f"t_stored{j}") for j in range(2)]
        ident_ready = sem("t_ident_ready")
        hi_ready, rest_ready, mid_ready, rest2_ready, lo_ready = (
            sem(f"t_{n}_ready") for n in ("hi", "rest", "mid", "rest2", "lo"))
        row_ready, row_free, low_half = sem("t_row_ready"), sem("t_row_free"), sem("t_low_half")
        block = ctx.enter_context(nc.Block())

        @block.sync
        def _(sp):
            sp.dma_start(w_t[:, :, :], a["Wt"].rearrange("(t p) d -> p t d", p=P)).then_inc(const_in, 16)
            sp.dma_start(ident[:, :], a["ident"]).then_inc(const_in, 16)

            def load(m, j):
                sp.dma_start(x_f[j][:, :, :], xn3t_dram[:, :, ds(m * TB, TB)].rearrange("k p t -> p k t"))\
                  .then_inc(x_in[j], 16)

            def store(m, j):
                sp.wait_ge(row_free, (m + 1) * D + 2)
                sp.dma_start(t_dram[:, :, ds(m * TB, TB)].rearrange("f p t -> p f t"), acc[j][:, :, :])\
                  .then_inc(stored[j], 16)

            for j in range(2):
                load(j, j)
            with sp.Fori(0, BLOCKS // 2 - 1) as i:
                for j in range(2):
                    store(2 * i + j, j)
                    load(2 * i + j + 2, j)
            for j in range(2):
                store(BLOCKS - 2 + j, j)
            for j in range(2):
                sp.wait_ge(stored[j], 16 * (BLOCKS // 2))

        @block.scalar
        def _(act):
            act.wait_ge(const_in, 32)
            act.activation(ident_b[:, :], ident[:, :], ACT.Copy).then_inc(ident_ready, 1)

            def split(i, j, first):
                m = 2 * i + j
                act.wait_ge(x_in[j], 16 * (i + 1))
                if not first:
                    act.wait_ge(row_ready, (m - 1) * D)
                act.activation(part[j][0][:, :, :], x_f[j][:, :, :], ACT.Copy).then_inc(hi_ready, 1)
                act.wait_ge(rest_ready, m + 1)
                act.activation(part[j][1][:, :, :], rest[:, :, :], ACT.Copy).then_inc(mid_ready, 1)
                act.wait_ge(rest2_ready, m + 1)
                act.activation(part[j][2][:, :, :], rest2[:, :, :], ACT.Copy).then_inc(lo_ready, 1)

            for j in range(2):
                split(0, j, True)
            with act.Fori(1, BLOCKS // 2) as i:
                for j in range(2):
                    split(i, j, False)

        @block.gpsimd
        def _(pool):
            with pool.Fori(0, BLOCKS // 2) as i:
                for j in range(2):
                    m = 2 * i + j
                    pool.wait_ge(hi_ready, m + 1)
                    pool.tensor_tensor(rest[:, :, :], x_f[j][:, :, :], part[j][0][:, :, :], ALU.subtract)\
                        .then_inc(rest_ready, 1)
                    pool.wait_ge(mid_ready, m + 1)
                    pool.tensor_tensor(rest2[:, :, :], rest[:, :, :], part[j][1][:, :, :], ALU.subtract)\
                        .then_inc(rest2_ready, 1)

        @block.tensor
        def _(pe):
            pe.wait_ge(ident_ready, 1)

            def spread(d0, g, k, j, r):
                pe.wait_ge(row_free, g + 1)
                one_row = ident_b[:, ds(d0, 1)].to_broadcast([P, P])
                for c in range(TB // CH):
                    for s in range(3):
                        mm = pe.matmul(row[r][:, c * CH:(c + 1) * CH], one_row, part[j][s][:, k, c * CH:(c + 1) * CH],
                                       start=(s == 0), stop=(s == 2))
                mm.then_inc(row_ready, 1)

            with pe.Fori(0, BLOCKS // 2) as i:
                for j in range(2):
                    for k in range(KD):
                        with pe.Fori(0, P // 2) as pair:
                            pe.wait_ge(lo_ready, 2 * i + j + 1)
                            for r in range(2):
                                spread(2 * pair + r, (2 * i + j) * D + k * P + 2 * pair + r, k, j, r)

        @block.vector
        def _(dve):
            dve.wait_ge(const_in, 32)
            dve.sem_inc(row_free, 2)

            def use(d, g, j, r, first):
                dve.wait_ge(row_ready, g + 1)
                for f in range(FT):
                    if not first and f == 0:
                        dve.wait_ge(low_half, g)
                    if not first and f == FT // 2:
                        dve.wait_ge(row_free, g + 2)
                    if first:
                        op = dve.tensor_scalar(acc[j][:, f, :], row[r][:, :], w_t[:, f, ds(d, 1)], None, ALU.add)
                    else:
                        op = dve.scalar_tensor_tensor(acc[j][:, f, :], row[r][:, :], w_t[:, f, ds(d, 1)],
                                                      acc[j][:, f, :], ALU.add, ALU.max)
                    if f == FT // 2 - 1:
                        op.then_inc(low_half, 1)
                op.then_inc(row_free, 1)

            def whole(i, j):
                m = 2 * i + j
                wait_past(dve, stored[j], 16 * i)
                for r in range(2):
                    use(r, m * D + r, j, r, r == 0)
                with dve.Fori(1, D // 2) as pair:
                    for r in range(2):
                        use(2 * pair + r, m * D + 2 * pair + r, j, r, False)

            for j in range(2):
                whole(0, j)
            with dve.Fori(1, BLOCKS // 2) as i:
                for j in range(2):
                    whole(i, j)


def stage_ffn(nc, a, x3t_dram, xn3t_dram, t_dram, out):
    CB = 512
    BLOCKS = TOK // CB
    with ExitStack() as ctx:
        def sb(name, shape, dt=F32):
            return ctx.enter_context(nc.sbuf_tensor(name, shape, dt))

        def ps(name):
            return ctx.enter_context(nc.psum_tensor(name, [P, CB], F32))

        def sem(name):
            return ctx.enter_context(nc.semaphore(name))

        def sems(*names):
            return [sem("f_" + n) for n in names]

        w_c = sb("f_wc", [P, KD, FFN])
        w_g = sb("f_wg", [P, KD, FFN])
        w_d = sb("f_wd", [P, FT, D])
        slope = [sb(f"f_slope{s}", [P, FT, PIECES]) for s in range(2)]
        offset = [sb(f"f_offset{s}", [P, FT, PIECES]) for s in range(2)]
        shift = [sb(f"f_shift{s}", [P, FT, PIECES]) for s in range(2)]
        b_t, b_c, b_g = sb("f_bt", [P, FT]), sb("f_bc", [P, FT]), sb("f_bg", [P, FT])
        alpha = sb("f_alpha", [P, FT])
        b_d = sb("f_bd", [P, KD])
        half_bg = sb("f_half_bg", [P, FT])
        tanh_a = sb("f_tanh_a", [P, FT])
        share = [sb(f"f_share{s}", [P, FT]) for s in range(2)]
        x3 = [sb(f"f_x3{j}", [P, KD, CB]) for j in range(2)]
        x = [sb(f"f_x{j}", [P, KD, CB]) for j in range(2)]
        t = [sb(f"f_t{j}", [P, FT, CB]) for j in range(2)]
        lines = [[sb(f"f_lines{v}{s}", [P, PIECES, CB]) for s in range(2)] for v in range(2)]
        cls = [sb(f"f_cls{v}", [P, CB]) for v in range(2)]
        th = [sb(f"f_th{v}", [P, CB]) for v in range(2)]
        convex = sb("f_convex", [P, CB])
        trop = [sb(f"f_trop{v}", [P, CB]) for v in range(2)]
        diff = [sb(f"f_diff{v}", [P, CB]) for v in range(2)]
        gated = [sb(f"f_gated{v}", [P, CB]) for v in range(2)]
        fused = [sb(f"f_fused{v}", [P, CB]) for v in range(2)]
        o_b = sb("f_ob", [P, KD, CB])
        o_x = [sb(f"f_ox{j}", [P, KD, CB]) for j in range(2)]
        ps_c = [ps(f"f_psc{v}") for v in range(2)]
        ps_g = [ps(f"f_psg{v}") for v in range(2)]
        ps_o = [[ps(f"f_pso{j}{k}") for k in range(KD)] for j in range(2)]

        const_in, consts_ready = sems("const_in", "consts_ready")
        shift_ready, = sems("shift_ready")
        block_in = sems("block_in0", "block_in1")
        stored = sems("stored0", "stored1")
        c_done, g_done, cls_ready, th_ready = sems("c_done", "g_done", "cls_ready", "th_ready")
        lines_ready = sems("convex_lines_ready", "concave_lines_ready")
        trop_ready, diff_ready, gated_ready, fused_ready = sems("trop_ready", "diff_ready", "gated_ready", "fused_ready")
        fused_used, ob_ready, ox_ready = sems("fused_used", "ob_ready", "ox_ready")
        dve_steps = Steps(sem("f_dve_steps"), 7)

        block = ctx.enter_context(nc.Block())
        PIECE_CONSTS = ((slope[0], "sl_cvx"), (offset[0], "of_cvx"), (slope[1], "sl_ccv"), (offset[1], "of_ccv"))
        VECTORS = ((b_t, "bt"), (b_c, "bc"), (b_g, "bg"), (alpha, "alpha"), (b_d, "bd"))
        CONSTS = 3 + len(PIECE_CONSTS) + len(VECTORS)

        def rounds(eng, body):
            for j in range(2):
                body(0, j, j, True)
            with eng.Fori(1, BLOCKS // 2) as i:
                for j in range(2):
                    body(i, j, 2 * i + j, False)

        @block.sync
        def _(sp):
            sp.dma_start(w_c[:, :, :], a["Wc"].rearrange("(k p) f -> p k f", p=P)).then_inc(const_in, 16)
            sp.dma_start(w_g[:, :, :], a["Wg"].rearrange("(k p) f -> p k f", p=P)).then_inc(const_in, 16)
            sp.dma_start(w_d[:, :, :], a["Wd"].rearrange("(t p) d -> p t d", p=P)).then_inc(const_in, 16)
            for dst, name in PIECE_CONSTS:
                sp.dma_start(dst[:, :, :], a[name].rearrange("(t p) q -> p t q", p=P)).then_inc(const_in, 16)
            for dst, name in VECTORS:
                sp.dma_start(dst[:, :], a[name]).then_inc(const_in, 16)

            def load(m, j):
                sp.dma_start(x[j][:, :, :], xn3t_dram[:, :, ds(m * CB, CB)].rearrange("k p t -> p k t"))\
                  .then_inc(block_in[j], 16)
                sp.dma_start(x3[j][:, :, :], x3t_dram[:, :, ds(m * CB, CB)].rearrange("k p t -> p k t"))\
                  .then_inc(block_in[j], 16)
                sp.dma_start(t[j][:, :, :], t_dram[:, :, ds(m * CB, CB)].rearrange("f p t -> p f t"))\
                  .then_inc(block_in[j], 16)

            def store(m, j):
                sp.wait_ge(ox_ready, m + 1)
                sp.dma_start(out[:, :, ds(m * CB, CB)].rearrange("k p t -> p k t"), o_x[j][:, :, :])\
                  .then_inc(stored[j], 16)

            for j in range(2):
                load(j, j)
            with sp.Fori(0, BLOCKS // 2 - 1) as i:
                for j in range(2):
                    store(2 * i + j, j)
                    load(2 * i + j + 2, j)
            for j in range(2):
                store(BLOCKS - 2 + j, j)
            for j in range(2):
                sp.wait_ge(stored[j], 16 * (BLOCKS // 2) + 16)

        @block.gpsimd
        def _(pool):
            def body(i, j, m, first):
                for u in range(FT):
                    v, q = u % 2, m * FT + u
                    pool.wait_ge(cls_ready, q + 1)
                    pool.wait_ge(trop_ready, q + 1)
                    pool.tensor_tensor(diff[v][:, :], trop[v][:, :], cls[v][:, :], ALU.subtract).then_inc(diff_ready, 1)
                    if u == 3 and not (first and j == 0):
                        total(m - 1, 1 - j, i if j else i - 1)

            def total(m, j, i):
                pool.wait_ge(stored[j], 16 * i + 16)
                pool.wait_ge(ob_ready, m + 1)
                pool.tensor_tensor(o_x[j][:, :, :], o_b[:, :, :], x3[j][:, :, :], ALU.add).then_inc(ox_ready, 1)

            for j in range(2):
                pool.sem_inc(stored[j], 16)
            rounds(pool, body)
            total(BLOCKS - 1, 1, BLOCKS // 2 - 1)

        @block.scalar
        def _(act):
            act.wait_ge(const_in, 16 * CONSTS)
            act.activation(tanh_a[:, :], alpha[:, :], ACT.Tanh, scale=0.5).then_inc(consts_ready, 1)
            act.activation(half_bg[:, :], b_g[:, :], ACT.Copy, scale=0.5).then_inc(consts_ready, 1)
            act.wait_ge(consts_ready, 2)
            act.wait_ge(shift_ready, 4 * FT)

            def body(i, j, m, first):
                act.wait_ge(block_in[j], 48 * (i + 1))
                for u in range(FT):
                    v, q = u % 2, m * FT + u
                    if not (first and j == 0 and u < 2):
                        act.wait_ge(trop_ready, q - 1)
                    for s in range(2):
                        for n in range(PIECES):
                            last = act.activation(lines[v][s][:, n, :], t[j][:, u, :], ACT.Identity,
                                                  scale=slope[s][:, u, n:n + 1], bias=shift[s][:, u, n:n + 1])
                        last.then_inc(lines_ready[s], 1)
                    act.wait_ge(c_done, q + 1)
                    if not (first and j == 0 and u < 2):
                        act.wait_ge(fused_ready, q - 1)
                    act.activation(cls[v][:, :], ps_c[v][:, :], ACT.Gelu, bias=b_c[:, u:u + 1]).then_inc(cls_ready, 1)
                    act.wait_ge(g_done, q + 1)
                    act.activation(th[v][:, :], ps_g[v][:, :], ACT.Tanh, scale=0.5, bias=half_bg[:, u:u + 1])\
                       .then_inc(th_ready, 1)
                    if u == 2 and not (first and j == 0):
                        finish(m - 1, 1 - j)

            def finish(m, j):
                act.wait_ge(fused_used, (m + 1) * FT)
                wait_past(act, ox_ready, m)
                for k in range(KD):
                    last = act.activation(o_b[:, k, :], ps_o[j][k][:, :], ACT.Identity, bias=b_d[:, k:k + 1])
                last.then_inc(ob_ready, 1)

            rounds(act, body)
            finish(BLOCKS - 1, 1)

        @block.tensor
        def _(pe):
            pe.wait_ge(const_in, 16 * CONSTS)

            def output_part(m, j, u, early):
                v, q = u % 2, m * FT + u
                if u == 0 and not early:
                    pe.wait_ge(ob_ready, m - 1)
                pe.wait_ge(fused_ready, q + 1)
                for k in range(KD):
                    mm = pe.matmul(ps_o[j][k][:, :], w_d[:, u, k * P:(k + 1) * P], fused[v][:, :],
                                   start=(u == 0), stop=(u == FT - 1))
                mm.then_inc(fused_used, 1)

            def body(i, j, m, first):
                pe.wait_ge(block_in[j], 48 * (i + 1))
                for u in range(FT):
                    v, q = u % 2, m * FT + u
                    for ps_, w_, done, read in ((ps_c, w_c, c_done, cls_ready), (ps_g, w_g, g_done, th_ready)):
                        if not (first and j == 0 and u < 2):
                            pe.wait_ge(read, q - 1)
                        for k in range(KD):
                            mm = pe.matmul(ps_[v][:, :], w_[:, k, u * P:(u + 1) * P], x[j][:, k, :],
                                           start=(k == 0), stop=(k == KD - 1))
                        mm.then_inc(done, 1)
                    if u > 0:
                        output_part(m, j, u - 1, first)
                    elif not (first and j == 0):
                        output_part(m - 1, 1 - j, FT - 1, first)

            rounds(pe, body)
            output_part(BLOCKS - 1, 1, FT - 1, False)

        @block.vector
        def _(dve):
            dve.wait_ge(const_in, 16 * CONSTS)
            for s in range(2):
                for u in range(FT):
                    dve.tensor_scalar(shift[s][:, u, :], slope[s][:, u, :], b_t[:, u:u + 1], None, ALU.mult)\
                       .then_inc(shift_ready, 1)
            dve.wait_ge(shift_ready, 2 * FT)
            for s in range(2):
                for u in range(FT):
                    dve.tensor_tensor(shift[s][:, u, :], shift[s][:, u, :], offset[s][:, u, :], ALU.add)\
                       .then_inc(shift_ready, 1)
            dve.wait_ge(consts_ready, 2)
            dve.tensor_scalar(share[0][:, :], tanh_a[:, :], 0.5, 0.5, ALU.mult, ALU.add).then_inc(consts_ready, 1)
            dve.tensor_scalar(share[1][:, :], tanh_a[:, :], -0.5, 0.5, ALU.mult, ALU.add).then_inc(consts_ready, 1)
            dve.wait_ge(consts_ready, 4)

            def fuse(m, u, peeled):
                v, q = u % 2, m * FT + u
                dve.wait_ge(diff_ready, q + 1)
                dve.wait_ge(th_ready, q + 1)
                dve.scalar_tensor_tensor(gated[v][:, :], th[v][:, :], 1.0, diff[v][:, :], ALU.add, ALU.mult)\
                   .then_inc(gated_ready, 1)
                dve.wait_ge(gated_ready, q + 1)
                if not peeled:
                    dve.wait_ge(fused_used, q - 1)
                dve.scalar_tensor_tensor(fused[v][:, :], gated[v][:, :], 0.5, cls[v][:, :], ALU.mult, ALU.add)\
                   .then_inc(fused_ready, 1)

            def body(i, j, m, first):
                for u in range(FT):
                    v, q = u % 2, m * FT + u
                    dve_steps.begin(q)
                    for s, op in ((0, ALU.max), (1, ALU.min)):
                        dve.wait_ge(lines_ready[s], q + 1)
                        l = lines[v][s]
                        for n in (4, 2, 1):
                            w = dve_steps.done(dve.tensor_tensor(l[:, 0:n, :], l[:, 0:n, :], l[:, n:2 * n, :], op))
                            dve.wait_ge(dve_steps.sem, w)
                    w = dve_steps.done(dve.tensor_scalar(convex[:, :], lines[v][0][:, 0, :], share[0][:, u:u + 1],
                                                         None, ALU.mult))
                    dve.wait_ge(dve_steps.sem, w)
                    dve.scalar_tensor_tensor(trop[v][:, :], lines[v][1][:, 0, :], share[1][:, u:u + 1], convex[:, :],
                                             ALU.mult, ALU.add).then_inc(trop_ready, 1)
                    dve_steps.end()
                    if u > 0:
                        fuse(m, u - 1, first and j == 0 and u < 3)
                    elif not (first and j == 0):
                        fuse(m - 1, FT - 1, False)

            rounds(dve, body)
            fuse(BLOCKS - 1, FT - 1, False)


def full_kernel(nc, a, out):
    x1_dram = nc.dram_tensor("x1_kept", [B, N, D], F32, kind="Internal").ap()
    x3t_dram = nc.dram_tensor("x3_transposed", [KD, P, TOK], F32, kind="Internal").ap()
    xn3t_dram = nc.dram_tensor("x3_normalised_transposed", [KD, P, TOK], F32, kind="Internal").ap()
    t_dram = nc.dram_tensor("t_transposed", [FT, P, TOK], F32, kind="Internal").ap()
    with ExitStack() as ctx:
        hx = ctx.enter_context(nc.sbuf_tensor("hx", [P, KD, 1 + N, B], F32))
        stage_gnn0(nc, a, hx, x1_dram)
        stage_lstm(nc, a, hx)
        stage_gnn1(nc, a, hx, x1_dram, x3t_dram, xn3t_dram)
    stage_tropical(nc, a, xn3t_dram, t_dram)
    stage_ffn(nc, a, x3t_dram, xn3t_dram, t_dram, out)


def kernel(**inputs):
    import concourse.bacc as bacc
    from concourse.bass_utils import run_bass_kernel_spmd

    given = {k: np.asarray(v) for k, v in inputs.items()}

    def gates_first_g(w):
        i, f, g, o = np.split(w, GATES, axis=0)
        return np.ascontiguousarray(np.concatenate([g, i, f, o], axis=0))

    def turned(w):
        return np.ascontiguousarray(w.T)

    def columns(v):
        return np.ascontiguousarray(v.reshape(-1, P).T)

    which = np.zeros((2, 2, 2, 4 * B), np.float32)
    which[:, 0, 0], which[:, 1, 1] = 1.0, 1.0
    ones = np.ones((P, P), np.float32)
    arrays = {
        "x": given["x"], "adj": given["adj"],
        "adjt": np.ascontiguousarray(given["adj"].transpose(0, 2, 1)),
        "theta": given["L0_gnn_theta"], "W_h": given["L0_gnn_W_h"], "W_t": given["L0_gnn_W_t"],
        "b_t": given["L0_gnn_b_t"].reshape(1, D),
        "w_ih_t": turned(gates_first_g(given["L0_ffn_W_ih"])),
        "w_hh_t": turned(gates_first_g(given["L0_ffn_W_hh"])),
        "b_ih": gates_first_g(given["L0_ffn_b_ih"]), "b_hh": gates_first_g(given["L0_ffn_b_hh"]),
        "w_lin_t": turned(given["L0_ffn_W_lin"]), "b_lin": given["L0_ffn_b_lin"].reshape(1, 2),
        "fw_att": given["L0_ffn_fw_att"], "bw_att": given["L0_ffn_bw_att"],
        "W1": given["L1_gnn_W"], "b1": given["L1_gnn_b"].reshape(1, D),
        "Wt": given["L1_ffn_Wt"], "Wc": given["L1_ffn_Wc"], "Wg": given["L1_ffn_Wg"], "Wd": given["L1_ffn_Wd"],
        "sl_cvx": given["L1_ffn_sl_cvx"], "of_cvx": given["L1_ffn_of_cvx"],
        "sl_ccv": given["L1_ffn_sl_ccv"], "of_ccv": given["L1_ffn_of_ccv"],
        "bt": columns(given["L1_ffn_bt"]), "bc": columns(given["L1_ffn_bc"]), "bg": columns(given["L1_ffn_bg"]),
        "alpha": columns(given["L1_ffn_alpha"]), "bd": columns(given["L1_ffn_bd"]),
        "ident": np.eye(P, dtype=np.float32),
        "before": np.triu(ones, 1), "after": np.tril(ones, -1), "which": which.reshape(4, 2 * 4 * B),
    }
    nc = bacc.Bacc("TRN2", target_bir_lowering=False, num_devices=1)
    a = {k: nc.dram_tensor(f"in_{k}", v.shape, mybir.dt.from_np(v.dtype), kind="ExternalInput").ap()
         for k, v in arrays.items()}
    out = nc.dram_tensor("out_t", [KD, P, TOK], F32, kind="ExternalOutput").ap()
    full_kernel(nc, a, out)
    r = run_bass_kernel_spmd(nc, [{f"in_{k}": v for k, v in arrays.items()}], core_ids=[0])
    out_t = np.asarray(r.results[0]["out_t"]).reshape(D, TOK)
    return np.ascontiguousarray(out_t.T).reshape(B, N, D)
```

```python
from contextlib import ExitStack
import numpy as np
import concourse.bass as bass
from concourse import mybir

F32 = mybir.dt.float32
BF16 = mybir.dt.bfloat16
ALU = mybir.AluOpType
ACT = mybir.ActivationFunctionType
AX = mybir.AxisListType
ds = bass.ds

P = 128
B, N, D = 64, 256, 256
KD = D // P
NT = N // P
TOK = B * N
H = 256
GATES = 4
FFN, PIECES = 1024, 8
FT = FFN // P
LN_EPS = 1e-5


def wait_past(eng, sem, value):
    if not isinstance(value, int) or value > 0:
        eng.wait_ge(sem, value)


def graph_rounds(eng, body):
    for j in range(2):
        body(0, j, j)
    with eng.Fori(1, B // 2) as i:
        for j in range(2):
            body(i, j, 2 * i + j)


def clear_semaphores(nc, sems):
    with nc.Block() as block:
        @block.sync
        def _(sp):
            for s in sems:
                sp.sem_clear(s)


class Steps:

    def __init__(self, sem, per):
        self.sem, self.per = sem, per

    def begin(self, round_):
        self.base, self.k = round_ * self.per, 0

    def done(self, instruction):
        instruction.then_inc(self.sem, 1)
        self.k += 1
        return self.base + self.k

    def end(self):
        assert self.k == self.per, (self.k, self.per)


def stage_gnn0(nc, a, hx, x1_dram):
    sems = []
    with ExitStack() as ctx:
        def sb(name, shape, dt=F32):
            return ctx.enter_context(nc.sbuf_tensor(name, shape, dt))

        def ps(name, shape):
            return ctx.enter_context(nc.psum_tensor(name, shape, F32))

        def sem(name):
            sems.append(ctx.enter_context(nc.semaphore(name)))
            return sems[-1]

        w_cat = sb("g0_w", [P, KD, 3 * D])
        bt_row = sb("g0_bt", [1, D])
        ones_row = sb("g0_ones", [1, P])
        pause = sb("g0_pause", [1, 1])
        ident = sb("g0_ident", [P, P])
        x_in = [sb(f"g0_x{j}", [P, NT, D]) for j in range(2)]
        adj_in = [sb(f"g0_adj{j}", [P, NT, N]) for j in range(2)]
        adjt_in = [sb(f"g0_adjt{j}", [P, NT, N]) for j in range(2)]
        x1_out = [sb(f"g0_x1{j}", [P, NT, D]) for j in range(2)]
        stats = sb("g0_stats", [P, NT, 6])
        mv = sb("g0_mv", [P, NT, 2])
        rstd = sb("g0_rstd", [P, NT])
        mv1 = sb("g0_mv1", [P, NT, 2])
        rstd1 = sb("g0_rstd1", [P, NT])
        half = sb("g0_half", [P, NT])
        eps_ln = sb("g0_eps_ln", [P, NT])
        eps_deg = sb("g0_eps_deg", [P, NT])
        vare = sb("g0_vare", [P, NT])
        dege = sb("g0_dege", [P, NT])
        deg = sb("g0_deg", [P, NT])
        norm = sb("g0_norm", [P, NT])
        junk = sb("g0_junk", [P, NT, N])
        xn = sb("g0_xn", [P, NT, D])
        xn_t = sb("g0_xnt", [P, KD, N])
        f_hom = sb("g0_fhom", [P, NT, D])
        f_het = sb("g0_fhet", [P, NT, D])
        tanh_z = sb("g0_tanh_z", [P, NT, D])
        gate = sb("g0_gate", [P, NT, D])
        u = sb("g0_u", [P, NT, D])
        o = sb("g0_o", [P, NT, D])
        neg = sb("g0_neg", [P, NT, D])
        y = sb("g0_y", [P, NT, D])
        ps_t = ps("g0_pst", [P, KD, N])
        ps_hom_het = [ps(f"g0_psa{t}", [P, 2 * D]) for t in range(NT)]
        ps_gate = ps("g0_psg", [P, NT, D])
        ps_agg = ps("g0_psf", [P, NT, D])
        ps_t1 = ps("g0_pst1", [P, KD, N])

        const_in = sem("g0_const_in")
        graph_in = [sem(f"g0_graph_in{j}") for j in range(2)]
        x1_stored = [sem(f"g0_x1_stored{j}") for j in range(2)]
        half_set = sem("g0_half_set")
        ones_set = sem("g0_ones_set")
        dve_steps = Steps(sem("g0_dve_steps"), 7)
        pool_steps = Steps(sem("g0_pool_steps"), 3)
        mv_ready = sem("g0_mv_ready")
        rstd_ready = sem("g0_rstd_ready")
        xn_ready = sem("g0_xn_ready")
        xt_done = sem("g0_xt_done")
        xn_t_ready = sem("g0_xn_t_ready")
        proj_done = sem("g0_proj_done")
        gate_done = sem("g0_gate_done")
        deg_ready = sem("g0_deg_ready")
        norm_ready = sem("g0_norm_ready")
        f_hom_ready = sem("g0_f_hom_ready")
        f_het_ready = sem("g0_f_het_ready")
        tanh_z_ready = sem("g0_tanh_z_ready")
        agg_done = sem("g0_agg_done")
        neg_ready = sem("g0_neg_ready")
        exp_ready = sem("g0_exp_ready")
        x1_ready = sem("g0_x1_ready")
        mv1_ready = sem("g0_mv1_ready")
        rstd1_ready = sem("g0_rstd1_ready")
        xn1_ready = sem("g0_xn1_ready")
        xt1_done = sem("g0_xt1_done")
        hx_written = sem("g0_hx_written")
        CONST_DMAS = 5

        block = ctx.enter_context(nc.Block())

        @block.sync
        def _(sp):
            sp.dma_start(w_cat[:, :, 0:D], a["theta"].rearrange("(k p) e -> p k e", p=P)).then_inc(const_in, 16)
            sp.dma_start(w_cat[:, :, D:2 * D], a["W_h"].rearrange("(k p) e -> p k e", p=P)).then_inc(const_in, 16)
            sp.dma_start(w_cat[:, :, 2 * D:3 * D], a["W_t"].rearrange("(k p) e -> p k e", p=P)).then_inc(const_in, 16)
            sp.dma_start(bt_row[:, :], a["b_t"]).then_inc(const_in, 16)
            sp.dma_start(ident[:, :], a["ident"]).then_inc(const_in, 16)

            def load(n, j):
                for dst, src in ((x_in, "x"), (adj_in, "adj"), (adjt_in, "adjt")):
                    sp.dma_start(dst[j][:, :, :], a[src][ds(n, 1)].rearrange("o (t p) e -> p (o t) e", p=P))\
                      .then_inc(graph_in[j], 16)

            def store(n, j):
                sp.wait_ge(x1_ready, n + 1)
                sp.dma_start(x1_dram[ds(n, 1)].rearrange("o (t p) e -> p (o t) e", p=P), x1_out[j][:, :, :])\
                  .then_inc(x1_stored[j], 16)

            for j in range(2):
                load(j, j)
            with sp.Fori(0, B // 2 - 1) as i:
                for j in range(2):
                    store(2 * i + j, j)
                    load(2 * i + j + 2, j)
            for j in range(2):
                store(B - 2 + j, j)
            for j in range(2):
                sp.wait_ge(x1_stored[j], 16 * (B // 2))

        @block.gpsimd
        def _(pool):
            pool.memset(half[:, :], -0.5).then_inc(half_set, 1)
            pool.memset(eps_ln[:, :], LN_EPS).then_inc(half_set, 1)
            pool.memset(eps_deg[:, :], 1e-6).then_inc(half_set, 1)
            pool.wait_ge(half_set, 3)

            def body(i, j, n):
                pool_steps.begin(n)
                pool.wait_ge(mv_ready, n + 1)
                t = pool_steps.done(pool.tensor_tensor(vare[:, :], mv[:, :, 1], eps_ln[:, :], ALU.add))
                pool.wait_ge(pool_steps.sem, t)
                pool.tensor_tensor(rstd[:, :], vare[:, :], half[:, :], ALU.pow).then_inc(rstd_ready, 1)
                pool.wait_ge(deg_ready, n + 1)
                t = pool_steps.done(pool.tensor_tensor(dege[:, :], deg[:, :], eps_deg[:, :], ALU.add))
                pool.wait_ge(pool_steps.sem, t)
                pool.tensor_tensor(norm[:, :], dege[:, :], half[:, :], ALU.pow).then_inc(norm_ready, 1)
                pool.wait_ge(mv1_ready, n + 1)
                t = pool_steps.done(pool.tensor_tensor(vare[:, :], mv1[:, :, 1], eps_ln[:, :], ALU.add))
                pool.wait_ge(pool_steps.sem, t)
                pool.tensor_tensor(rstd1[:, :], vare[:, :], half[:, :], ALU.pow).then_inc(rstd1_ready, 1)
                pool_steps.end()

            graph_rounds(pool, body)

        @block.scalar
        def _(act):
            def body(i, j, n):
                act.wait_ge(graph_in[j], 48 * (i + 1))
                wait_past(act, x1_ready, n)
                for t in range(NT):
                    last = act.activation(junk[:, t, :], adj_in[j][:, t, :], ACT.Abs, accum_out=deg[:, t:t + 1])
                last.then_inc(deg_ready, 1)
                act.wait_ge(xt_done, n + 1)
                act.activation(xn_t[:, :, :], ps_t[:, :, :], ACT.Copy).then_inc(xn_t_ready, 1)
                act.wait_ge(norm_ready, n + 1)
                act.wait_ge(proj_done, n + 1)
                for t in range(NT):
                    last = act.activation(f_hom[:, t, :], ps_hom_het[t][:, 0:D], ACT.Copy, scale=norm[:, t:t + 1])
                last.then_inc(f_hom_ready, 1)
                for t in range(NT):
                    last = act.activation(f_het[:, t, :], ps_hom_het[t][:, D:2 * D], ACT.Copy)
                last.then_inc(f_het_ready, 1)
                act.wait_ge(gate_done, n + 1)
                act.activation(tanh_z[:, :, :], ps_gate[:, :, :], ACT.Tanh, scale=0.5).then_inc(tanh_z_ready, 1)
                act.wait_ge(neg_ready, n + 1)
                act.activation(neg[:, :, :], neg[:, :, :], ACT.Exp).then_inc(exp_ready, 1)
                act.wait_ge(xt1_done, n + 1)
                act.activation(hx[:, :, 1:1 + N, ds(n, 1)].rearrange("p k t o -> p k (t o)"), ps_t1[:, :, :], ACT.Copy)\
                   .then_inc(hx_written, 1)

            graph_rounds(act, body)

        @block.tensor
        def _(pe):
            pe.wait_ge(const_in, 16 * CONST_DMAS)
            pe.wait_ge(ones_set, 1)

            def turn(dst, src):
                for k in range(KD):
                    for t in range(NT):
                        last = pe.transpose(dst[:, k, t * P:(t + 1) * P], src[:, t, k * P:(k + 1) * P], ident[:, :])
                return last

            def body(i, j, n):
                pe.wait_ge(xn_ready, n + 1)
                turn(ps_t, xn).then_inc(xt_done, 1)
                pe.wait_ge(xn_t_ready, n + 1)
                for t in range(NT):
                    for k in range(KD):
                        last = pe.matmul(ps_hom_het[t][:, :], xn_t[:, k, t * P:(t + 1) * P], w_cat[:, k, 0:2 * D],
                                         start=(k == 0), stop=(k == KD - 1))
                last.then_inc(proj_done, 1)
                for t in range(NT):
                    for k in range(KD):
                        pe.matmul(ps_gate[:, t, :], xn_t[:, k, t * P:(t + 1) * P], w_cat[:, k, 2 * D:3 * D],
                                  start=(k == 0), stop=False)
                    last = pe.matmul(ps_gate[:, t, :], ones_row[:, :], bt_row[:, :], start=False, stop=True)
                last.then_inc(gate_done, 1)
                pe.wait_ge(graph_in[j], 48 * (i + 1))
                pe.wait_ge(f_hom_ready, n + 1)
                for t in range(NT):
                    for m in range(NT):
                        last = pe.matmul(ps_agg[:, t, :], adjt_in[j][:, m, t * P:(t + 1) * P], f_hom[:, m, :],
                                         start=(m == 0), stop=(m == NT - 1))
                last.then_inc(agg_done, 1)
                pe.wait_ge(xn1_ready, n + 1)
                turn(ps_t1, xn).then_inc(xt1_done, 1)

            graph_rounds(pe, body)

        @block.vector
        def _(dve):
            dve.memset(ones_row[:, :], 1.0).then_inc(ones_set, 1)

            def normalise(src, mv_, mv_sem, rstd_, rstd_sem, xn_sem, n):
                for t in range(NT):
                    last = dve.bn_stats(stats[:, t, :], src[:, t, :])
                v = dve_steps.done(last)
                dve.wait_ge(dve_steps.sem, v)
                dve.memset(pause[:, :], 0.0)
                for t in range(NT):
                    last = dve.bn_aggr(mv_[:, t, :], stats[:, t, :])
                last.then_inc(mv_sem, 1)
                dve.wait_ge(rstd_sem, n + 1)
                for t in range(NT):
                    last = dve.tensor_scalar(xn[:, t, :], src[:, t, :], mv_[:, t, 0:1], rstd_[:, t:t + 1],
                                             ALU.subtract, ALU.mult)
                last.then_inc(xn_sem, 1)

            def body(i, j, n):
                dve_steps.begin(n)
                dve.wait_ge(graph_in[j], 48 * (i + 1))
                wait_past(dve, xt1_done, n)
                normalise(x_in[j], mv, mv_ready, rstd, rstd_ready, xn_ready, n)
                dve.wait_ge(tanh_z_ready, n + 1)
                v = dve_steps.done(dve.tensor_scalar(gate[:, :, :], tanh_z[:, :, :], 0.5, 0.5, ALU.mult, ALU.add))
                dve.wait_ge(agg_done, n + 1)
                dve.wait_ge(f_het_ready, n + 1)
                for t in range(NT):
                    last = dve.scalar_tensor_tensor(u[:, t, :], ps_agg[:, t, :], norm[:, t:t + 1], f_het[:, t, :],
                                                    ALU.mult, ALU.subtract)
                v = dve_steps.done(last)
                dve.wait_ge(dve_steps.sem, v)
                v = dve_steps.done(dve.tensor_tensor(u[:, :, :], u[:, :, :], gate[:, :, :], ALU.mult))
                dve.wait_ge(dve_steps.sem, v)
                v = dve_steps.done(dve.tensor_tensor(o[:, :, :], u[:, :, :], f_het[:, :, :], ALU.add))
                dve.wait_ge(dve_steps.sem, v)
                dve.tensor_scalar(neg[:, :, :], o[:, :, :], 0.0, None, ALU.min).then_inc(neg_ready, 1)
                v = dve_steps.done(dve.scalar_tensor_tensor(y[:, :, :], o[:, :, :], 0.0, x_in[j][:, :, :],
                                                            ALU.max, ALU.add))
                dve.wait_ge(dve_steps.sem, v)
                dve.wait_ge(exp_ready, n + 1)
                wait_past(dve, x1_stored[j], 16 * i)
                dve.scalar_tensor_tensor(x1_out[j][:, :, :], neg[:, :, :], -1.0, y[:, :, :],
                                         ALU.add, ALU.add).then_inc(x1_ready, 1)
                dve.wait_ge(x1_ready, n + 1)
                normalise(x1_out[j], mv1, mv1_ready, rstd1, rstd1_ready, xn1_ready, n)
                dve_steps.end()

            graph_rounds(dve, body)
    clear_semaphores(nc, sems)


def stage_lstm(nc, a, hx):
    T, S = N, 4
    ROWS = GATES * H // P
    sems = []
    with ExitStack() as ctx:
        def sb(name, shape, dt=F32):
            return ctx.enter_context(nc.sbuf_tensor(name, shape, dt))

        def sem(name):
            sems.append(ctx.enter_context(nc.semaphore(name)))
            return sems[-1]

        w_ih = sb("l_wih", [P, KD, GATES * H])
        w_hh = sb("l_whh", [P, KD, GATES * H])
        bias = sb("l_bias", [4, GATES, P])
        which = sb("l_which", [4, 2 * S * B])
        act_g = [sb(f"l_act{q}", [P, 2, B]) for q in range(GATES)]
        c = sb("l_c", [P, 2, B])
        ig = sb("l_ig", [P, 2, B])
        tc_ = sb("l_tc", [P, 2, B])
        ps_g = [[ctx.enter_context(nc.psum_tensor(f"l_ps{s}{q}", [P, 2, S, B], F32)) for q in range(GATES)]
                for s in range(2)]

        const_in = sem("l_const_in")
        zero_set = sem("l_zero_set")
        gate_done = [sem(f"l_gate_done{q}") for q in range(GATES)]
        act_ready = [sem(f"l_act_ready{q}") for q in range(GATES)]
        ig_ready = sem("l_ig_ready")
        fc_ready = sem("l_fc_ready")
        c_ready = sem("l_c_ready")
        tanh_c_ready = sem("l_tanh_c_ready")
        h_ready = sem("l_h_ready")
        block = ctx.enter_context(nc.Block())

        @block.sync
        def _(sp):
            sp.dma_start(w_ih[:, :, :], a["w_ih_t"].rearrange("(k p) g -> p k g", p=P)).then_inc(const_in, 16)
            sp.dma_start(w_hh[:, :, :], a["w_hh_t"].rearrange("(k p) g -> p k g", p=P)).then_inc(const_in, 16)
            sp.dma_start(bias[0:2, :, :], a["b_ih"].rearrange("(q c m) -> c q m", q=GATES, c=2)).then_inc(const_in, 16)
            sp.dma_start(bias[2:4, :, :], a["b_hh"].rearrange("(q c m) -> c q m", q=GATES, c=2)).then_inc(const_in, 16)
            sp.dma_start(which[:, :], a["which"]).then_inc(const_in, 16)

        @block.vector
        def _(dve):
            dve.memset(hx[:, :, 0:1, :], 0.0).then_inc(zero_set, 1)
            dve.memset(c[:, :, :], 0.0).then_inc(zero_set, 1)
            dve.wait_ge(zero_set, 2)

            def step(t):
                dve.wait_ge(act_ready[0], t + 1)
                dve.wait_ge(act_ready[1], t + 1)
                dve.tensor_tensor(ig[:, :, :], act_g[0][:, :, :], act_g[1][:, :, :], ALU.mult).then_inc(ig_ready, 1)
                dve.wait_ge(act_ready[2], t + 1)
                wait_past(dve, c_ready, t)
                dve.tensor_tensor(c[:, :, :], c[:, :, :], act_g[2][:, :, :], ALU.mult).then_inc(fc_ready, 1)
                dve.wait_ge(ig_ready, t + 1)
                dve.wait_ge(fc_ready, t + 1)
                dve.tensor_tensor(c[:, :, :], c[:, :, :], ig[:, :, :], ALU.add).then_inc(c_ready, 1)
                dve.wait_ge(act_ready[3], t + 1)
                dve.wait_ge(tanh_c_ready, t + 1)
                dve.tensor_tensor(hx[:, :, ds(t + 1, 1), :].rearrange("p k o b -> p k (o b)"), act_g[3][:, :, :],
                                  tc_[:, :, :], ALU.mult).then_inc(h_ready, 1)

            step(0)
            with dve.Fori(1, T) as t:
                step(t)

        @block.scalar
        def _(act):
            def step(t, s, r):
                for q in range(GATES):
                    act.wait_ge(gate_done[q], t + 1)
                    if q == 0:
                        wait_past(act, h_ready, t)
                    act.activation(act_g[q][:, :, :], ps_g[s][q][:, :, r, :], ACT.Tanh if q == 0 else ACT.Sigmoid)\
                       .then_inc(act_ready[q], 1)
                act.wait_ge(c_ready, t + 1)
                act.activation(tc_[:, :, :], c[:, :, :], ACT.Tanh).then_inc(tanh_c_ready, 1)

            def groups(i):
                for s in range(2):
                    for r in range(S):
                        step(2 * S * i + S * s + r, s, r)

            groups(0)
            with act.Fori(1, T // (2 * S)) as i:
                groups(i)

        @block.tensor
        def _(pe):
            def input_part(group, s, q):
                pe.matmul(ps_g[s][q][:, :, :, :], bias[:, q, :], which[:, :], start=True, stop=False,
                          skip_group_check=True)
                for c2 in range(2):
                    row = (2 * q + c2) * P
                    for k in range(KD):
                        pe.matmul(ps_g[s][q][:, c2, :, :], w_ih[:, k, row:row + P],
                                  hx[:, k, ds(S * group + 1, S), :], start=False, stop=False,
                                  skip_group_check=True)

            def steps(i, s, last):
                group = 2 * i + s
                for r in range(S):
                    t = S * group + r
                    wait_past(pe, h_ready, t)
                    for q in range(GATES):
                        for c2 in range(2):
                            row = (2 * q + c2) * P
                            for k in range(KD):
                                mm = pe.matmul(ps_g[s][q][:, c2, r, :], w_hh[:, k, row:row + P],
                                               hx[:, k, ds(t, 1), :].rearrange("p o b -> p (o b)"), start=False,
                                               stop=(r == S - 1 and c2 == 1 and k == KD - 1), skip_group_check=True)
                        mm.then_inc(gate_done[q], 1)
                    if not last:
                        input_part(group + 1, 1 - s, r)

            pe.wait_ge(const_in, 16 * 5)
            pe.wait_ge(zero_set, 2)
            for q in range(GATES):
                input_part(0, 0, q)
            for s in range(2):
                steps(0, s, False)
            with pe.Fori(1, T // (2 * S) - 1) as i:
                for s in range(2):
                    steps(i, s, False)
            for s in range(2):
                steps(T // (2 * S) - 1, s, s == 1)
    clear_semaphores(nc, sems)


def stage_gnn1(nc, a, hx, x1_dram, x3t_dram, xn3t_dram, xn3_dram):
    sems = []
    with ExitStack() as ctx:
        def sb(name, shape, dt=F32):
            return ctx.enter_context(nc.sbuf_tensor(name, shape, dt))

        def ps(name, shape):
            return ctx.enter_context(nc.psum_tensor(name, shape, F32))

        def sem(name):
            sems.append(ctx.enter_context(nc.semaphore(name)))
            return sems[-1]

        w = sb("g1_w", [P, KD, D])
        w_lin = sb("g1_wlin", [P, KD, 2])
        b_lin = sb("g1_blin", [1, 2])
        ones_row = sb("g1_ones_row", [1, P])
        ones_sq = sb("g1_ones_sq", [P, P])
        before = sb("g1_before", [P, P])
        after = sb("g1_after", [P, P])
        ident = sb("g1_ident", [P, P])
        fw = sb("g1_fw", [P, NT, D])
        bw = sb("g1_bw", [P, NT, D])
        b_all = sb("g1_b", [P, NT, D])
        x1_in = [sb(f"g1_x1{j}", [P, NT, D]) for j in range(2)]
        adj_in = [sb(f"g1_adj{j}", [P, NT, N]) for j in range(2)]
        adjt_in = [sb(f"g1_adjt{j}", [P, NT, N]) for j in range(2)]
        xn3_out = [sb(f"g1_xn3{j}", [P, NT, D]) for j in range(2)]
        x3t_out = [sb(f"g1_x3t{j}", [P, KD, N]) for j in range(2)]
        xn3t_out = [sb(f"g1_xn3t{j}", [P, KD, N]) for j in range(2)]
        mv3 = sb("g1_mv3", [P, NT, 2])
        rstd3 = sb("g1_rstd3", [P, NT])
        h_t = sb("g1_ht", [P, KD, N])
        h = sb("g1_h", [P, NT, D])
        logit = sb("g1_logit", [P, NT, 2])
        picked = sb("g1_picked", [P, NT])
        wh = sb("g1_wh", [P, NT, D])
        y = sb("g1_y", [P, NT, D])
        z = sb("g1_z", [P, NT, D])
        x2 = sb("g1_x2", [P, NT, D])
        x2b = sb("g1_x2b", [P, NT, D])
        x3 = sb("g1_x3", [P, NT, D])
        pause = sb("g1_pause", [1, 1])
        stats = sb("g1_stats", [P, NT, 6])
        mv = sb("g1_mv", [P, NT, 2])
        rstd = sb("g1_rstd", [P, NT])
        half = sb("g1_half", [P, NT])
        eps = sb("g1_eps", [P, NT])
        one = sb("g1_one", [P, NT])
        vare = sb("g1_vare", [P, NT])
        row_sum = sb("g1_row_sum", [P, NT])
        is_zero = sb("g1_is_zero", [P, NT])
        deg_safe = sb("g1_deg_safe", [P, NT])
        keep = sb("g1_keep", [P, NT])
        power = sb("g1_power", [P, NT])
        dinv = sb("g1_dinv", [P, NT])
        junk = sb("g1_junk", [P, NT, N])
        xn = sb("g1_xn", [P, NT, D])
        xn_t = sb("g1_xnt", [P, KD, N])
        hs = sb("g1_hs", [P, NT, D])
        ps_logit = ps("g1_ps_logit", [P, NT, 2])
        ps_h = ps("g1_ps_h", [P, NT, D])
        ps_pre = ps("g1_ps_pre", [P, NT, D])
        ps_suf = ps("g1_ps_suf", [P, NT, D])
        ps_t = ps("g1_ps_t", [P, KD, N])
        ps_w = ps("g1_ps_w", [P, NT, D])
        ps_agg = ps("g1_ps_agg", [P, NT, D])
        ps_x3t = ps("g1_ps_x3t", [P, KD, N])

        const_in = sem("g1_const_in")
        graph_in = [sem(f"g1_graph_in{j}") for j in range(2)]
        x3t_stored = [sem(f"g1_x3t_stored{j}") for j in range(2)]
        consts_set = sem("g1_consts_set")
        ones_set = sem("g1_ones_set")
        dve_steps = Steps(sem("g1_dve_steps"), 8)
        pool_steps = Steps(sem("g1_pool_steps"), 3)
        h_t_ready = sem("g1_h_t_ready")
        logit_done = sem("g1_logit_done")
        logit_ready = sem("g1_logit_ready")
        h_done = sem("g1_h_done")
        h_ready = sem("g1_h_ready")
        picked_ready = sem("g1_picked_ready")
        wh_ready = sem("g1_wh_ready")
        sums_done = sem("g1_sums_done")
        mv_ready = sem("g1_mv_ready")
        rstd_ready = sem("g1_rstd_ready")
        xn_ready = sem("g1_xn_ready")
        xt_done = sem("g1_xt_done")
        xn_t_ready = sem("g1_xn_t_ready")
        proj_done = sem("g1_proj_done")
        row_sum_ready = sem("g1_row_sum_ready")
        deg_ready = sem("g1_deg_ready")
        dinv_ready = sem("g1_dinv_ready")
        hs_ready = sem("g1_hs_ready")
        agg_done = sem("g1_agg_done")
        x3_ready = sem("g1_x3_ready")
        x3t_done = sem("g1_x3t_done")
        mv3_ready = sem("g1_mv3_ready")
        rstd3_ready = sem("g1_rstd3_ready")
        xn3_ready = sem("g1_xn3_ready")
        xn3t_done = sem("g1_xn3t_done")
        xn3t_ready = sem("g1_xn3t_ready")
        CONSTS = ("w", "w_lin", "b_lin", "ident", "before", "after", "fw", "bw", "b")

        block = ctx.enter_context(nc.Block())

        @block.sync
        def _(sp):
            sp.dma_start(w[:, :, :], a["W1"].rearrange("(k p) e -> p k e", p=P)).then_inc(const_in, 16)
            sp.dma_start(w_lin[:, :, :], a["w_lin_t"].rearrange("(k p) c -> p k c", p=P)).then_inc(const_in, 16)
            sp.dma_start(b_lin[:, :], a["b_lin"]).then_inc(const_in, 16)
            sp.dma_start(ident[:, :], a["ident"]).then_inc(const_in, 16)
            sp.dma_start(before[:, :], a["before"]).then_inc(const_in, 16)
            sp.dma_start(after[:, :], a["after"]).then_inc(const_in, 16)
            for t in range(NT):
                for dst, src in ((fw, "fw_att"), (bw, "bw_att"), (b_all, "b1")):
                    sp.dma_start(dst[:, t, :], a[src].to_broadcast([P, D])).then_inc(const_in, 16)

            def load(n, j):
                for dst, src in ((x1_in, x1_dram), (adj_in, a["adj"]), (adjt_in, a["adjt"])):
                    sp.dma_start(dst[j][:, :, :], src[ds(n, 1)].rearrange("o (t p) e -> p (o t) e", p=P))\
                      .then_inc(graph_in[j], 16)

            def store(n, j):
                sp.wait_ge(xn3t_ready, n + 1)
                for dst, src in ((x3t_dram, x3t_out), (xn3t_dram, xn3t_out)):
                    sp.dma_start(dst[:, :, ds(n * N, N)].rearrange("k p t -> p k t"), src[j][:, :, :])\
                      .then_inc(x3t_stored[j], 16)
                sp.dma_start(xn3_dram[ds(n * N, N), :].rearrange("(t p) e -> p t e", p=P), xn3_out[j][:, :, :])\
                  .then_inc(x3t_stored[j], 16)

            for j in range(2):
                load(j, j)
            with sp.Fori(0, B // 2 - 1) as i:
                for j in range(2):
                    store(2 * i + j, j)
                    load(2 * i + j + 2, j)
            for j in range(2):
                store(B - 2 + j, j)
            for j in range(2):
                sp.wait_ge(x3t_stored[j], 48 * (B // 2))

        @block.gpsimd
        def _(pool):
            pool.memset(half[:, :], -0.5).then_inc(consts_set, 1)
            pool.memset(eps[:, :], LN_EPS).then_inc(consts_set, 1)
            pool.memset(one[:, :], 1.0).then_inc(consts_set, 1)
            pool.wait_ge(consts_set, 3)

            def body(i, j, n):
                pool_steps.begin(n)
                pool.wait_ge(deg_ready, n + 1)
                pool.tensor_tensor(power[:, :], deg_safe[:, :], half[:, :], ALU.pow)
                t = pool_steps.done(pool.tensor_tensor(keep[:, :], one[:, :], is_zero[:, :], ALU.subtract))
                pool.wait_ge(pool_steps.sem, t)
                pool.tensor_tensor(dinv[:, :], power[:, :], keep[:, :], ALU.mult).then_inc(dinv_ready, 1)
                pool.wait_ge(mv_ready, n + 1)
                t = pool_steps.done(pool.tensor_tensor(vare[:, :], mv[:, :, 1], eps[:, :], ALU.add))
                pool.wait_ge(pool_steps.sem, t)
                pool.tensor_tensor(rstd[:, :], vare[:, :], half[:, :], ALU.pow).then_inc(rstd_ready, 1)
                pool.wait_ge(mv3_ready, n + 1)
                t = pool_steps.done(pool.tensor_tensor(vare[:, :], mv3[:, :, 1], eps[:, :], ALU.add))
                pool.wait_ge(pool_steps.sem, t)
                pool.tensor_tensor(rstd3[:, :], vare[:, :], half[:, :], ALU.pow).then_inc(rstd3_ready, 1)
                pool_steps.end()

            graph_rounds(pool, body)

        @block.scalar
        def _(act):
            def body(i, j, n):
                wait_past(act, x3_ready, n)
                act.activation(h_t[:, :, :], hx[:, :, 1:1 + N, ds(n, 1)].rearrange("p k t o -> p k (t o)"), ACT.Copy)\
                   .then_inc(h_t_ready, 1)
                act.wait_ge(logit_done, n + 1)
                act.activation(logit[:, :, :], ps_logit[:, :, :], ACT.Copy).then_inc(logit_ready, 1)
                act.wait_ge(h_done, n + 1)
                act.activation(h[:, :, :], ps_h[:, :, :], ACT.Copy).then_inc(h_ready, 1)
                act.wait_ge(graph_in[j], 48 * (i + 1))
                for t in range(NT):
                    last = act.activation(junk[:, t, :], adj_in[j][:, t, :], ACT.Copy, accum_out=row_sum[:, t:t + 1])
                last.then_inc(row_sum_ready, 1)
                act.wait_ge(xt_done, n + 1)
                act.activation(xn_t[:, :, :], ps_t[:, :, :], ACT.Copy).then_inc(xn_t_ready, 1)
                act.wait_ge(dinv_ready, n + 1)
                act.wait_ge(proj_done, n + 1)
                for t in range(NT):
                    last = act.activation(hs[:, t, :], ps_w[:, t, :], ACT.Copy, scale=dinv[:, t:t + 1])
                last.then_inc(hs_ready, 1)
                act.wait_ge(x3t_done, n + 1)
                wait_past(act, x3t_stored[j], 48 * i)
                act.activation(x3t_out[j][:, :, :], ps_x3t[:, :, :], ACT.Copy)
                act.wait_ge(xn3t_done, n + 1)
                act.activation(xn3t_out[j][:, :, :], ps_t[:, :, :], ACT.Copy).then_inc(xn3t_ready, 1)

            graph_rounds(act, body)

        @block.tensor
        def _(pe):
            pe.wait_ge(const_in, 16 * (len(CONSTS) + 3))
            pe.wait_ge(ones_set, 2)

            def turn(dst, src):
                for k in range(2):
                    for t in range(2):
                        last = pe.transpose(dst[:, k, t * P:(t + 1) * P], src[:, t, k * P:(k + 1) * P], ident[:, :])
                return last

            def body(i, j, n):
                pe.wait_ge(h_t_ready, n + 1)
                for t in range(NT):
                    for k in range(KD):
                        pe.matmul(ps_logit[:, t, :], h_t[:, k, t * P:(t + 1) * P], w_lin[:, k, :],
                                  start=(k == 0), stop=False)
                    last = pe.matmul(ps_logit[:, t, :], ones_row[:, :], b_lin[:, :], start=False, stop=True)
                last.then_inc(logit_done, 1)
                turn(ps_h, h_t).then_inc(h_done, 1)
                pe.wait_ge(wh_ready, n + 1)
                pe.matmul(ps_pre[:, 0, :], before[:, :], wh[:, 0, :], start=True, stop=True)
                pe.matmul(ps_pre[:, 1, :], ones_sq[:, :], wh[:, 0, :], start=True, stop=False)
                pe.matmul(ps_pre[:, 1, :], before[:, :], wh[:, 1, :], start=False, stop=True)
                pe.matmul(ps_suf[:, 0, :], after[:, :], wh[:, 0, :], start=True, stop=False)
                pe.matmul(ps_suf[:, 0, :], ones_sq[:, :], wh[:, 1, :], start=False, stop=True)
                pe.matmul(ps_suf[:, 1, :], after[:, :], wh[:, 1, :], start=True, stop=True).then_inc(sums_done, 1)
                pe.wait_ge(xn_ready, n + 1)
                turn(ps_t, xn).then_inc(xt_done, 1)
                pe.wait_ge(xn_t_ready, n + 1)
                for t in range(NT):
                    for k in range(KD):
                        last = pe.matmul(ps_w[:, t, :], xn_t[:, k, t * P:(t + 1) * P], w[:, k, :],
                                         start=(k == 0), stop=(k == KD - 1))
                last.then_inc(proj_done, 1)
                pe.wait_ge(graph_in[j], 48 * (i + 1))
                pe.wait_ge(hs_ready, n + 1)
                for t in range(NT):
                    for m in range(NT):
                        last = pe.matmul(ps_agg[:, t, :], adjt_in[j][:, m, t * P:(t + 1) * P], hs[:, m, :],
                                         start=(m == 0), stop=(m == NT - 1))
                last.then_inc(agg_done, 1)
                pe.wait_ge(x3_ready, n + 1)
                turn(ps_x3t, x3).then_inc(x3t_done, 1)
                pe.wait_ge(xn3_ready, n + 1)
                turn(ps_t, xn3_out[j]).then_inc(xn3t_done, 1)

            graph_rounds(pe, body)

        @block.vector
        def _(dve):
            dve.memset(ones_row[:, :], 1.0).then_inc(ones_set, 1)
            dve.memset(ones_sq[:, :], 1.0).then_inc(ones_set, 1)
            dve.wait_ge(const_in, 16 * (len(CONSTS) + 3))

            def normalise(dst, src, mv_, mv_sem, rstd_, rstd_sem, xn_sem, n):
                for t in range(NT):
                    last = dve.bn_stats(stats[:, t, :], src[:, t, :])
                v = dve_steps.done(last)
                dve.wait_ge(dve_steps.sem, v)
                dve.memset(pause[:, :], 0.0)
                for t in range(NT):
                    last = dve.bn_aggr(mv_[:, t, :], stats[:, t, :])
                last.then_inc(mv_sem, 1)
                if src is x2:
                    dve.tensor_tensor(x2b[:, :, :], x2[:, :, :], b_all[:, :, :], ALU.add)
                dve.wait_ge(rstd_sem, n + 1)
                for t in range(NT):
                    last = dve.tensor_scalar(dst[:, t, :], src[:, t, :], mv_[:, t, 0:1], rstd_[:, t:t + 1],
                                             ALU.subtract, ALU.mult)
                last.then_inc(xn_sem, 1)

            def body(i, j, n):
                dve_steps.begin(n)
                dve.wait_ge(logit_ready, n + 1)
                dve.tensor_tensor(picked[:, :], logit[:, :, 1], logit[:, :, 0], ALU.is_gt).then_inc(picked_ready, 1)
                dve.wait_ge(picked_ready, n + 1)
                dve.wait_ge(h_ready, n + 1)
                for t in range(NT):
                    last = dve.tensor_scalar(wh[:, t, :], h[:, t, :], picked[:, t:t + 1], None, ALU.mult)
                last.then_inc(wh_ready, 1)
                dve.wait_ge(row_sum_ready, n + 1)
                v = dve_steps.done(dve.tensor_scalar(is_zero[:, :], row_sum[:, :], 1.0, 0.0, ALU.add, ALU.is_equal))
                dve.wait_ge(dve_steps.sem, v)
                dve.scalar_tensor_tensor(deg_safe[:, :], row_sum[:, :], 1.0, is_zero[:, :], ALU.add, ALU.add)\
                   .then_inc(deg_ready, 1)
                dve.wait_ge(sums_done, n + 1)
                dve.tensor_tensor(y[:, :, :], ps_pre[:, :, :], fw[:, :, :], ALU.mult)
                v = dve_steps.done(dve.tensor_tensor(z[:, :, :], ps_suf[:, :, :], bw[:, :, :], ALU.mult))
                dve.wait_ge(dve_steps.sem, v)
                v = dve_steps.done(dve.scalar_tensor_tensor(y[:, :, :], h[:, :, :], 2.0, y[:, :, :],
                                                            ALU.mult, ALU.add))
                dve.wait_ge(dve_steps.sem, v)
                v = dve_steps.done(dve.tensor_tensor(y[:, :, :], y[:, :, :], z[:, :, :], ALU.add))
                dve.wait_ge(dve_steps.sem, v)
                dve.wait_ge(graph_in[j], 48 * (i + 1))
                v = dve_steps.done(dve.tensor_tensor(x2[:, :, :], x1_in[j][:, :, :], y[:, :, :], ALU.add))
                dve.wait_ge(dve_steps.sem, v)
                normalise(xn, x2, mv, mv_ready, rstd, rstd_ready, xn_ready, n)
                dve.wait_ge(agg_done, n + 1)
                v = dve_steps.done(dve.tensor_tensor(z[:, :, :], ps_agg[:, :, :], hs[:, :, :], ALU.add))
                dve.wait_ge(dve_steps.sem, v)
                for t in range(NT):
                    last = dve.scalar_tensor_tensor(x3[:, t, :], z[:, t, :], dinv[:, t:t + 1], x2b[:, t, :],
                                                    ALU.mult, ALU.add)
                last.then_inc(x3_ready, 1)
                dve.wait_ge(x3_ready, n + 1)
                wait_past(dve, x3t_stored[j], 48 * i)
                normalise(xn3_out[j], x3, mv3, mv3_ready, rstd3, rstd3_ready, xn3_ready, n)
                dve_steps.end()

            graph_rounds(dve, body)
    clear_semaphores(nc, sems)


LEVELS = 4
CAND = 8
TILES = TOK // P
SLOTS = TILES + 4
LOWEST = -3.0e38


def stage_tropical(nc, a, xn3_dram, left_dram, t_dram, wmax_dram):
    with ExitStack() as ctx:
        def sb(name, shape, dt=F32):
            return ctx.enter_context(nc.sbuf_tensor(name, shape, dt))

        I32 = mybir.dt.int32
        v = dict(
            ident=sb("t_ident", [P, P]), ident_b=sb("t_identb", [P, P], BF16),
            w_part=[sb(f"t_wpart{s}", [P, KD, FFN], BF16) for s in range(3)],
            p_minus=sb("t_pminus", [P, 1]), p_plus=sb("t_pplus", [P, 1]),
            wmax=sb("t_wmax", [P, KD, P]),
            acc=[sb(f"t_acc{r}", [P, FFN]) for r in range(2)],
            t_out=[sb(f"t_tout{j}", [P, FFN]) for j in range(2)],
            certified=sb("t_certified", [P, SLOTS]),
            order=sb("t_order", [P, SLOTS]),
            index=[ctx.enter_context(nc.psum_tensor(f"t_index{b}", [P, 4 * P], F32)) for b in range(2)],
            fetched=[ctx.enter_context(nc.psum_tensor(f"t_fetched{r}", [P, FFN], F32)) for r in range(2)],
            ps_count=ctx.enter_context(nc.psum_tensor("t_pscount", [1, P], F32)),
            from_all=sb("t_fromall", [P, SLOTS], I32), to_all=sb("t_toall", [P, SLOTS], I32),
            most_int=sb("t_mostint", [1, 1], I32),
        )
        tropical_consts(nc, a, v, xn3_dram, left_dram, t_dram, wmax_dram)
        for level in range(LEVELS):
            plan_slots(nc, v, level)
            tropical_level(nc, v, level, xn3_dram, left_dram, t_dram)
        plan_slots(nc, v, LEVELS)
        tropical_general(nc, v, xn3_dram, t_dram)


def tropical_consts(nc, a, v, xn3_dram, left_dram, t_dram, wmax_dram):
    with ExitStack() as ctx:
        def sb(name, shape, dt=F32):
            return ctx.enter_context(nc.sbuf_tensor(name, shape, dt))

        def sem(name):
            return ctx.enter_context(nc.semaphore("tc_" + name))

        w_t = sb("tc_w", [P, KD, FFN])
        w_rest, w_rest2 = sb("tc_wrest", [P, KD, FFN]), sb("tc_wrest2", [P, KD, FFN])
        wmax_col = sb("tc_wmaxcol", [P, KD])
        zeros = sb("tc_zeros", [P, FFN])
        w_part, wmax = v["w_part"], v["wmax"]
        const_in, w_split, w_hi, w_mid, w_rest_ready = (
            sem(n) for n in ("const_in", "w_split", "w_hi", "w_mid", "w_rest_ready"))
        wmax_col_ready, wmax_kept, wmax_in, zeros_ready, spare_kept = (
            sem(n) for n in ("wmax_col_ready", "wmax_kept", "wmax_in", "zeros_ready", "spare_kept"))
        block = ctx.enter_context(nc.Block())

        @block.sync
        def _(sp):
            sp.dma_start(w_t[:, :, :], a["Wt_t"].rearrange("(k p) f -> p k f", p=P)).then_inc(const_in, 16)
            sp.dma_start(v["ident"][:, :], a["ident"]).then_inc(const_in, 16)
            sp.dma_start(v["p_minus"][:, :], a["p_minus"]).then_inc(const_in, 16)
            sp.dma_start(v["p_plus"][:, :], a["p_plus"]).then_inc(const_in, 16)
            sp.dma_start(v["order"][:, :], a["tile_no"].to_broadcast([P, SLOTS])).then_inc(const_in, 16)
            sp.wait_ge(zeros_ready, 1)
            sp.dma_start(t_dram[TOK:TOK + P, :], zeros[:, :]).then_inc(spare_kept, 16)
            sp.dma_start(left_dram[TOK:TOK + P, :], zeros[:, 0:D]).then_inc(spare_kept, 16)
            sp.dma_start(xn3_dram[TOK:TOK + P, :], zeros[:, 0:D]).then_inc(spare_kept, 16)
            sp.wait_ge(wmax_col_ready, 1)
            for k in range(KD):
                sp.dma_start(wmax_dram[:, k * P:(k + 1) * P].rearrange("o p -> p o"), wmax_col[:, k:k + 1])\
                  .then_inc(wmax_kept, 16)
            sp.wait_ge(wmax_kept, 16 * KD)
            sp.dma_start(wmax[:, :, :], wmax_dram.to_broadcast([P, D]).rearrange("p (k d) -> p k d", k=KD))\
              .then_inc(wmax_in, 16)
            sp.wait_ge(wmax_in, 16)
            sp.wait_ge(spare_kept, 48)

        @block.gpsimd
        def _(pool):
            pool.wait_ge(w_hi, 1)
            pool.tensor_tensor(w_rest[:, :, :], w_t[:, :, :], w_part[0][:, :, :], ALU.subtract)\
                .then_inc(w_rest_ready, 1)
            pool.wait_ge(w_mid, 1)
            pool.tensor_tensor(w_rest2[:, :, :], w_rest[:, :, :], w_part[1][:, :, :], ALU.subtract)\
                .then_inc(w_rest_ready, 1)

        @block.scalar
        def _(act):
            act.wait_ge(const_in, 80)
            act.activation(v["ident_b"][:, :], v["ident"][:, :], ACT.Copy)
            act.activation(w_part[0][:, :, :], w_t[:, :, :], ACT.Copy).then_inc(w_hi, 1)
            act.wait_ge(w_rest_ready, 1)
            act.activation(w_part[1][:, :, :], w_rest[:, :, :], ACT.Copy).then_inc(w_mid, 1)
            act.wait_ge(w_rest_ready, 2)
            act.activation(w_part[2][:, :, :], w_rest2[:, :, :], ACT.Copy).then_inc(w_split, 1)

        @block.vector
        def _(dve):
            dve.memset(zeros[:, :], 0.0).then_inc(zeros_ready, 1)
            dve.memset(v["certified"][:, :], 0.0)
            dve.wait_ge(const_in, 80)
            dve.tensor_reduce(wmax_col[:, :], w_t[:, :, :], AX.X, ALU.max).then_inc(wmax_col_ready, 1)


def plan_slots(nc, v, level):
    with ExitStack() as ctx:
        def sb(name, shape, dt=F32):
            return ctx.enter_context(nc.sbuf_tensor(f"tp{level}_{name}", shape, dt))

        def sem(name):
            return ctx.enter_context(nc.semaphore(f"tp{level}_{name}"))

        open_, is_open, key, left_key = (sb(n, [P, SLOTS]) for n in ("open", "isopen", "key", "leftkey"))
        row, no_token, no_token2 = (sb(n, [P, SLOTS]) for n in ("row", "notoken", "notoken2"))
        count, most = sb("count", [P, 1]), sb("most", [1, 1])
        certified, order, from_all, to_all, most_int = (
            v[n] for n in ("certified", "order", "from_all", "to_all", "most_int"))
        counted, count_turned = sem("counted"), sem("count_turned")
        steps = Steps(sem("steps"), 7 + 2 * (TILES // 8))
        block = ctx.enter_context(nc.Block())

        @block.tensor
        def _(pe):
            pe.wait_ge(counted, 1)
            pe.transpose(v["ps_count"][:, :], count[:, :], v["ident"][:, :]).then_inc(count_turned, 1)

        @block.vector
        def _(dve):
            def then(instruction):
                dve.wait_ge(steps.sem, steps.done(instruction))

            steps.begin(0)
            then(dve.tensor_scalar(open_[:, :], certified[:, :], -1.0, 1.0, ALU.mult, ALU.add))
            then(dve.tensor_tensor(key[:, :], open_[:, :], order[:, :], ALU.mult))
            then(dve.tensor_scalar(is_open[:, :], key[:, :], 0.0, None, ALU.is_gt))
            dve.tensor_reduce(count[:, :], is_open[:, :], AX.X, ALU.add).then_inc(counted, 1)
            src = key
            for r in range(TILES // 8):
                eight = slice(8 * r, 8 * r + 8)
                then(dve.max(order[:, eight], src[:, 0:TILES]))
                then(dve.match_replace(left_key[:, 0:TILES], order[:, eight], src[:, 0:TILES], -1.0))
                src = left_key
            dve.tensor_scalar(row[:, :], order[:, :], -1.0, float(P), ALU.add, ALU.mult)
            then(dve.tensor_scalar(no_token[:, :], order[:, :], 0.0, float(TOK + P), ALU.is_equal, ALU.mult))
            then(dve.tensor_scalar(row[:, :], row[:, :], v["p_plus"][:, :], None, ALU.add))
            dve.tensor_tensor(from_all[:, :], row[:, :], no_token[:, :], ALU.add)
            then(dve.tensor_scalar(no_token2[:, :], order[:, :], 0.0, float(TOK + 2 * P), ALU.is_equal, ALU.mult))
            dve.tensor_tensor(to_all[:, :], row[:, :], no_token2[:, :], ALU.add)
            dve.wait_ge(count_turned, 1)
            then(dve.tensor_reduce(most[:, :], v["ps_count"][:, :], AX.X, ALU.max))
            dve.tensor_scalar(most_int[:, :], most[:, :], 1.0, None, ALU.max)
            steps.end()


def tropical_level(nc, v, level, xn3_dram, left_dram, t_dram):
    resume = level > 0
    go_on = level < LEVELS - 1
    src_dram = left_dram if resume else xn3_dram
    IN = 32 if resume else 16
    OUT = 32 if go_on else 16
    GRP = 4
    CANDS = KD * CAND
    G = CANDS // GRP
    CH = 512
    assert G % 2 == 0 and CAND == 8
    with ExitStack() as ctx:
        def sb(name, shape, dt=F32):
            return ctx.enter_context(nc.sbuf_tensor(f"t{level}_{name}", shape, dt))

        def sem(name):
            return ctx.enter_context(nc.semaphore(f"t{level}_{name}"))

        x = [sb(f"x{j}", [P, KD, P]) for j in range(2)]
        left = [sb(f"left{j}", [P, KD, P]) for j in range(2)]
        t_in = [sb(f"tin{j}", [P, FFN]) for j in range(2)]
        top = [sb(f"top{j}", [P, KD, CAND]) for j in range(2)]
        place = sb("place", [P, KD, CAND], mybir.dt.uint32)
        cand = [sb(f"cand{j}", [P, KD * CAND], BF16) for j in range(2)]
        bounds, bound = sb("bounds", [P, KD * P]), [sb(f"bound{j}", [P, 1]) for j in range(2)]
        dist = [sb(f"dist{b}", [P, GRP * P]) for b in range(2)]
        one_hot = [sb(f"onehot{b}", [P, GRP * P], BF16) for b in range(2)]
        least, pause = sb("least", [P, 1]), sb("pause", [1, 3])
        pool_pause, pool_zero = sb("poolpause", [1, 4]), sb("poolzero", [1, 1])
        from_now = [sb(f"fromnow{j}", [P, 1], mybir.dt.int32) for j in range(2)]
        to_now = [sb(f"tonow{j}", [P, 1], mybir.dt.int32) for j in range(2)]
        certified, ident_b, w_part, wmax, acc, t_out, index, fetched, most_int = (
            v[n] for n in ("certified", "ident_b", "w_part", "wmax", "acc", "t_out", "index", "fetched", "most_int"))
        rows_in = [sem(f"rows_in{j}") for j in range(2)]
        rows_out = [sem(f"rows_out{j}") for j in range(2)]
        written = [sem(f"written{j}") for j in range(2)]
        selected, index_ready, dist_ready, one_hot_ready = (
            sem(n) for n in ("selected", "index_ready", "dist_ready", "one_hot_ready"))
        fetched_ready, fetched_used, merged, least_ready = (
            sem(n) for n in ("fetched_ready", "fetched_used", "merged", "least_ready"))
        numbers_ready, zero_ready = sem("numbers_ready"), sem("zero_ready")
        select_steps = Steps(sem("select_steps"), 2)
        block = ctx.enter_context(nc.Block())

        def slot_pairs(eng, body):
            slots = eng.value_load(most_int[0:1, 0:1], min_val=1, max_val=TILES)
            with eng.Fori(0, slots, 2) as i:
                body(i)

        @block.gpsimd
        def _(pool):
            def gather(j):
                at = bass.IndirectOffsetOnAxis(from_now[j][:, 0:1], 0)
                pool.indirect_dma_start(x[j][:, :, :].rearrange("p k d -> p (k d)"), None, src_dram[0:TOK + P, :], at)\
                    .then_inc(rows_in[j], 16)
                if resume:
                    pool.indirect_dma_start(t_in[j][:, :], None, t_dram[0:TOK + P, :], at).then_inc(rows_in[j], 16)

            def held(k, sem_, value):
                pool.wait_ge(sem_, value)
                return pool.tensor_tensor(pool_pause[:, k:k + 1], pool_zero[:, :], pool_zero[:, :], ALU.add)

            pool.memset(pool_zero[:, :], 0.0).then_inc(zero_ready, 1)
            for j in range(2):
                pool.tensor_copy(from_now[j][:, :], v["from_all"][:, j:j + 1]).then_inc(numbers_ready, 1)
            pool.wait_ge(zero_ready, 1)
            pool.wait_ge(numbers_ready, 2)
            for j in range(2):
                gather(j)

            def body(i):
                for j in range(2):
                    held(0, merged, i + j + 1)
                    pool.tensor_copy(to_now[j][:, :], v["to_all"][:, ds(i + j, 1)])
                    pool.tensor_copy(from_now[j][:, :], v["from_all"][:, ds(i + j + 2, 1)]).then_inc(numbers_ready, 1)
                    held(1, numbers_ready, i + j + 3)
                    at = bass.IndirectOffsetOnAxis(to_now[j][:, 0:1], 0)
                    pool.indirect_dma_start(t_dram, at, t_out[j][:, :], None).then_inc(rows_out[j], 16)
                    if go_on:
                        pool.indirect_dma_start(left_dram, at, left[j][:, :, :].rearrange("p k d -> p (k d)"), None)\
                            .then_inc(rows_out[j], 16)
                    gather(j)
                    held(2, rows_out[j], (i + 2) * (OUT // 2))
                    held(3, rows_in[j], (i + 4) * (IN // 2)).then_inc(written[j], 2)
                    pool.wait_ge(written[j], i + 4)

            slot_pairs(pool, body)

        @block.scalar
        def _(act):
            def turn_hot(g, b):
                act.wait_ge(index_ready, g + 1)
                act.activation(dist[b][:, :], index[b][:, :], ACT.Abs, bias=v["p_minus"][:, :]).then_inc(dist_ready, 1)
                act.wait_ge(dist_ready, g + 1)
                act.activation(one_hot[b][:, :], dist[b][:, :], ACT.Relu, scale=-1.0, bias=1.0)\
                   .then_inc(one_hot_ready, 1)

            def body(i):
                for g in range(2 * G):
                    turn_hot(i * G + g, g % 2)

            slot_pairs(act, body)

        @block.tensor
        def _(pe):
            def spread(s, j, g):
                pe.wait_ge(selected, s + 1)
                for c in range(GRP):
                    one = cand[j][:, g * GRP + c:g * GRP + c + 1].to_broadcast([P, P])
                    mm = pe.matmul(index[g % 2][:, c * P:(c + 1) * P], one, ident_b[:, :], start=True, stop=True)
                mm.then_inc(index_ready, 1)

            def fetch(s, g):
                k = g * GRP // CAND
                pe.wait_ge(one_hot_ready, s * G + g + 1)
                for c in range(GRP):
                    pe.wait_ge(fetched_used, s * CANDS + g * GRP + c + 1)
                    for h in range(FFN // CH):
                        for part in range(3):
                            mm = pe.matmul(fetched[c % 2][:, h * CH:(h + 1) * CH],
                                           one_hot[g % 2][:, c * P:(c + 1) * P],
                                           w_part[part][:, k, h * CH:(h + 1) * CH],
                                           start=(part == 0), stop=(part == 2))
                    mm.then_inc(fetched_ready, 1)

            def body(i):
                for j in range(2):
                    for g in range(G):
                        if g < G - 1:
                            spread(i + j, j, g + 1)
                        else:
                            spread(i + j + 1, 1 - j, 0)
                        fetch(i + j, g)

            spread(0, 0, 0)
            slot_pairs(pe, body)

        @block.vector
        def _(dve):
            dve.sem_inc(fetched_used, 2)
            for j in range(2):
                dve.sem_inc(written[j], 2)
            dve.memset(certified[:, :], 0.0)

            def select(s, j, rows, free, stage):
                def held(n, sem_, value):
                    dve.wait_ge(sem_, value)
                    dve.memset(pause[:, n:n + 1], 0.0)

                if stage == 0:
                    select_steps.begin(s)
                    held(0, rows_in[j], rows)
                    for k in range(KD):
                        last = dve.max(top[j][:, k, :], x[j][:, k, :])
                    return select_steps.done(last)
                elif stage == 1:
                    select_steps.begin(s)
                    held(1, select_steps.sem, select_steps.base + 1)
                    held(2, written[j], free)
                    for k in range(KD):
                        dve.max_index(place[:, k, :], top[j][:, k, :], x[j][:, k, :])
                        last = dve.match_replace(left[j][:, k, :], top[j][:, k, :], x[j][:, k, :], LOWEST)
                    last.then_inc(select_steps.sem, 1)
                else:
                    select_steps.begin(s)
                    dve.wait_ge(select_steps.sem, select_steps.base + 2)
                    dve.tensor_copy(cand[j][:, :], place[:, :, :].rearrange("p k c -> p (k c)"))
                    dve.tensor_tensor_reduce(bounds[:, :], left[j][:, :, :].rearrange("p k d -> p (k d)"),
                                             wmax[:, :, :].rearrange("p k d -> p (k d)"), 1.0, LOWEST,
                                             ALU.add, ALU.max, bound[j][:, :]).then_inc(selected, 1)

            def use(s, j, c):
                q, r = s * CANDS + c, c % 2
                value = top[j][:, c // CAND, c % CAND:c % CAND + 1]
                dve.wait_ge(fetched_ready, q + 1)
                if c >= 2 or (c == 0 and resume):
                    dve.wait_ge(fetched_used, q + 1)
                    op = dve.scalar_tensor_tensor(acc[r][:, :], fetched[r][:, :], value,
                                                  (t_in[j] if c == 0 else acc[r])[:, :], ALU.add, ALU.max)
                else:
                    op = dve.tensor_scalar(acc[r][:, :], fetched[r][:, :], value, None, ALU.add)
                op.then_inc(fetched_used, 1)

            def body(i):
                for j in range(2):
                    s = i + j
                    for c in range(CANDS):
                        use(s, j, c)
                        if c in (8, 9, 10):
                            select(s + 1, 1 - j, (i + 2 * j + 2) * (IN // 2), i + 2 * j + 2, c - 8)
                    dve.wait_ge(fetched_used, (s + 1) * CANDS + 2)
                    dve.wait_ge(written[j], i + 2)
                    dve.tensor_tensor(t_out[j][:, :], acc[0][:, :], acc[1][:, :], ALU.max).then_inc(merged, 1)
                    dve.wait_ge(merged, s + 1)
                    dve.tensor_reduce(least[:, :], t_out[j][:, :], AX.X, ALU.min).then_inc(least_ready, 1)
                    dve.wait_ge(least_ready, s + 1)
                    dve.tensor_tensor(certified[:, ds(s, 1)], bound[j][:, :], least[:, :], ALU.is_lt)

            for stage in range(3):
                select(0, 0, IN, 2, stage)
            slot_pairs(dve, body)


def tropical_general(nc, v, xn3_dram, t_dram):
    CH = 512
    with ExitStack() as ctx:
        def sb(name, shape, dt=F32):
            return ctx.enter_context(nc.sbuf_tensor(name, shape, dt))

        def sem(name):
            return ctx.enter_context(nc.semaphore("tg_" + name))

        x_slot = sb("tg_x", [P, D])
        from_now, to_now = (sb(f"tg_{n}now", [P, 1], mybir.dt.int32) for n in ("from", "to"))
        pool_pause, pool_zero = sb("tg_poolpause", [1, 3]), sb("tg_poolzero", [1, 1])
        ident_b, w_part, acc, t_out, fetched, most_int = (
            v[n] for n in ("ident_b", "w_part", "acc", "t_out", "fetched", "most_int"))
        zero_ready, slot_ready, rows_in, dense_ready, dense_used, merged, rows_out, slot_free = (
            sem(n) for n in ("zero_ready", "slot_ready", "rows_in", "dense_ready", "dense_used", "merged",
                             "rows_out", "slot_free"))
        block = ctx.enter_context(nc.Block())

        @block.gpsimd
        def _(pool):
            def held(k, sem_, value):
                pool.wait_ge(sem_, value)
                return pool.tensor_tensor(pool_pause[:, k:k + 1], pool_zero[:, :], pool_zero[:, :], ALU.add)

            pool.memset(pool_zero[:, :], 0.0).then_inc(zero_ready, 1)
            pool.wait_ge(zero_ready, 1)
            slots = pool.value_load(most_int[0:1, 0:1], min_val=1, max_val=TILES)
            with pool.Fori(0, slots) as s:
                held(0, slot_ready, s + 1)
                pool.indirect_dma_start(x_slot[:, :], None, xn3_dram,
                                        bass.IndirectOffsetOnAxis(from_now[:, 0:1], 0)).then_inc(rows_in, 16)
                held(1, merged, s + 1)
                pool.indirect_dma_start(t_dram, bass.IndirectOffsetOnAxis(to_now[:, 0:1], 0),
                                        t_out[0][:, :], None).then_inc(rows_out, 16)
                held(2, rows_out, 16 * s + 16).then_inc(slot_free, 1)

        @block.tensor
        def _(pe):
            slots = pe.value_load(most_int[0:1, 0:1], min_val=1, max_val=TILES)
            with pe.Fori(0, slots) as s:
                for k in range(KD):
                    with pe.Fori(0, P // 2) as pair:
                        for r in range(2):
                            pe.wait_ge(dense_used, s * D + k * P + 2 * pair + r + 1)
                            one_row = ident_b[:, ds(2 * pair + r, 1)].to_broadcast([P, P])
                            for h in range(FFN // CH):
                                for part in range(3):
                                    mm = pe.matmul(fetched[r][:, h * CH:(h + 1) * CH], one_row,
                                                   w_part[part][:, k, h * CH:(h + 1) * CH],
                                                   start=(part == 0), stop=(part == 2))
                            mm.then_inc(dense_ready, 1)

        @block.vector
        def _(dve):
            dve.sem_inc(dense_used, 2)
            dve.sem_inc(slot_free, 1)
            slots = dve.value_load(most_int[0:1, 0:1], min_val=1, max_val=TILES)

            def use(s, k, d, r, first):
                q = s * D + k * P + d
                dve.wait_ge(dense_ready, q + 1)
                if first:
                    op = dve.tensor_scalar(acc[r][:, :], fetched[r][:, :], x_slot[:, d:d + 1], None, ALU.add)
                else:
                    dve.wait_ge(dense_used, q + 1)
                    op = dve.scalar_tensor_tensor(acc[r][:, :], fetched[r][:, :], x_slot[:, ds(k * P + d, 1)],
                                                  acc[r][:, :], ALU.add, ALU.max)
                op.then_inc(dense_used, 1)

            with dve.Fori(0, slots) as s:
                dve.wait_ge(slot_free, s + 1)
                dve.tensor_copy(from_now[:, :], v["from_all"][:, ds(s, 1)])
                dve.tensor_copy(to_now[:, :], v["to_all"][:, ds(s, 1)]).then_inc(slot_ready, 1)
                dve.wait_ge(rows_in, 16 * s + 16)
                for r in range(2):
                    use(s, 0, r, r, True)
                with dve.Fori(1, P // 2) as pair:
                    for r in range(2):
                        use(s, 0, 2 * pair + r, r, False)
                with dve.Fori(0, P // 2) as pair:
                    for r in range(2):
                        use(s, 1, 2 * pair + r, r, False)
                dve.wait_ge(dense_used, s * D + D + 2)
                dve.tensor_tensor(t_out[0][:, :], acc[0][:, :], acc[1][:, :], ALU.max).then_inc(merged, 1)


def stage_ffn(nc, a, x3t_dram, xn3t_dram, t_dram, out):
    CB = 512
    BLOCKS = TOK // CB
    with ExitStack() as ctx:
        def sb(name, shape, dt=F32):
            return ctx.enter_context(nc.sbuf_tensor(name, shape, dt))

        def ps(name):
            return ctx.enter_context(nc.psum_tensor(name, [P, CB], F32))

        def sem(name):
            return ctx.enter_context(nc.semaphore(name))

        def sems(*names):
            return [sem("f_" + n) for n in names]

        w_c = sb("f_wc", [P, KD, FFN])
        w_g = sb("f_wg", [P, KD, FFN])
        w_d = sb("f_wd", [P, FT, D])
        slope = [sb(f"f_slope{s}", [P, FT, PIECES]) for s in range(2)]
        offset = [sb(f"f_offset{s}", [P, FT, PIECES]) for s in range(2)]
        shift = [sb(f"f_shift{s}", [P, FT, PIECES]) for s in range(2)]
        b_t, b_c, b_g = sb("f_bt", [P, FT]), sb("f_bc", [P, FT]), sb("f_bg", [P, FT])
        alpha = sb("f_alpha", [P, FT])
        b_d = sb("f_bd", [P, KD])
        half_bg = sb("f_half_bg", [P, FT])
        tanh_a = sb("f_tanh_a", [P, FT])
        share = [sb(f"f_share{s}", [P, FT]) for s in range(2)]
        x3 = [sb(f"f_x3{j}", [P, KD, CB]) for j in range(2)]
        x = [sb(f"f_x{j}", [P, KD, CB]) for j in range(2)]
        t = [sb(f"f_t{j}", [P, CB // P, FFN]) for j in range(2)]
        ident = sb("f_ident", [P, P])
        lines = [[sb(f"f_lines{v}{s}", [P, PIECES, CB]) for s in range(2)] for v in range(2)]
        cls = [sb(f"f_cls{v}", [P, CB]) for v in range(2)]
        th = [sb(f"f_th{v}", [P, CB]) for v in range(2)]
        convex = sb("f_convex", [P, CB])
        trop = [sb(f"f_trop{v}", [P, CB]) for v in range(2)]
        diff = [sb(f"f_diff{v}", [P, CB]) for v in range(2)]
        gated = [sb(f"f_gated{v}", [P, CB]) for v in range(2)]
        fused = [sb(f"f_fused{v}", [P, CB]) for v in range(2)]
        o_b = sb("f_ob", [P, KD, CB])
        o_x = [sb(f"f_ox{j}", [P, KD, CB]) for j in range(2)]
        ps_c = [ps(f"f_psc{v}") for v in range(2)]
        ps_g = [ps(f"f_psg{v}") for v in range(2)]
        ps_t = [ps(f"f_pst{v}") for v in range(2)]
        ps_o = [ps(f"f_pso{k}") for k in range(KD)]

        const_in, consts_ready = sems("const_in", "consts_ready")
        shift_ready, t_turned = sems("shift_ready", "t_turned")
        block_in = sems("block_in0", "block_in1")
        stored = sems("stored0", "stored1")
        c_done, g_done, cls_ready, th_ready = sems("c_done", "g_done", "cls_ready", "th_ready")
        lines_ready = sems("convex_lines_ready", "concave_lines_ready")
        trop_ready, diff_ready, gated_ready, fused_ready = sems("trop_ready", "diff_ready", "gated_ready", "fused_ready")
        fused_used, ob_ready, ox_ready = sems("fused_used", "ob_ready", "ox_ready")
        dve_steps = Steps(sem("f_dve_steps"), 7)

        block = ctx.enter_context(nc.Block())
        PIECE_CONSTS = ((slope[0], "sl_cvx"), (offset[0], "of_cvx"), (slope[1], "sl_ccv"), (offset[1], "of_ccv"))
        VECTORS = ((b_t, "bt"), (b_c, "bc"), (b_g, "bg"), (alpha, "alpha"), (b_d, "bd"))
        CONSTS = 4 + len(PIECE_CONSTS) + len(VECTORS)

        def rounds(eng, body):
            for j in range(2):
                body(0, j, j, True)
            with eng.Fori(1, BLOCKS // 2) as i:
                for j in range(2):
                    body(i, j, 2 * i + j, False)

        @block.sync
        def _(sp):
            sp.dma_start(w_c[:, :, :], a["Wc"].rearrange("(k p) f -> p k f", p=P)).then_inc(const_in, 16)
            sp.dma_start(w_g[:, :, :], a["Wg"].rearrange("(k p) f -> p k f", p=P)).then_inc(const_in, 16)
            sp.dma_start(w_d[:, :, :], a["Wd"].rearrange("(t p) d -> p t d", p=P)).then_inc(const_in, 16)
            sp.dma_start(ident[:, :], a["ident"]).then_inc(const_in, 16)
            for dst, name in PIECE_CONSTS:
                sp.dma_start(dst[:, :, :], a[name].rearrange("(t p) q -> p t q", p=P)).then_inc(const_in, 16)
            for dst, name in VECTORS:
                sp.dma_start(dst[:, :], a[name]).then_inc(const_in, 16)

            def load(m, j):
                sp.dma_start(x[j][:, :, :], xn3t_dram[:, :, ds(m * CB, CB)].rearrange("k p t -> p k t"))\
                  .then_inc(block_in[j], 16)
                sp.dma_start(x3[j][:, :, :], x3t_dram[:, :, ds(m * CB, CB)].rearrange("k p t -> p k t"))\
                  .then_inc(block_in[j], 16)
                sp.dma_start(t[j][:, :, :], t_dram[ds(m * CB, CB), :].rearrange("(g p) f -> p g f", p=P))\
                  .then_inc(block_in[j], 16)

            def store(m, j):
                sp.wait_ge(ox_ready, m + 1)
                sp.dma_start(out[:, :, ds(m * CB, CB)].rearrange("k p t -> p k t"), o_x[j][:, :, :])\
                  .then_inc(stored[j], 16)

            for j in range(2):
                load(j, j)
            with sp.Fori(0, BLOCKS // 2 - 1) as i:
                for j in range(2):
                    store(2 * i + j, j)
                    load(2 * i + j + 2, j)
            for j in range(2):
                store(BLOCKS - 2 + j, j)
            for j in range(2):
                sp.wait_ge(stored[j], 16 * (BLOCKS // 2) + 16)

        @block.gpsimd
        def _(pool):
            def body(i, j, m, first):
                for u in range(FT):
                    v, q = u % 2, m * FT + u
                    pool.wait_ge(cls_ready, q + 1)
                    pool.wait_ge(trop_ready, q + 1)
                    pool.tensor_tensor(diff[v][:, :], trop[v][:, :], cls[v][:, :], ALU.subtract).then_inc(diff_ready, 1)
                    if u == 3 and not (first and j == 0):
                        total(m - 1, 1 - j, i if j else i - 1)

            def total(m, j, i):
                pool.wait_ge(stored[j], 16 * i + 16)
                pool.wait_ge(ob_ready, m + 1)
                pool.tensor_tensor(o_x[j][:, :, :], o_b[:, :, :], x3[j][:, :, :], ALU.add).then_inc(ox_ready, 1)

            for j in range(2):
                pool.sem_inc(stored[j], 16)
            rounds(pool, body)
            total(BLOCKS - 1, 1, BLOCKS // 2 - 1)

        @block.scalar
        def _(act):
            act.wait_ge(const_in, 16 * CONSTS)
            act.activation(tanh_a[:, :], alpha[:, :], ACT.Tanh, scale=0.5).then_inc(consts_ready, 1)
            act.activation(half_bg[:, :], b_g[:, :], ACT.Copy, scale=0.5).then_inc(consts_ready, 1)
            act.wait_ge(consts_ready, 2)
            act.wait_ge(shift_ready, 4 * FT)

            def body(i, j, m, first):
                act.wait_ge(block_in[j], 48 * (i + 1))
                for u in range(FT):
                    v, q = u % 2, m * FT + u
                    if not (first and j == 0 and u < 2):
                        act.wait_ge(trop_ready, q - 1)
                    act.wait_ge(t_turned, q + 1)
                    for s in range(2):
                        for n in range(PIECES):
                            last = act.activation(lines[v][s][:, n, :], ps_t[v][:, :], ACT.Identity,
                                                  scale=slope[s][:, u, n:n + 1], bias=shift[s][:, u, n:n + 1])
                        last.then_inc(lines_ready[s], 1)
                    act.wait_ge(c_done, q + 1)
                    if not (first and j == 0 and u < 2):
                        act.wait_ge(fused_ready, q - 1)
                    act.activation(cls[v][:, :], ps_c[v][:, :], ACT.Gelu, bias=b_c[:, u:u + 1]).then_inc(cls_ready, 1)
                    act.wait_ge(g_done, q + 1)
                    act.activation(th[v][:, :], ps_g[v][:, :], ACT.Tanh, scale=0.5, bias=half_bg[:, u:u + 1])\
                       .then_inc(th_ready, 1)
                    if u == 1 and not (first and j == 0):
                        finish(m - 1)

            def finish(m):
                act.wait_ge(fused_used, (m + 1) * FT)
                wait_past(act, ox_ready, m)
                for k in range(KD):
                    last = act.activation(o_b[:, k, :], ps_o[k][:, :], ACT.Identity, bias=b_d[:, k:k + 1])
                last.then_inc(ob_ready, 1)

            rounds(act, body)
            finish(BLOCKS - 1)

        @block.tensor
        def _(pe):
            pe.wait_ge(const_in, 16 * CONSTS)

            def output_part(m, u, early):
                v, q = u % 2, m * FT + u
                if u == 0 and not early:
                    pe.wait_ge(ob_ready, m)
                pe.wait_ge(fused_ready, q + 1)
                for k in range(KD):
                    mm = pe.matmul(ps_o[k][:, :], w_d[:, u, k * P:(k + 1) * P], fused[v][:, :],
                                   start=(u == 0), stop=(u == FT - 1))
                mm.then_inc(fused_used, 1)

            def body(i, j, m, first):
                pe.wait_ge(block_in[j], 48 * (i + 1))
                for u in range(FT):
                    v, q = u % 2, m * FT + u
                    if not (first and j == 0 and u < 2):
                        pe.wait_ge(lines_ready[1], q - 1)
                    for g in range(CB // P):
                        mm = pe.transpose(ps_t[v][:, g * P:(g + 1) * P], t[j][:, g, u * P:(u + 1) * P], ident[:, :])
                    mm.then_inc(t_turned, 1)
                    for ps_, w_, done, read in ((ps_c, w_c, c_done, cls_ready), (ps_g, w_g, g_done, th_ready)):
                        if not (first and j == 0 and u < 2):
                            pe.wait_ge(read, q - 1)
                        for k in range(KD):
                            mm = pe.matmul(ps_[v][:, :], w_[:, k, u * P:(u + 1) * P], x[j][:, k, :],
                                           start=(k == 0), stop=(k == KD - 1))
                        mm.then_inc(done, 1)
                    if u > 0:
                        output_part(m, u - 1, first and j == 0)
                    elif not (first and j == 0):
                        output_part(m - 1, FT - 1, False)

            rounds(pe, body)
            output_part(BLOCKS - 1, FT - 1, False)

        @block.vector
        def _(dve):
            dve.wait_ge(const_in, 16 * CONSTS)
            for s in range(2):
                for u in range(FT):
                    dve.tensor_scalar(shift[s][:, u, :], slope[s][:, u, :], b_t[:, u:u + 1], None, ALU.mult)\
                       .then_inc(shift_ready, 1)
            dve.wait_ge(shift_ready, 2 * FT)
            for s in range(2):
                for u in range(FT):
                    dve.tensor_tensor(shift[s][:, u, :], shift[s][:, u, :], offset[s][:, u, :], ALU.add)\
                       .then_inc(shift_ready, 1)
            dve.wait_ge(consts_ready, 2)
            dve.tensor_scalar(share[0][:, :], tanh_a[:, :], 0.5, 0.5, ALU.mult, ALU.add).then_inc(consts_ready, 1)
            dve.tensor_scalar(share[1][:, :], tanh_a[:, :], -0.5, 0.5, ALU.mult, ALU.add).then_inc(consts_ready, 1)
            dve.wait_ge(consts_ready, 4)

            def fuse(m, u, peeled):
                v, q = u % 2, m * FT + u
                dve.wait_ge(diff_ready, q + 1)
                dve.wait_ge(th_ready, q + 1)
                dve.scalar_tensor_tensor(gated[v][:, :], th[v][:, :], 1.0, diff[v][:, :], ALU.add, ALU.mult)\
                   .then_inc(gated_ready, 1)
                dve.wait_ge(gated_ready, q + 1)
                if not peeled:
                    dve.wait_ge(fused_used, q - 1)
                dve.scalar_tensor_tensor(fused[v][:, :], gated[v][:, :], 0.5, cls[v][:, :], ALU.mult, ALU.add)\
                   .then_inc(fused_ready, 1)

            def body(i, j, m, first):
                for u in range(FT):
                    v, q = u % 2, m * FT + u
                    dve_steps.begin(q)
                    for s, op in ((0, ALU.max), (1, ALU.min)):
                        dve.wait_ge(lines_ready[s], q + 1)
                        l = lines[v][s]
                        for n in (4, 2, 1):
                            w = dve_steps.done(dve.tensor_tensor(l[:, 0:n, :], l[:, 0:n, :], l[:, n:2 * n, :], op))
                            dve.wait_ge(dve_steps.sem, w)
                    w = dve_steps.done(dve.tensor_scalar(convex[:, :], lines[v][0][:, 0, :], share[0][:, u:u + 1],
                                                         None, ALU.mult))
                    dve.wait_ge(dve_steps.sem, w)
                    dve.scalar_tensor_tensor(trop[v][:, :], lines[v][1][:, 0, :], share[1][:, u:u + 1], convex[:, :],
                                             ALU.mult, ALU.add).then_inc(trop_ready, 1)
                    dve_steps.end()
                    if u > 0:
                        fuse(m, u - 1, first and j == 0 and u < 3)
                    elif not (first and j == 0):
                        fuse(m - 1, FT - 1, False)

            rounds(dve, body)
            fuse(BLOCKS - 1, FT - 1, False)


def full_kernel(nc, a, out):
    x1_dram = nc.dram_tensor("x1_kept", [B, N, D], F32, kind="Internal").ap()
    x3t_dram = nc.dram_tensor("x3_transposed", [KD, P, TOK], F32, kind="Internal").ap()
    xn3t_dram = nc.dram_tensor("x3_normalised_transposed", [KD, P, TOK], F32, kind="Internal").ap()
    xn3_dram = nc.dram_tensor("x3_normalised", [TOK + P, D], F32, kind="Internal").ap()
    left_dram = nc.dram_tensor("x3_normalised_left", [TOK + 2 * P, D], F32, kind="Internal").ap()
    t_dram = nc.dram_tensor("t", [TOK + 2 * P, FFN], F32, kind="Internal").ap()
    wmax_dram = nc.dram_tensor("Wt_maxima", [1, D], F32, kind="Internal").ap()
    with ExitStack() as ctx:
        hx = ctx.enter_context(nc.sbuf_tensor("hx", [P, KD, 1 + N, B], F32))
        stage_gnn0(nc, a, hx, x1_dram)
        stage_lstm(nc, a, hx)
        stage_gnn1(nc, a, hx, x1_dram, x3t_dram, xn3t_dram, xn3_dram)
    stage_tropical(nc, a, xn3_dram, left_dram, t_dram, wmax_dram)
    stage_ffn(nc, a, x3t_dram, xn3t_dram, t_dram, out)


def kernel(**inputs):
    import concourse.bacc as bacc
    from concourse.bass_utils import run_bass_kernel_spmd

    given = {k: np.asarray(v) for k, v in inputs.items()}

    def gates_first_g(w):
        i, f, g, o = np.split(w, GATES, axis=0)
        return np.ascontiguousarray(np.concatenate([g, i, f, o], axis=0))

    def turned(w):
        return np.ascontiguousarray(w.T)

    def columns(v):
        return np.ascontiguousarray(v.reshape(-1, P).T)

    which = np.zeros((2, 2, 2, 4 * B), np.float32)
    which[:, 0, 0], which[:, 1, 1] = 1.0, 1.0
    ones = np.ones((P, P), np.float32)
    arrays = {
        "x": given["x"], "adj": given["adj"],
        "adjt": np.ascontiguousarray(given["adj"].transpose(0, 2, 1)),
        "theta": given["L0_gnn_theta"], "W_h": given["L0_gnn_W_h"], "W_t": given["L0_gnn_W_t"],
        "b_t": given["L0_gnn_b_t"].reshape(1, D),
        "w_ih_t": turned(gates_first_g(given["L0_ffn_W_ih"])),
        "w_hh_t": turned(gates_first_g(given["L0_ffn_W_hh"])),
        "b_ih": gates_first_g(given["L0_ffn_b_ih"]), "b_hh": gates_first_g(given["L0_ffn_b_hh"]),
        "w_lin_t": turned(given["L0_ffn_W_lin"]), "b_lin": given["L0_ffn_b_lin"].reshape(1, 2),
        "fw_att": given["L0_ffn_fw_att"], "bw_att": given["L0_ffn_bw_att"],
        "W1": given["L1_gnn_W"], "b1": given["L1_gnn_b"].reshape(1, D),
        "Wt_t": turned(given["L1_ffn_Wt"]), "Wc": given["L1_ffn_Wc"], "Wg": given["L1_ffn_Wg"], "Wd": given["L1_ffn_Wd"],
        "sl_cvx": given["L1_ffn_sl_cvx"], "of_cvx": given["L1_ffn_of_cvx"],
        "sl_ccv": given["L1_ffn_sl_ccv"], "of_ccv": given["L1_ffn_of_ccv"],
        "bt": columns(given["L1_ffn_bt"]), "bc": columns(given["L1_ffn_bc"]), "bg": columns(given["L1_ffn_bg"]),
        "alpha": columns(given["L1_ffn_alpha"]), "bd": columns(given["L1_ffn_bd"]),
        "ident": np.eye(P, dtype=np.float32),
        "before": np.triu(ones, 1), "after": np.tril(ones, -1), "which": which.reshape(4, 2 * 4 * B),
    }
    numbers = np.arange(P, dtype=np.float32)[:, None]
    tile_no = np.zeros((1, SLOTS), np.float32)
    tile_no[0, :TILES] = np.arange(1, TILES + 1)
    arrays |= {"p_plus": numbers, "p_minus": -numbers, "tile_no": tile_no}
    nc = bacc.Bacc("TRN2", target_bir_lowering=False, num_devices=1)
    a = {k: nc.dram_tensor(f"in_{k}", v.shape, mybir.dt.from_np(v.dtype), kind="ExternalInput").ap()
         for k, v in arrays.items()}
    out = nc.dram_tensor("out_t", [KD, P, TOK], F32, kind="ExternalOutput").ap()
    full_kernel(nc, a, out)
    r = run_bass_kernel_spmd(nc, [{f"in_{k}": v for k, v in arrays.items()}], core_ids=[0])
    out_t = np.asarray(r.results[0]["out_t"]).reshape(D, TOK)
    return np.ascontiguousarray(out_t.T).reshape(B, N, D)
```

```python
from contextlib import ExitStack
import numpy as np
import concourse.bass as bass
from concourse import mybir

F32 = mybir.dt.float32
BF16 = mybir.dt.bfloat16
ALU = mybir.AluOpType
ACT = mybir.ActivationFunctionType
AX = mybir.AxisListType
ds = bass.ds

P = 128
B, N, D = 64, 256, 256
KD = D // P
NT = N // P
TOK = B * N
H = 256
GATES = 4
FFN, PIECES = 1024, 8
FT = FFN // P
LN_EPS = 1e-5


def wait_past(eng, sem, value):
    if not isinstance(value, int) or value > 0:
        eng.wait_ge(sem, value)


def side_by_side(eng, parts, front, back):
    def both(i, j):
        for part in range(parts):
            front(i + j, 1 - j, 2 * i + j + 1, part)
            back(i, j, 2 * i + j, part)

    for part in range(parts):
        front(0, 0, 0, part)
    for j in range(2):
        both(0, j)
    with eng.Fori(1, B // 2 - 1) as i:
        for j in range(2):
            both(i, j)
    both(B // 2 - 1, 0)
    for part in range(parts):
        back(B // 2 - 1, 1, B - 1, part)


def clear_semaphores(nc, sems):
    with nc.Block() as block:
        @block.sync
        def _(sp):
            for s in sems:
                sp.sem_clear(s)


class Steps:

    def __init__(self, sem, per):
        self.sem, self.per = sem, per

    def begin(self, round_):
        self.base, self.k = round_ * self.per, 0

    def done(self, instruction):
        instruction.then_inc(self.sem, 1)
        self.k += 1
        return self.base + self.k

    def end(self):
        assert self.k == self.per, (self.k, self.per)


def stage_gnn0(nc, a, hx, x1_dram):
    sems = []
    with ExitStack() as ctx:
        def sb(name, shape, dt=F32):
            return ctx.enter_context(nc.sbuf_tensor(name, shape, dt))

        def ps(name, shape):
            return ctx.enter_context(nc.psum_tensor(name, shape, F32))

        def sem(name):
            sems.append(ctx.enter_context(nc.semaphore(name)))
            return sems[-1]

        w_cat = sb("g0_w", [P, KD, 3 * D])
        bt_row = sb("g0_bt", [1, D])
        ones_row = sb("g0_ones", [1, P])
        pause = sb("g0_pause", [1, 2])
        ident = sb("g0_ident", [P, P])
        x_in = [sb(f"g0_x{j}", [P, NT, D]) for j in range(2)]
        adj_in = [sb(f"g0_adj{j}", [P, NT, N]) for j in range(2)]
        adjt_in = [sb(f"g0_adjt{j}", [P, NT, N]) for j in range(2)]
        x1_out = [sb(f"g0_x1{j}", [P, NT, D]) for j in range(2)]
        stats = sb("g0_stats", [P, NT, 6])
        stats1 = sb("g0_stats1", [P, NT, 6])
        mv = sb("g0_mv", [P, NT, 2])
        rstd = sb("g0_rstd", [P, NT])
        mv1 = sb("g0_mv1", [P, NT, 2])
        rstd1 = sb("g0_rstd1", [P, NT])
        half = sb("g0_half", [P, NT])
        eps_ln = sb("g0_eps_ln", [P, NT])
        eps_deg = sb("g0_eps_deg", [P, NT])
        vare = sb("g0_vare", [P, NT])
        vare1 = sb("g0_vare1", [P, NT])
        dege = sb("g0_dege", [P, NT])
        deg = sb("g0_deg", [P, NT])
        norm = [sb(f"g0_norm{j}", [P, NT]) for j in range(2)]
        junk = sb("g0_junk", [P, NT, N])
        xn = sb("g0_xn", [P, NT, D])
        xn1 = sb("g0_xn1", [P, NT, D])
        xn_t = sb("g0_xnt", [P, KD, N])
        f_hom = [sb(f"g0_fhom{j}", [P, NT, D]) for j in range(2)]
        f_het = [sb(f"g0_fhet{j}", [P, NT, D]) for j in range(2)]
        tanh_z = [sb(f"g0_tanh_z{j}", [P, NT, D]) for j in range(2)]
        gate = sb("g0_gate", [P, NT, D])
        u = sb("g0_u", [P, NT, D])
        o = sb("g0_o", [P, NT, D])
        neg = sb("g0_neg", [P, NT, D])
        y = sb("g0_y", [P, NT, D])
        ps_t = ps("g0_pst", [P, KD, N])
        ps_hom_het = [ps(f"g0_psa{t}", [P, 2 * D]) for t in range(NT)]
        ps_gate = ps("g0_psg", [P, NT, D])
        ps_agg = ps("g0_psf", [P, NT, D])
        ps_t1 = ps("g0_pst1", [P, KD, N])

        const_in = sem("g0_const_in")
        graph_in = [sem(f"g0_graph_in{j}") for j in range(2)]
        x1_stored = [sem(f"g0_x1_stored{j}") for j in range(2)]
        half_set = sem("g0_half_set")
        ones_set = sem("g0_ones_set")
        front_steps = Steps(sem("g0_front_steps"), 1)
        back_steps = Steps(sem("g0_back_steps"), 6)
        pool_steps = Steps(sem("g0_pool_steps"), 2)
        pool_back_steps = Steps(sem("g0_pool_back_steps"), 1)
        mv_ready = sem("g0_mv_ready")
        rstd_ready = sem("g0_rstd_ready")
        xn_ready = sem("g0_xn_ready")
        xt_done = sem("g0_xt_done")
        xn_t_ready = sem("g0_xn_t_ready")
        proj_done = sem("g0_proj_done")
        gate_done = sem("g0_gate_done")
        deg_ready = sem("g0_deg_ready")
        norm_ready = sem("g0_norm_ready")
        f_hom_ready = sem("g0_f_hom_ready")
        f_het_ready = sem("g0_f_het_ready")
        tanh_z_ready = sem("g0_tanh_z_ready")
        agg_done = sem("g0_agg_done")
        neg_ready = sem("g0_neg_ready")
        exp_ready = sem("g0_exp_ready")
        x1_ready = sem("g0_x1_ready")
        mv1_ready = sem("g0_mv1_ready")
        rstd1_ready = sem("g0_rstd1_ready")
        xn1_ready = sem("g0_xn1_ready")
        xt1_done = sem("g0_xt1_done")
        hx_written = sem("g0_hx_written")
        CONST_DMAS = 5

        PARTS = 4
        block = ctx.enter_context(nc.Block())

        @block.sync
        def _(sp):
            sp.dma_start(w_cat[:, :, 0:D], a["theta"].rearrange("(k p) e -> p k e", p=P)).then_inc(const_in, 16)
            sp.dma_start(w_cat[:, :, D:2 * D], a["W_h"].rearrange("(k p) e -> p k e", p=P)).then_inc(const_in, 16)
            sp.dma_start(w_cat[:, :, 2 * D:3 * D], a["W_t"].rearrange("(k p) e -> p k e", p=P)).then_inc(const_in, 16)
            sp.dma_start(bt_row[:, :], a["b_t"]).then_inc(const_in, 16)
            sp.dma_start(ident[:, :], a["ident"]).then_inc(const_in, 16)

            def load(n, j):
                for dst, src in ((x_in, "x"), (adj_in, "adj"), (adjt_in, "adjt")):
                    sp.dma_start(dst[j][:, :, :], a[src][ds(n, 1)].rearrange("o (t p) e -> p (o t) e", p=P))\
                      .then_inc(graph_in[j], 16)

            def store(n, j):
                sp.wait_ge(x1_ready, n + 1)
                sp.dma_start(x1_dram[ds(n, 1)].rearrange("o (t p) e -> p (o t) e", p=P), x1_out[j][:, :, :])\
                  .then_inc(x1_stored[j], 16)

            for j in range(2):
                load(j, j)
            with sp.Fori(0, B // 2 - 1) as i:
                for j in range(2):
                    store(2 * i + j, j)
                    load(2 * i + j + 2, j)
            for j in range(2):
                store(B - 2 + j, j)
            for j in range(2):
                sp.wait_ge(x1_stored[j], 16 * (B // 2))

        @block.gpsimd
        def _(pool):
            pool.memset(half[:, :], -0.5).then_inc(half_set, 1)
            pool.memset(eps_ln[:, :], LN_EPS).then_inc(half_set, 1)
            pool.memset(eps_deg[:, :], 1e-6).then_inc(half_set, 1)
            pool.wait_ge(half_set, 3)

            def front(i, j, n, part):
                if part == 0:
                    pool_steps.begin(n)
                    pool.wait_ge(mv_ready, n + 1)
                    t = pool_steps.done(pool.tensor_tensor(vare[:, :], mv[:, :, 1], eps_ln[:, :], ALU.add))
                    pool.wait_ge(pool_steps.sem, t)
                    pool.tensor_tensor(rstd[:, :], vare[:, :], half[:, :], ALU.pow).then_inc(rstd_ready, 1)
                    pool.wait_ge(deg_ready, n + 1)
                    t = pool_steps.done(pool.tensor_tensor(dege[:, :], deg[:, :], eps_deg[:, :], ALU.add))
                    pool.wait_ge(pool_steps.sem, t)
                    pool.tensor_tensor(norm[j][:, :], dege[:, :], half[:, :], ALU.pow).then_inc(norm_ready, 1)
                    pool_steps.end()

            def back(i, j, n, part):
                if part == 2:
                    pool_back_steps.begin(n)
                    pool.wait_ge(mv1_ready, n + 1)
                    t = pool_back_steps.done(pool.tensor_tensor(vare1[:, :], mv1[:, :, 1], eps_ln[:, :], ALU.add))
                    pool.wait_ge(pool_back_steps.sem, t)
                    pool.tensor_tensor(rstd1[:, :], vare1[:, :], half[:, :], ALU.pow).then_inc(rstd1_ready, 1)
                    pool_back_steps.end()

            side_by_side(pool, PARTS, front, back)

        @block.scalar
        def _(act):
            def front(i, j, n, part):
                if part == 0:
                    act.wait_ge(graph_in[j], 48 * (i + 1))
                    wait_past(act, norm_ready, n)
                    wait_past(act, x1_ready, n - 1)
                    for t in range(NT):
                        last = act.activation(junk[:, t, :], adj_in[j][:, t, :], ACT.Abs, accum_out=deg[:, t:t + 1])
                    last.then_inc(deg_ready, 1)
                elif part == 1:
                    act.wait_ge(xt_done, n + 1)
                    wait_past(act, gate_done, n)
                    act.activation(xn_t[:, :, :], ps_t[:, :, :], ACT.Copy).then_inc(xn_t_ready, 1)
                elif part == 2:
                    act.wait_ge(norm_ready, n + 1)
                    act.wait_ge(proj_done, n + 1)
                    for t in range(NT):
                        last = act.activation(f_hom[j][:, t, :], ps_hom_het[t][:, 0:D], ACT.Copy, scale=norm[j][:, t:t + 1])
                    last.then_inc(f_hom_ready, 1)
                    for t in range(NT):
                        last = act.activation(f_het[j][:, t, :], ps_hom_het[t][:, D:2 * D], ACT.Copy)
                    last.then_inc(f_het_ready, 1)
                    act.wait_ge(gate_done, n + 1)
                    act.activation(tanh_z[j][:, :, :], ps_gate[:, :, :], ACT.Tanh, scale=0.5).then_inc(tanh_z_ready, 1)

            def back(i, j, n, part):
                if part == 1:
                    act.wait_ge(neg_ready, n + 1)
                    act.activation(neg[:, :, :], neg[:, :, :], ACT.Exp).then_inc(exp_ready, 1)
                elif part == 3:
                    act.wait_ge(xt1_done, n + 1)
                    act.activation(hx[:, :, 1:1 + N, ds(n, 1)].rearrange("p k t o -> p k (t o)"), ps_t1[:, :, :], ACT.Copy)\
                       .then_inc(hx_written, 1)

            side_by_side(act, PARTS, front, back)

        @block.tensor
        def _(pe):
            pe.wait_ge(const_in, 16 * CONST_DMAS)
            pe.wait_ge(ones_set, 1)

            def turn(dst, src):
                for k in range(KD):
                    for t in range(NT):
                        last = pe.transpose(dst[:, k, t * P:(t + 1) * P], src[:, t, k * P:(k + 1) * P], ident[:, :])
                return last

            def front(i, j, n, part):
                if part == 1:
                    pe.wait_ge(xn_ready, n + 1)
                    wait_past(pe, xn_t_ready, n)
                    turn(ps_t, xn).then_inc(xt_done, 1)
                elif part == 2:
                    pe.wait_ge(xn_t_ready, n + 1)
                    wait_past(pe, f_het_ready, n)
                    for t in range(NT):
                        for k in range(KD):
                            last = pe.matmul(ps_hom_het[t][:, :], xn_t[:, k, t * P:(t + 1) * P], w_cat[:, k, 0:2 * D],
                                             start=(k == 0), stop=(k == KD - 1))
                    last.then_inc(proj_done, 1)
                    wait_past(pe, tanh_z_ready, n)
                    for t in range(NT):
                        for k in range(KD):
                            pe.matmul(ps_gate[:, t, :], xn_t[:, k, t * P:(t + 1) * P], w_cat[:, k, 2 * D:3 * D],
                                      start=(k == 0), stop=False)
                        last = pe.matmul(ps_gate[:, t, :], ones_row[:, :], bt_row[:, :], start=False, stop=True)
                    last.then_inc(gate_done, 1)

            def back(i, j, n, part):
                if part == 0:
                    pe.wait_ge(graph_in[j], 48 * (i + 1))
                    pe.wait_ge(f_hom_ready, n + 1)
                    wait_past(pe, neg_ready, n)
                    for t in range(NT):
                        for m in range(NT):
                            last = pe.matmul(ps_agg[:, t, :], adjt_in[j][:, m, t * P:(t + 1) * P], f_hom[j][:, m, :],
                                             start=(m == 0), stop=(m == NT - 1))
                    last.then_inc(agg_done, 1)
                elif part == 3:
                    pe.wait_ge(xn1_ready, n + 1)
                    wait_past(pe, hx_written, n)
                    turn(ps_t1, xn1).then_inc(xt1_done, 1)

            side_by_side(pe, PARTS, front, back)

        @block.vector
        def _(dve):
            dve.memset(ones_row[:, :], 1.0).then_inc(ones_set, 1)

            def statistics(src, stats_, steps, k, mv_, mv_sem):
                for t in range(NT):
                    last = dve.bn_stats(stats_[:, t, :], src[:, t, :])
                v = steps.done(last)
                dve.wait_ge(steps.sem, v)
                dve.memset(pause[:, k:k + 1], 0.0)
                for t in range(NT):
                    last = dve.bn_aggr(mv_[:, t, :], stats_[:, t, :])
                last.then_inc(mv_sem, 1)

            def normalised(dst, src, mv_, rstd_, rstd_sem, xn_sem, n):
                dve.wait_ge(rstd_sem, n + 1)
                for t in range(NT):
                    last = dve.tensor_scalar(dst[:, t, :], src[:, t, :], mv_[:, t, 0:1], rstd_[:, t:t + 1],
                                             ALU.subtract, ALU.mult)
                last.then_inc(xn_sem, 1)

            def front(i, j, n, part):
                if part == 0:
                    front_steps.begin(n)
                    dve.wait_ge(graph_in[j], 48 * (i + 1))
                    statistics(x_in[j], stats, front_steps, 0, mv, mv_ready)
                    front_steps.end()
                elif part == 1:
                    wait_past(dve, xt_done, n)
                    normalised(xn, x_in[j], mv, rstd, rstd_ready, xn_ready, n)

            def back(i, j, n, part):
                if part == 0:
                    back_steps.begin(n)
                    dve.wait_ge(tanh_z_ready, n + 1)
                    v = back_steps.done(dve.tensor_scalar(gate[:, :, :], tanh_z[j][:, :, :], 0.5, 0.5, ALU.mult, ALU.add))
                elif part == 1:
                    dve.wait_ge(agg_done, n + 1)
                    dve.wait_ge(f_het_ready, n + 1)
                    for t in range(NT):
                        last = dve.scalar_tensor_tensor(u[:, t, :], ps_agg[:, t, :], norm[j][:, t:t + 1], f_het[j][:, t, :],
                                                        ALU.mult, ALU.subtract)
                    v = back_steps.done(last)
                    dve.wait_ge(back_steps.sem, v)
                    v = back_steps.done(dve.tensor_tensor(u[:, :, :], u[:, :, :], gate[:, :, :], ALU.mult))
                    dve.wait_ge(back_steps.sem, v)
                    v = back_steps.done(dve.tensor_tensor(o[:, :, :], u[:, :, :], f_het[j][:, :, :], ALU.add))
                    dve.wait_ge(back_steps.sem, v)
                    dve.tensor_scalar(neg[:, :, :], o[:, :, :], 0.0, None, ALU.min).then_inc(neg_ready, 1)
                    v = back_steps.done(dve.scalar_tensor_tensor(y[:, :, :], o[:, :, :], 0.0, x_in[j][:, :, :],
                                                                 ALU.max, ALU.add))
                elif part == 2:
                    dve.wait_ge(back_steps.sem, 6 * n + 5)
                    dve.wait_ge(exp_ready, n + 1)
                    wait_past(dve, x1_stored[j], 16 * i)
                    dve.scalar_tensor_tensor(x1_out[j][:, :, :], neg[:, :, :], -1.0, y[:, :, :],
                                             ALU.add, ALU.add).then_inc(x1_ready, 1)
                    dve.wait_ge(x1_ready, n + 1)
                    statistics(x1_out[j], stats1, back_steps, 1, mv1, mv1_ready)
                elif part == 3:
                    wait_past(dve, xt1_done, n)
                    normalised(xn1, x1_out[j], mv1, rstd1, rstd1_ready, xn1_ready, n)
                    back_steps.end()

            side_by_side(dve, PARTS, front, back)
    clear_semaphores(nc, sems)




def stage_lstm(nc, a, hx):
    T, S = N, 4
    ROWS = GATES * H // P
    sems = []
    with ExitStack() as ctx:
        def sb(name, shape, dt=F32):
            return ctx.enter_context(nc.sbuf_tensor(name, shape, dt))

        def sem(name):
            sems.append(ctx.enter_context(nc.semaphore(name)))
            return sems[-1]

        w_ih = sb("l_wih", [P, KD, GATES * H])
        w_hh = sb("l_whh", [P, KD, GATES * H])
        bias = sb("l_bias", [4, GATES, P])
        which = sb("l_which", [4, 2 * S * B])
        act_g = [sb(f"l_act{q}", [P, 2, B]) for q in range(GATES)]
        c = sb("l_c", [P, 2, B])
        ig = sb("l_ig", [P, 2, B])
        tc_ = sb("l_tc", [P, 2, B])
        ps_g = [[ctx.enter_context(nc.psum_tensor(f"l_ps{s}{q}", [P, 2, S, B], F32)) for q in range(GATES)]
                for s in range(2)]

        const_in = sem("l_const_in")
        zero_set = sem("l_zero_set")
        gate_done = [sem(f"l_gate_done{q}") for q in range(GATES)]
        act_ready = [sem(f"l_act_ready{q}") for q in range(GATES)]
        ig_ready = sem("l_ig_ready")
        fc_ready = sem("l_fc_ready")
        c_ready = sem("l_c_ready")
        tanh_c_ready = sem("l_tanh_c_ready")
        h_ready = sem("l_h_ready")
        block = ctx.enter_context(nc.Block())

        @block.sync
        def _(sp):
            sp.dma_start(w_ih[:, :, :], a["w_ih_t"].rearrange("(k p) g -> p k g", p=P)).then_inc(const_in, 16)
            sp.dma_start(w_hh[:, :, :], a["w_hh_t"].rearrange("(k p) g -> p k g", p=P)).then_inc(const_in, 16)
            sp.dma_start(bias[0:2, :, :], a["b_ih"].rearrange("(q c m) -> c q m", q=GATES, c=2)).then_inc(const_in, 16)
            sp.dma_start(bias[2:4, :, :], a["b_hh"].rearrange("(q c m) -> c q m", q=GATES, c=2)).then_inc(const_in, 16)
            sp.dma_start(which[:, :], a["which"]).then_inc(const_in, 16)

        @block.vector
        def _(dve):
            dve.memset(hx[:, :, 0:1, :], 0.0).then_inc(zero_set, 1)
            dve.memset(c[:, :, :], 0.0).then_inc(zero_set, 1)
            dve.wait_ge(zero_set, 2)

            def step(t):
                dve.wait_ge(act_ready[0], t + 1)
                dve.wait_ge(act_ready[1], t + 1)
                dve.tensor_tensor(ig[:, :, :], act_g[0][:, :, :], act_g[1][:, :, :], ALU.mult).then_inc(ig_ready, 1)
                dve.wait_ge(act_ready[2], t + 1)
                wait_past(dve, c_ready, t)
                dve.tensor_tensor(c[:, :, :], c[:, :, :], act_g[2][:, :, :], ALU.mult).then_inc(fc_ready, 1)
                dve.wait_ge(ig_ready, t + 1)
                dve.wait_ge(fc_ready, t + 1)
                dve.tensor_tensor(c[:, :, :], c[:, :, :], ig[:, :, :], ALU.add).then_inc(c_ready, 1)
                dve.wait_ge(act_ready[3], t + 1)
                dve.wait_ge(tanh_c_ready, t + 1)
                dve.tensor_tensor(hx[:, :, ds(t + 1, 1), :].rearrange("p k o b -> p k (o b)"), act_g[3][:, :, :],
                                  tc_[:, :, :], ALU.mult).then_inc(h_ready, 1)

            step(0)
            with dve.Fori(1, T) as t:
                step(t)

        @block.scalar
        def _(act):
            def step(t, s, r):
                for q in range(GATES):
                    act.wait_ge(gate_done[q], t + 1)
                    if q == 0:
                        wait_past(act, h_ready, t)
                    act.activation(act_g[q][:, :, :], ps_g[s][q][:, :, r, :], ACT.Tanh if q == 0 else ACT.Sigmoid)\
                       .then_inc(act_ready[q], 1)
                act.wait_ge(c_ready, t + 1)
                act.activation(tc_[:, :, :], c[:, :, :], ACT.Tanh).then_inc(tanh_c_ready, 1)

            def groups(i):
                for s in range(2):
                    for r in range(S):
                        step(2 * S * i + S * s + r, s, r)

            groups(0)
            with act.Fori(1, T // (2 * S)) as i:
                groups(i)

        @block.tensor
        def _(pe):
            def input_part(group, s, q):
                pe.matmul(ps_g[s][q][:, :, :, :], bias[:, q, :], which[:, :], start=True, stop=False,
                          skip_group_check=True)
                for c2 in range(2):
                    row = (2 * q + c2) * P
                    for k in range(KD):
                        pe.matmul(ps_g[s][q][:, c2, :, :], w_ih[:, k, row:row + P],
                                  hx[:, k, ds(S * group + 1, S), :], start=False, stop=False,
                                  skip_group_check=True)

            def steps(i, s, last):
                group = 2 * i + s
                for r in range(S):
                    t = S * group + r
                    wait_past(pe, h_ready, t)
                    for q in range(GATES):
                        for c2 in range(2):
                            row = (2 * q + c2) * P
                            for k in range(KD):
                                mm = pe.matmul(ps_g[s][q][:, c2, r, :], w_hh[:, k, row:row + P],
                                               hx[:, k, ds(t, 1), :].rearrange("p o b -> p (o b)"), start=False,
                                               stop=(r == S - 1 and c2 == 1 and k == KD - 1), skip_group_check=True)
                        mm.then_inc(gate_done[q], 1)
                    if not last:
                        input_part(group + 1, 1 - s, r)

            pe.wait_ge(const_in, 16 * 5)
            pe.wait_ge(zero_set, 2)
            for q in range(GATES):
                input_part(0, 0, q)
            for s in range(2):
                steps(0, s, False)
            with pe.Fori(1, T // (2 * S) - 1) as i:
                for s in range(2):
                    steps(i, s, False)
            for s in range(2):
                steps(T // (2 * S) - 1, s, s == 1)
    clear_semaphores(nc, sems)


def stage_gnn1(nc, a, hx, x1_dram, x3t_dram, xn3t_dram, xn3_dram):
    sems = []
    with ExitStack() as ctx:
        def sb(name, shape, dt=F32):
            return ctx.enter_context(nc.sbuf_tensor(name, shape, dt))

        def ps(name, shape):
            return ctx.enter_context(nc.psum_tensor(name, shape, F32))

        def sem(name):
            sems.append(ctx.enter_context(nc.semaphore(name)))
            return sems[-1]

        w = sb("g1_w", [P, KD, D])
        w_lin = sb("g1_wlin", [P, KD, 2])
        b_lin = sb("g1_blin", [1, 2])
        ones_row = sb("g1_ones_row", [1, P])
        ones_sq = sb("g1_ones_sq", [P, P])
        before = sb("g1_before", [P, P])
        after = sb("g1_after", [P, P])
        ident = sb("g1_ident", [P, P])
        fw = sb("g1_fw", [P, NT, D])
        bw = sb("g1_bw", [P, NT, D])
        b_all = sb("g1_b", [P, NT, D])
        x1_in = [sb(f"g1_x1{j}", [P, NT, D]) for j in range(2)]
        adj_in = [sb(f"g1_adj{j}", [P, NT, N]) for j in range(2)]
        adjt_in = [sb(f"g1_adjt{j}", [P, NT, N]) for j in range(2)]
        xn3_out = [sb(f"g1_xn3{j}", [P, NT, D]) for j in range(2)]
        x3t_out = [sb(f"g1_x3t{j}", [P, KD, N]) for j in range(2)]
        xn3t_out = [sb(f"g1_xn3t{j}", [P, KD, N]) for j in range(2)]
        mv3 = sb("g1_mv3", [P, NT, 2])
        rstd3 = sb("g1_rstd3", [P, NT])
        h_t = sb("g1_ht", [P, KD, N])
        h = sb("g1_h", [P, NT, D])
        logit = sb("g1_logit", [P, NT, 2])
        picked = sb("g1_picked", [P, NT])
        wh = sb("g1_wh", [P, NT, D])
        y = sb("g1_y", [P, NT, D])
        z = sb("g1_z", [P, NT, D])
        z3 = sb("g1_z3", [P, NT, D])
        x2 = sb("g1_x2", [P, NT, D])
        x2b = [sb(f"g1_x2b{j}", [P, NT, D]) for j in range(2)]
        x3 = sb("g1_x3", [P, NT, D])
        pause = sb("g1_pause", [1, 2])
        stats = sb("g1_stats", [P, NT, 6])
        stats3 = sb("g1_stats3", [P, NT, 6])
        mv = sb("g1_mv", [P, NT, 2])
        rstd = sb("g1_rstd", [P, NT])
        half = sb("g1_half", [P, NT])
        eps = sb("g1_eps", [P, NT])
        one = sb("g1_one", [P, NT])
        vare = sb("g1_vare", [P, NT])
        vare3 = sb("g1_vare3", [P, NT])
        row_sum = sb("g1_row_sum", [P, NT])
        is_zero = sb("g1_is_zero", [P, NT])
        deg_safe = sb("g1_deg_safe", [P, NT])
        keep = sb("g1_keep", [P, NT])
        power = sb("g1_power", [P, NT])
        dinv = [sb(f"g1_dinv{j}", [P, NT]) for j in range(2)]
        junk = sb("g1_junk", [P, NT, N])
        xn = [sb(f"g1_xn{j}", [P, NT, D]) for j in range(2)]
        xn_t = sb("g1_xnt", [P, KD, N])
        hs = sb("g1_hs", [P, NT, D])
        ps_logit = ps("g1_ps_logit", [P, NT, 2])
        ps_h = ps("g1_ps_h", [P, NT, D])
        ps_pre = ps("g1_ps_pre", [P, NT, D])
        ps_suf = ps("g1_ps_suf", [P, NT, D])
        ps_t = ps("g1_ps_t", [P, KD, N])
        ps_w = ps("g1_ps_w", [P, NT, D])
        ps_agg = ps("g1_ps_agg", [P, NT, D])
        ps_x3t = ps("g1_ps_x3t", [P, KD, N])

        const_in = sem("g1_const_in")
        graph_in = [sem(f"g1_graph_in{j}") for j in range(2)]
        x3t_stored = [sem(f"g1_x3t_stored{j}") for j in range(2)]
        consts_set = sem("g1_consts_set")
        ones_set = sem("g1_ones_set")
        front_steps = Steps(sem("g1_front_steps"), 6)
        back_steps = Steps(sem("g1_back_steps"), 2)
        pool_steps = Steps(sem("g1_pool_steps"), 2)
        pool_back_steps = Steps(sem("g1_pool_back_steps"), 1)
        h_t_ready = sem("g1_h_t_ready")
        logit_done = sem("g1_logit_done")
        logit_ready = sem("g1_logit_ready")
        h_done = sem("g1_h_done")
        h_ready = sem("g1_h_ready")
        picked_ready = sem("g1_picked_ready")
        wh_ready = sem("g1_wh_ready")
        sums_done = sem("g1_sums_done")
        mv_ready = sem("g1_mv_ready")
        rstd_ready = sem("g1_rstd_ready")
        xn_ready = sem("g1_xn_ready")
        xt_done = sem("g1_xt_done")
        xn_t_ready = sem("g1_xn_t_ready")
        proj_done = sem("g1_proj_done")
        row_sum_ready = sem("g1_row_sum_ready")
        deg_ready = sem("g1_deg_ready")
        dinv_ready = sem("g1_dinv_ready")
        hs_ready = sem("g1_hs_ready")
        agg_done = sem("g1_agg_done")
        x2_ready = sem("g1_x2_ready")
        x3_ready = sem("g1_x3_ready")
        x3t_done = sem("g1_x3t_done")
        mv3_ready = sem("g1_mv3_ready")
        rstd3_ready = sem("g1_rstd3_ready")
        xn3_ready = sem("g1_xn3_ready")
        xn3t_done = sem("g1_xn3t_done")
        xn3t_ready = sem("g1_xn3t_ready")
        CONSTS = ("w", "w_lin", "b_lin", "ident", "before", "after", "fw", "bw", "b")

        PARTS = 5
        block = ctx.enter_context(nc.Block())

        @block.sync
        def _(sp):
            sp.dma_start(w[:, :, :], a["W1"].rearrange("(k p) e -> p k e", p=P)).then_inc(const_in, 16)
            sp.dma_start(w_lin[:, :, :], a["w_lin_t"].rearrange("(k p) c -> p k c", p=P)).then_inc(const_in, 16)
            sp.dma_start(b_lin[:, :], a["b_lin"]).then_inc(const_in, 16)
            sp.dma_start(ident[:, :], a["ident"]).then_inc(const_in, 16)
            sp.dma_start(before[:, :], a["before"]).then_inc(const_in, 16)
            sp.dma_start(after[:, :], a["after"]).then_inc(const_in, 16)
            for t in range(NT):
                for dst, src in ((fw, "fw_att"), (bw, "bw_att"), (b_all, "b1")):
                    sp.dma_start(dst[:, t, :], a[src].to_broadcast([P, D])).then_inc(const_in, 16)

            def load(n, j):
                for dst, src in ((x1_in, x1_dram), (adj_in, a["adj"]), (adjt_in, a["adjt"])):
                    sp.dma_start(dst[j][:, :, :], src[ds(n, 1)].rearrange("o (t p) e -> p (o t) e", p=P))\
                      .then_inc(graph_in[j], 16)

            def store(n, j):
                sp.wait_ge(xn3t_ready, n + 1)
                for dst, src in ((x3t_dram, x3t_out), (xn3t_dram, xn3t_out)):
                    sp.dma_start(dst[:, :, ds(n * N, N)].rearrange("k p t -> p k t"), src[j][:, :, :])\
                      .then_inc(x3t_stored[j], 16)
                sp.dma_start(xn3_dram[ds(n * N, N), :].rearrange("(t p) e -> p t e", p=P), xn3_out[j][:, :, :])\
                  .then_inc(x3t_stored[j], 16)

            for j in range(2):
                load(j, j)
            with sp.Fori(0, B // 2 - 1) as i:
                for j in range(2):
                    store(2 * i + j, j)
                    load(2 * i + j + 2, j)
            for j in range(2):
                store(B - 2 + j, j)
            for j in range(2):
                sp.wait_ge(x3t_stored[j], 48 * (B // 2))

        @block.gpsimd
        def _(pool):
            pool.memset(half[:, :], -0.5).then_inc(consts_set, 1)
            pool.memset(eps[:, :], LN_EPS).then_inc(consts_set, 1)
            pool.memset(one[:, :], 1.0).then_inc(consts_set, 1)
            pool.wait_ge(consts_set, 3)

            def front(i, j, n, part):
                if part == 1:
                    pool_steps.begin(n)
                    pool.wait_ge(deg_ready, n + 1)
                    pool.tensor_tensor(power[:, :], deg_safe[:, :], half[:, :], ALU.pow)
                    t = pool_steps.done(pool.tensor_tensor(keep[:, :], one[:, :], is_zero[:, :], ALU.subtract))
                    pool.wait_ge(pool_steps.sem, t)
                    pool.tensor_tensor(dinv[j][:, :], power[:, :], keep[:, :], ALU.mult).then_inc(dinv_ready, 1)
                elif part == 2:
                    pool.wait_ge(mv_ready, n + 1)
                    t = pool_steps.done(pool.tensor_tensor(vare[:, :], mv[:, :, 1], eps[:, :], ALU.add))
                    pool.wait_ge(pool_steps.sem, t)
                    pool.tensor_tensor(rstd[:, :], vare[:, :], half[:, :], ALU.pow).then_inc(rstd_ready, 1)
                    pool_steps.end()

            def back(i, j, n, part):
                if part == 2:
                    pool_back_steps.begin(n)
                    pool.wait_ge(mv3_ready, n + 1)
                    t = pool_back_steps.done(pool.tensor_tensor(vare3[:, :], mv3[:, :, 1], eps[:, :], ALU.add))
                    pool.wait_ge(pool_back_steps.sem, t)
                    pool.tensor_tensor(rstd3[:, :], vare3[:, :], half[:, :], ALU.pow).then_inc(rstd3_ready, 1)
                    pool_back_steps.end()

            side_by_side(pool, PARTS, front, back)

        @block.scalar
        def _(act):
            def front(i, j, n, part):
                if part == 0:
                    wait_past(act, h_done, n)
                    act.activation(h_t[:, :, :], hx[:, :, 1:1 + N, ds(n, 1)].rearrange("p k t o -> p k (t o)"), ACT.Copy)\
                       .then_inc(h_t_ready, 1)
                    wait_past(act, x2_ready, n)
                    act.wait_ge(logit_done, n + 1)
                    act.activation(logit[:, :, :], ps_logit[:, :, :], ACT.Copy).then_inc(logit_ready, 1)
                    act.wait_ge(h_done, n + 1)
                    act.activation(h[:, :, :], ps_h[:, :, :], ACT.Copy).then_inc(h_ready, 1)
                elif part == 1:
                    act.wait_ge(graph_in[j], 48 * (i + 1))
                    wait_past(act, dinv_ready, n)
                    for t in range(NT):
                        last = act.activation(junk[:, t, :], adj_in[j][:, t, :], ACT.Copy, accum_out=row_sum[:, t:t + 1])
                    last.then_inc(row_sum_ready, 1)

            def back(i, j, n, part):
                if part == 0:
                    act.wait_ge(xt_done, n + 1)
                    act.activation(xn_t[:, :, :], ps_t[:, :, :], ACT.Copy).then_inc(xn_t_ready, 1)
                elif part == 1:
                    act.wait_ge(dinv_ready, n + 1)
                    act.wait_ge(proj_done, n + 1)
                    for t in range(NT):
                        last = act.activation(hs[:, t, :], ps_w[:, t, :], ACT.Copy, scale=dinv[j][:, t:t + 1])
                    last.then_inc(hs_ready, 1)
                elif part == 4:
                    act.wait_ge(x3t_done, n + 1)
                    wait_past(act, x3t_stored[j], 48 * i)
                    act.activation(x3t_out[j][:, :, :], ps_x3t[:, :, :], ACT.Copy)
                    act.wait_ge(xn3t_done, n + 1)
                    act.activation(xn3t_out[j][:, :, :], ps_t[:, :, :], ACT.Copy).then_inc(xn3t_ready, 1)

            side_by_side(act, PARTS, front, back)

        @block.tensor
        def _(pe):
            pe.wait_ge(const_in, 16 * (len(CONSTS) + 3))
            pe.wait_ge(ones_set, 2)

            def turn(dst, src):
                for k in range(2):
                    for t in range(2):
                        last = pe.transpose(dst[:, k, t * P:(t + 1) * P], src[:, t, k * P:(k + 1) * P], ident[:, :])
                return last

            def front(i, j, n, part):
                if part == 0:
                    pe.wait_ge(h_t_ready, n + 1)
                    wait_past(pe, h_ready, n)
                    for t in range(NT):
                        for k in range(KD):
                            pe.matmul(ps_logit[:, t, :], h_t[:, k, t * P:(t + 1) * P], w_lin[:, k, :],
                                      start=(k == 0), stop=False)
                        last = pe.matmul(ps_logit[:, t, :], ones_row[:, :], b_lin[:, :], start=False, stop=True)
                    last.then_inc(logit_done, 1)
                    turn(ps_h, h_t).then_inc(h_done, 1)
                elif part == 1:
                    pe.wait_ge(wh_ready, n + 1)
                    pe.matmul(ps_pre[:, 0, :], before[:, :], wh[:, 0, :], start=True, stop=True)
                    pe.matmul(ps_pre[:, 1, :], ones_sq[:, :], wh[:, 0, :], start=True, stop=False)
                    pe.matmul(ps_pre[:, 1, :], before[:, :], wh[:, 1, :], start=False, stop=True)
                    pe.matmul(ps_suf[:, 0, :], after[:, :], wh[:, 0, :], start=True, stop=False)
                    pe.matmul(ps_suf[:, 0, :], ones_sq[:, :], wh[:, 1, :], start=False, stop=True)
                    pe.matmul(ps_suf[:, 1, :], after[:, :], wh[:, 1, :], start=True, stop=True).then_inc(sums_done, 1)

            def back(i, j, n, part):
                if part == 0:
                    pe.wait_ge(xn_ready, n + 1)
                    wait_past(pe, xn3t_ready, n)
                    turn(ps_t, xn[j]).then_inc(xt_done, 1)
                elif part == 1:
                    pe.wait_ge(xn_t_ready, n + 1)
                    for t in range(NT):
                        for k in range(KD):
                            last = pe.matmul(ps_w[:, t, :], xn_t[:, k, t * P:(t + 1) * P], w[:, k, :],
                                             start=(k == 0), stop=(k == KD - 1))
                    last.then_inc(proj_done, 1)
                elif part == 2:
                    pe.wait_ge(graph_in[j], 48 * (i + 1))
                    pe.wait_ge(hs_ready, n + 1)
                    for t in range(NT):
                        for m in range(NT):
                            last = pe.matmul(ps_agg[:, t, :], adjt_in[j][:, m, t * P:(t + 1) * P], hs[:, m, :],
                                             start=(m == 0), stop=(m == NT - 1))
                    last.then_inc(agg_done, 1)
                elif part == 3:
                    pe.wait_ge(x3_ready, n + 1)
                    turn(ps_x3t, x3).then_inc(x3t_done, 1)
                    pe.wait_ge(xn3_ready, n + 1)
                    turn(ps_t, xn3_out[j]).then_inc(xn3t_done, 1)

            side_by_side(pe, PARTS, front, back)

        @block.vector
        def _(dve):
            dve.memset(ones_row[:, :], 1.0).then_inc(ones_set, 1)
            dve.memset(ones_sq[:, :], 1.0).then_inc(ones_set, 1)
            dve.wait_ge(const_in, 16 * (len(CONSTS) + 3))

            def statistics(src, stats_, steps, k, mv_, mv_sem):
                for t in range(NT):
                    last = dve.bn_stats(stats_[:, t, :], src[:, t, :])
                v = steps.done(last)
                dve.wait_ge(steps.sem, v)
                dve.memset(pause[:, k:k + 1], 0.0)
                for t in range(NT):
                    last = dve.bn_aggr(mv_[:, t, :], stats_[:, t, :])
                last.then_inc(mv_sem, 1)

            def normalised(dst, src, mv_, rstd_, rstd_sem, xn_sem, n):
                dve.wait_ge(rstd_sem, n + 1)
                for t in range(NT):
                    last = dve.tensor_scalar(dst[:, t, :], src[:, t, :], mv_[:, t, 0:1], rstd_[:, t:t + 1],
                                             ALU.subtract, ALU.mult)
                last.then_inc(xn_sem, 1)

            def front(i, j, n, part):
                if part == 0:
                    front_steps.begin(n)
                    dve.wait_ge(logit_ready, n + 1)
                    dve.tensor_tensor(picked[:, :], logit[:, :, 1], logit[:, :, 0], ALU.is_gt).then_inc(picked_ready, 1)
                    dve.wait_ge(picked_ready, n + 1)
                    dve.wait_ge(h_ready, n + 1)
                    wait_past(dve, sums_done, n)
                    for t in range(NT):
                        last = dve.tensor_scalar(wh[:, t, :], h[:, t, :], picked[:, t:t + 1], None, ALU.mult)
                    last.then_inc(wh_ready, 1)
                    dve.wait_ge(row_sum_ready, n + 1)
                    v = front_steps.done(dve.tensor_scalar(is_zero[:, :], row_sum[:, :], 1.0, 0.0, ALU.add, ALU.is_equal))
                    dve.wait_ge(front_steps.sem, v)
                    dve.scalar_tensor_tensor(deg_safe[:, :], row_sum[:, :], 1.0, is_zero[:, :], ALU.add, ALU.add)\
                       .then_inc(deg_ready, 1)
                elif part == 1:
                    dve.wait_ge(sums_done, n + 1)
                    dve.tensor_tensor(y[:, :, :], ps_pre[:, :, :], fw[:, :, :], ALU.mult)
                    v = front_steps.done(dve.tensor_tensor(z[:, :, :], ps_suf[:, :, :], bw[:, :, :], ALU.mult))
                    dve.wait_ge(front_steps.sem, v)
                    v = front_steps.done(dve.scalar_tensor_tensor(y[:, :, :], h[:, :, :], 2.0, y[:, :, :],
                                                                  ALU.mult, ALU.add))
                    dve.wait_ge(front_steps.sem, v)
                    v = front_steps.done(dve.tensor_tensor(y[:, :, :], y[:, :, :], z[:, :, :], ALU.add))
                    dve.wait_ge(front_steps.sem, v)
                    dve.wait_ge(graph_in[j], 48 * (i + 1))
                    v = front_steps.done(dve.tensor_tensor(x2[:, :, :], x1_in[j][:, :, :], y[:, :, :], ALU.add))
                    dve.wait_ge(front_steps.sem, v)
                    dve.tensor_tensor(x2b[j][:, :, :], x2[:, :, :], b_all[:, :, :], ALU.add).then_inc(x2_ready, 1)
                    statistics(x2, stats, front_steps, 0, mv, mv_ready)
                elif part == 2:
                    normalised(xn[j], x2, mv, rstd, rstd_ready, xn_ready, n)
                    front_steps.end()

            def back(i, j, n, part):
                if part == 1:
                    back_steps.begin(n)
                    dve.wait_ge(agg_done, n + 1)
                    v = back_steps.done(dve.tensor_tensor(z3[:, :, :], ps_agg[:, :, :], hs[:, :, :], ALU.add))
                    dve.wait_ge(back_steps.sem, v)
                    wait_past(dve, x3t_done, n)
                    for t in range(NT):
                        last = dve.scalar_tensor_tensor(x3[:, t, :], z3[:, t, :], dinv[j][:, t:t + 1], x2b[j][:, t, :],
                                                        ALU.mult, ALU.add)
                    last.then_inc(x3_ready, 1)
                    dve.wait_ge(x3_ready, n + 1)
                    statistics(x3, stats3, back_steps, 1, mv3, mv3_ready)
                elif part == 2:
                    wait_past(dve, x3t_stored[j], 48 * i)
                    normalised(xn3_out[j], x3, mv3, rstd3, rstd3_ready, xn3_ready, n)
                    back_steps.end()

            side_by_side(dve, PARTS, front, back)
    clear_semaphores(nc, sems)


LEVELS = 4
CAND = 8
TILES = TOK // P
SLOTS = TILES + 4
LOWEST = -3.0e38
RING = 3


def ring(c):
    return c % RING, (RING if c > 1 else 2)


def stage_tropical(nc, a, xn3_dram, left_dram, t_dram, wmax_dram):
    with ExitStack() as ctx:
        def sb(name, shape, dt=F32):
            return ctx.enter_context(nc.sbuf_tensor(name, shape, dt))

        I32 = mybir.dt.int32
        v = dict(
            ident=sb("t_ident", [P, P]), ident_b=sb("t_identb", [P, P], BF16),
            w_part=[sb(f"t_wpart{s}", [P, KD, FFN], BF16) for s in range(3)],
            p_minus=sb("t_pminus", [P, 1]), p_plus=sb("t_pplus", [P, 1]),
            wmax=sb("t_wmax", [P, KD, P]),
            acc=[sb(f"t_acc{r}", [P, FFN]) for r in range(2)],
            t_out=[sb(f"t_tout{j}", [P, FFN]) for j in range(2)],
            certified=sb("t_certified", [P, SLOTS]),
            order=sb("t_order", [P, SLOTS]),
            index=[ctx.enter_context(nc.psum_tensor(f"t_index{b}", [P, 4 * P], F32)) for b in range(2)],
            fetched=[ctx.enter_context(nc.psum_tensor(f"t_fetched{r}", [P, FFN], F32)) for r in range(RING)],
            from_all=sb("t_fromall", [P, SLOTS], I32), to_all=sb("t_toall", [P, SLOTS], I32),
            most_int=sb("t_mostint", [1, 1], I32),
        )
        tropical_consts(nc, a, v, xn3_dram, left_dram, t_dram, wmax_dram)
        for level in range(LEVELS):
            plan_slots(nc, v, level)
            tropical_level(nc, v, level, xn3_dram, left_dram, t_dram)
        plan_slots(nc, v, LEVELS)
        tropical_general(nc, v, xn3_dram, t_dram)


def tropical_consts(nc, a, v, xn3_dram, left_dram, t_dram, wmax_dram):
    with ExitStack() as ctx:
        def sb(name, shape, dt=F32):
            return ctx.enter_context(nc.sbuf_tensor(name, shape, dt))

        def sem(name):
            return ctx.enter_context(nc.semaphore("tc_" + name))

        w_t = sb("tc_w", [P, KD, FFN])
        w_rest, w_rest2 = sb("tc_wrest", [P, KD, FFN]), sb("tc_wrest2", [P, KD, FFN])
        wmax_col = sb("tc_wmaxcol", [P, KD])
        zeros = sb("tc_zeros", [P, FFN])
        w_part, wmax = v["w_part"], v["wmax"]
        const_in, w_split, w_hi, w_mid, w_rest_ready = (
            sem(n) for n in ("const_in", "w_split", "w_hi", "w_mid", "w_rest_ready"))
        wmax_col_ready, wmax_kept, wmax_in, zeros_ready, spare_kept = (
            sem(n) for n in ("wmax_col_ready", "wmax_kept", "wmax_in", "zeros_ready", "spare_kept"))
        block = ctx.enter_context(nc.Block())

        @block.sync
        def _(sp):
            sp.dma_start(w_t[:, :, :], a["Wt_t"].rearrange("(k p) f -> p k f", p=P)).then_inc(const_in, 16)
            sp.dma_start(v["ident"][:, :], a["ident"]).then_inc(const_in, 16)
            sp.dma_start(v["p_minus"][:, :], a["p_minus"]).then_inc(const_in, 16)
            sp.dma_start(v["p_plus"][:, :], a["p_plus"]).then_inc(const_in, 16)
            sp.dma_start(v["order"][:, :], a["tile_no"].to_broadcast([P, SLOTS])).then_inc(const_in, 16)
            sp.wait_ge(zeros_ready, 1)
            sp.dma_start(t_dram[TOK:TOK + P, :], zeros[:, :]).then_inc(spare_kept, 16)
            sp.dma_start(left_dram[TOK:TOK + P, :], zeros[:, 0:D]).then_inc(spare_kept, 16)
            sp.dma_start(xn3_dram[TOK:TOK + P, :], zeros[:, 0:D]).then_inc(spare_kept, 16)
            sp.wait_ge(wmax_col_ready, 1)
            for k in range(KD):
                sp.dma_start(wmax_dram[:, k * P:(k + 1) * P].rearrange("o p -> p o"), wmax_col[:, k:k + 1])\
                  .then_inc(wmax_kept, 16)
            sp.wait_ge(wmax_kept, 16 * KD)
            sp.dma_start(wmax[:, :, :], wmax_dram.to_broadcast([P, D]).rearrange("p (k d) -> p k d", k=KD))\
              .then_inc(wmax_in, 16)
            sp.wait_ge(wmax_in, 16)
            sp.wait_ge(spare_kept, 48)

        @block.gpsimd
        def _(pool):
            pool.wait_ge(w_hi, 1)
            pool.tensor_tensor(w_rest[:, :, :], w_t[:, :, :], w_part[0][:, :, :], ALU.subtract)\
                .then_inc(w_rest_ready, 1)
            pool.wait_ge(w_mid, 1)
            pool.tensor_tensor(w_rest2[:, :, :], w_rest[:, :, :], w_part[1][:, :, :], ALU.subtract)\
                .then_inc(w_rest_ready, 1)

        @block.scalar
        def _(act):
            act.wait_ge(const_in, 80)
            act.activation(v["ident_b"][:, :], v["ident"][:, :], ACT.Copy)
            act.activation(w_part[0][:, :, :], w_t[:, :, :], ACT.Copy).then_inc(w_hi, 1)
            act.wait_ge(w_rest_ready, 1)
            act.activation(w_part[1][:, :, :], w_rest[:, :, :], ACT.Copy).then_inc(w_mid, 1)
            act.wait_ge(w_rest_ready, 2)
            act.activation(w_part[2][:, :, :], w_rest2[:, :, :], ACT.Copy).then_inc(w_split, 1)

        @block.vector
        def _(dve):
            dve.memset(zeros[:, :], 0.0).then_inc(zeros_ready, 1)
            dve.memset(v["certified"][:, :], 0.0)
            dve.wait_ge(const_in, 80)
            dve.tensor_reduce(wmax_col[:, :], w_t[:, :, :], AX.X, ALU.max).then_inc(wmax_col_ready, 1)


def plan_slots(nc, v, level):
    with ExitStack() as ctx:
        def sb(name, shape, dt=F32):
            return ctx.enter_context(nc.sbuf_tensor(f"tp{level}_{name}", shape, dt))

        def sem(name):
            return ctx.enter_context(nc.semaphore(f"tp{level}_{name}"))

        open_, is_open, key, left_key = (sb(n, [P, SLOTS]) for n in ("open", "isopen", "key", "leftkey"))
        row, no_token, no_token2 = (sb(n, [P, SLOTS]) for n in ("row", "notoken", "notoken2"))
        count, most = sb("count", [P, 1]), sb("most", [1, 1])
        certified, order, from_all, to_all, most_int = (
            v[n] for n in ("certified", "order", "from_all", "to_all", "most_int"))
        counted, count_turned = sem("counted"), sem("count_turned")
        steps = Steps(sem("steps"), 7 + 2 * (TILES // 8))
        block = ctx.enter_context(nc.Block())

        @block.tensor
        def _(pe):
            pe.wait_ge(counted, 1)
            pe.transpose(v["index"][0][0:1, 0:P], count[:, :], v["ident"][:, :]).then_inc(count_turned, 1)

        @block.vector
        def _(dve):
            def then(instruction):
                dve.wait_ge(steps.sem, steps.done(instruction))

            steps.begin(0)
            then(dve.tensor_scalar(open_[:, :], certified[:, :], -1.0, 1.0, ALU.mult, ALU.add))
            then(dve.tensor_tensor(key[:, :], open_[:, :], order[:, :], ALU.mult))
            then(dve.tensor_scalar(is_open[:, :], key[:, :], 0.0, None, ALU.is_gt))
            dve.tensor_reduce(count[:, :], is_open[:, :], AX.X, ALU.add).then_inc(counted, 1)
            src = key
            for r in range(TILES // 8):
                eight = slice(8 * r, 8 * r + 8)
                then(dve.max(order[:, eight], src[:, 0:TILES]))
                then(dve.match_replace(left_key[:, 0:TILES], order[:, eight], src[:, 0:TILES], -1.0))
                src = left_key
            dve.tensor_scalar(row[:, :], order[:, :], -1.0, float(P), ALU.add, ALU.mult)
            then(dve.tensor_scalar(no_token[:, :], order[:, :], 0.0, float(TOK + P), ALU.is_equal, ALU.mult))
            then(dve.tensor_scalar(row[:, :], row[:, :], v["p_plus"][:, :], None, ALU.add))
            dve.tensor_tensor(from_all[:, :], row[:, :], no_token[:, :], ALU.add)
            then(dve.tensor_scalar(no_token2[:, :], order[:, :], 0.0, float(TOK + 2 * P), ALU.is_equal, ALU.mult))
            dve.tensor_tensor(to_all[:, :], row[:, :], no_token2[:, :], ALU.add)
            dve.wait_ge(count_turned, 1)
            then(dve.tensor_reduce(most[:, :], v["index"][0][0:1, 0:P], AX.X, ALU.max))
            dve.tensor_scalar(most_int[:, :], most[:, :], 1.0, None, ALU.max)
            steps.end()


def tropical_level(nc, v, level, xn3_dram, left_dram, t_dram):
    resume = level > 0
    go_on = level < LEVELS - 1
    src_dram = left_dram if resume else xn3_dram
    IN = 32 if resume else 16
    OUT = 32 if go_on else 16
    GRP = 4
    CANDS = KD * CAND
    G = CANDS // GRP
    CH = 512
    assert G % 2 == 0 and CAND == 8
    with ExitStack() as ctx:
        def sb(name, shape, dt=F32):
            return ctx.enter_context(nc.sbuf_tensor(f"t{level}_{name}", shape, dt))

        def sem(name):
            return ctx.enter_context(nc.semaphore(f"t{level}_{name}"))

        x = [sb(f"x{j}", [P, KD, P]) for j in range(2)]
        left = [sb(f"left{j}", [P, KD, P]) for j in range(2)]
        t_in = [sb(f"tin{j}", [P, FFN]) for j in range(2)]
        top = [sb(f"top{j}", [P, KD, CAND]) for j in range(2)]
        place = sb("place", [P, KD, CAND], mybir.dt.uint32)
        cand = [sb(f"cand{j}", [P, KD * CAND], BF16) for j in range(2)]
        bounds, bound = sb("bounds", [P, KD * P]), [sb(f"bound{j}", [P, 1]) for j in range(2)]
        dist = [sb(f"dist{b}", [P, GRP * P]) for b in range(2)]
        one_hot = [sb(f"onehot{b}", [P, GRP * P], BF16) for b in range(2)]
        least, pause = sb("least", [P, 1]), sb("pause", [1, 3])
        pool_pause, pool_zero = sb("poolpause", [1, 4]), sb("poolzero", [1, 1])
        from_now = [sb(f"fromnow{j}", [P, 1], mybir.dt.int32) for j in range(2)]
        to_now = [sb(f"tonow{j}", [P, 1], mybir.dt.int32) for j in range(2)]
        certified, ident_b, w_part, wmax, acc, t_out, index, fetched, most_int = (
            v[n] for n in ("certified", "ident_b", "w_part", "wmax", "acc", "t_out", "index", "fetched", "most_int"))
        rows_in = [sem(f"rows_in{j}") for j in range(2)]
        rows_out = [sem(f"rows_out{j}") for j in range(2)]
        written = [sem(f"written{j}") for j in range(2)]
        selected, index_ready, dist_ready, one_hot_ready = (
            sem(n) for n in ("selected", "index_ready", "dist_ready", "one_hot_ready"))
        fetched_ready, fetched_used, merged, least_ready = (
            sem(n) for n in ("fetched_ready", "fetched_used", "merged", "least_ready"))
        numbers_ready, zero_ready = sem("numbers_ready"), sem("zero_ready")
        select_steps = Steps(sem("select_steps"), 2)
        block = ctx.enter_context(nc.Block())

        def slot_pairs(eng, body):
            slots = eng.value_load(most_int[0:1, 0:1], min_val=1, max_val=TILES)
            with eng.Fori(0, slots, 2) as i:
                body(i)

        @block.gpsimd
        def _(pool):
            def gather(j):
                at = bass.IndirectOffsetOnAxis(from_now[j][:, 0:1], 0)
                pool.indirect_dma_start(x[j][:, :, :].rearrange("p k d -> p (k d)"), None, src_dram[0:TOK + P, :], at)\
                    .then_inc(rows_in[j], 16)
                if resume:
                    pool.indirect_dma_start(t_in[j][:, :], None, t_dram[0:TOK + P, :], at).then_inc(rows_in[j], 16)

            def held(k, sem_, value):
                pool.wait_ge(sem_, value)
                return pool.tensor_tensor(pool_pause[:, k:k + 1], pool_zero[:, :], pool_zero[:, :], ALU.add)

            pool.memset(pool_zero[:, :], 0.0).then_inc(zero_ready, 1)
            for j in range(2):
                pool.tensor_copy(from_now[j][:, :], v["from_all"][:, j:j + 1]).then_inc(numbers_ready, 1)
            pool.wait_ge(zero_ready, 1)
            pool.wait_ge(numbers_ready, 2)
            for j in range(2):
                gather(j)

            def body(i):
                for j in range(2):
                    held(0, merged, i + j + 1)
                    pool.tensor_copy(to_now[j][:, :], v["to_all"][:, ds(i + j, 1)])
                    pool.tensor_copy(from_now[j][:, :], v["from_all"][:, ds(i + j + 2, 1)]).then_inc(numbers_ready, 1)
                    held(1, numbers_ready, i + j + 3)
                    at = bass.IndirectOffsetOnAxis(to_now[j][:, 0:1], 0)
                    pool.indirect_dma_start(t_dram, at, t_out[j][:, :], None).then_inc(rows_out[j], 16)
                    if go_on:
                        pool.indirect_dma_start(left_dram, at, left[j][:, :, :].rearrange("p k d -> p (k d)"), None)\
                            .then_inc(rows_out[j], 16)
                    gather(j)
                    held(2, rows_out[j], (i + 2) * (OUT // 2))
                    held(3, rows_in[j], (i + 4) * (IN // 2)).then_inc(written[j], 2)
                    pool.wait_ge(written[j], i + 4)

            slot_pairs(pool, body)

        @block.scalar
        def _(act):
            def turn_hot(g, b):
                act.wait_ge(index_ready, g + 1)
                act.activation(dist[b][:, :], index[b][:, :], ACT.Abs, bias=v["p_minus"][:, :]).then_inc(dist_ready, 1)
                act.wait_ge(dist_ready, g + 1)
                act.activation(one_hot[b][:, :], dist[b][:, :], ACT.Relu, scale=-1.0, bias=1.0)\
                   .then_inc(one_hot_ready, 1)

            def body(i):
                for g in range(2 * G):
                    turn_hot(i * G + g, g % 2)

            slot_pairs(act, body)

        @block.tensor
        def _(pe):
            def spread(s, j, g):
                pe.wait_ge(selected, s + 1)
                for c in range(GRP):
                    one = cand[j][:, g * GRP + c:g * GRP + c + 1].to_broadcast([P, P])
                    mm = pe.matmul(index[g % 2][:, c * P:(c + 1) * P], one, ident_b[:, :], start=True, stop=True)
                mm.then_inc(index_ready, 1)

            def fetch(s, j, g):
                k = g * GRP // CAND
                pe.wait_ge(one_hot_ready, s * G + g + 1)
                for c in range(GRP):
                    buf, ago = ring(j * CANDS + g * GRP + c)
                    pe.wait_ge(fetched_used, s * CANDS + g * GRP + c + 1 + RING - ago)
                    for h in range(FFN // CH):
                        for part in range(3):
                            mm = pe.matmul(fetched[buf][:, h * CH:(h + 1) * CH],
                                           one_hot[g % 2][:, c * P:(c + 1) * P],
                                           w_part[part][:, k, h * CH:(h + 1) * CH],
                                           start=(part == 0), stop=(part == 2))
                    mm.then_inc(fetched_ready, 1)

            def body(i):
                for j in range(2):
                    for g in range(G):
                        if g < G - 1:
                            spread(i + j, j, g + 1)
                        else:
                            spread(i + j + 1, 1 - j, 0)
                        fetch(i + j, j, g)

            spread(0, 0, 0)
            slot_pairs(pe, body)

        @block.vector
        def _(dve):
            dve.sem_inc(fetched_used, RING)
            for j in range(2):
                dve.sem_inc(written[j], 2)
            dve.memset(certified[:, :], 0.0)

            def select(s, j, rows, free, stage):
                def held(n, sem_, value):
                    dve.wait_ge(sem_, value)
                    dve.memset(pause[:, n:n + 1], 0.0)

                if stage == 0:
                    select_steps.begin(s)
                    held(0, rows_in[j], rows)
                    for k in range(KD):
                        last = dve.max(top[j][:, k, :], x[j][:, k, :])
                    return select_steps.done(last)
                elif stage == 1:
                    select_steps.begin(s)
                    held(1, select_steps.sem, select_steps.base + 1)
                    held(2, written[j], free)
                    for k in range(KD):
                        dve.max_index(place[:, k, :], top[j][:, k, :], x[j][:, k, :])
                        last = dve.match_replace(left[j][:, k, :], top[j][:, k, :], x[j][:, k, :], LOWEST)
                    last.then_inc(select_steps.sem, 1)
                else:
                    select_steps.begin(s)
                    dve.wait_ge(select_steps.sem, select_steps.base + 2)
                    dve.tensor_copy(cand[j][:, :], place[:, :, :].rearrange("p k c -> p (k c)"))
                    dve.tensor_tensor_reduce(bounds[:, :], left[j][:, :, :].rearrange("p k d -> p (k d)"),
                                             wmax[:, :, :].rearrange("p k d -> p (k d)"), 1.0, LOWEST,
                                             ALU.add, ALU.max, bound[j][:, :]).then_inc(selected, 1)

            def use(s, j, c):
                q, r = s * CANDS + c, c % 2
                column = fetched[ring(j * CANDS + c)[0]]
                value = top[j][:, c // CAND, c % CAND:c % CAND + 1]
                dve.wait_ge(fetched_ready, q + 1)
                if c >= 2 or (c == 0 and resume):
                    dve.wait_ge(fetched_used, q + RING - 1)
                    op = dve.scalar_tensor_tensor(acc[r][:, :], column[:, :], value,
                                                  (t_in[j] if c == 0 else acc[r])[:, :], ALU.add, ALU.max)
                else:
                    op = dve.tensor_scalar(acc[r][:, :], column[:, :], value, None, ALU.add)
                op.then_inc(fetched_used, 1)

            def body(i):
                for j in range(2):
                    s = i + j
                    for c in range(CANDS):
                        use(s, j, c)
                        if c in (5, 7, 9):
                            select(s + 1, 1 - j, (i + 2 * j + 2) * (IN // 2), i + 2 * j + 2, (c - 5) // 2)
                    dve.wait_ge(fetched_used, (s + 1) * CANDS + RING)
                    dve.wait_ge(written[j], i + 2)
                    dve.tensor_tensor(t_out[j][:, :], acc[0][:, :], acc[1][:, :], ALU.max).then_inc(merged, 1)
                    dve.wait_ge(merged, s + 1)
                    dve.tensor_reduce(least[:, :], t_out[j][:, :], AX.X, ALU.min).then_inc(least_ready, 1)
                    dve.wait_ge(least_ready, s + 1)
                    dve.tensor_tensor(certified[:, ds(s, 1)], bound[j][:, :], least[:, :], ALU.is_lt)

            for stage in range(3):
                select(0, 0, IN, 2, stage)
            slot_pairs(dve, body)


def tropical_general(nc, v, xn3_dram, t_dram):
    CH = 512
    RUN = 32
    with ExitStack() as ctx:
        def sb(name, shape, dt=F32):
            return ctx.enter_context(nc.sbuf_tensor(name, shape, dt))

        def sem(name):
            return ctx.enter_context(nc.semaphore("tg_" + name))

        x_slot = sb("tg_x", [P, D])
        from_now, to_now = (sb(f"tg_{n}now", [P, 1], mybir.dt.int32) for n in ("from", "to"))
        pool_pause, pool_zero = sb("tg_poolpause", [1, 3]), sb("tg_poolzero", [1, 1])
        ident_b, w_part, acc, t_out, fetched, most_int = (
            v[n] for n in ("ident_b", "w_part", "acc", "t_out", "fetched", "most_int"))
        zero_ready, slot_ready, rows_in, dense_ready, dense_used, merged, rows_out, slot_free = (
            sem(n) for n in ("zero_ready", "slot_ready", "rows_in", "dense_ready", "dense_used", "merged",
                             "rows_out", "slot_free"))
        block = ctx.enter_context(nc.Block())

        @block.gpsimd
        def _(pool):
            def held(k, sem_, value):
                pool.wait_ge(sem_, value)
                return pool.tensor_tensor(pool_pause[:, k:k + 1], pool_zero[:, :], pool_zero[:, :], ALU.add)

            pool.memset(pool_zero[:, :], 0.0).then_inc(zero_ready, 1)
            pool.wait_ge(zero_ready, 1)
            slots = pool.value_load(most_int[0:1, 0:1], min_val=1, max_val=TILES)
            with pool.Fori(0, slots) as s:
                held(0, slot_ready, s + 1)
                pool.indirect_dma_start(x_slot[:, :], None, xn3_dram,
                                        bass.IndirectOffsetOnAxis(from_now[:, 0:1], 0)).then_inc(rows_in, 16)
                held(1, merged, s + 1)
                pool.indirect_dma_start(t_dram, bass.IndirectOffsetOnAxis(to_now[:, 0:1], 0),
                                        t_out[0][:, :], None).then_inc(rows_out, 16)
                held(2, rows_out, 16 * s + 16).then_inc(slot_free, 1)

        @block.tensor
        def _(pe):
            slots = pe.value_load(most_int[0:1, 0:1], min_val=1, max_val=TILES)
            with pe.Fori(0, slots) as s:
                for k in range(KD):
                    with pe.Fori(0, P // RUN) as run:
                        for c in range(RUN):
                            buf, ago = ring(c)
                            pe.wait_ge(dense_used, s * D + k * P + RUN * run + c + 1 + RING - ago)
                            one_row = ident_b[:, ds(RUN * run + c, 1)].to_broadcast([P, P])
                            for h in range(FFN // CH):
                                for part in range(3):
                                    mm = pe.matmul(fetched[buf][:, h * CH:(h + 1) * CH], one_row,
                                                   w_part[part][:, k, h * CH:(h + 1) * CH],
                                                   start=(part == 0), stop=(part == 2))
                            mm.then_inc(dense_ready, 1)

        @block.vector
        def _(dve):
            dve.sem_inc(dense_used, RING)
            dve.sem_inc(slot_free, 1)
            slots = dve.value_load(most_int[0:1, 0:1], min_val=1, max_val=TILES)

            def use(s, k, run, c):
                d, r, row = RUN * run + c, c % 2, fetched[ring(c)[0]]
                q = s * D + k * P + d
                dve.wait_ge(dense_ready, q + 1)
                if isinstance(d, int) and k == 0 and d < 2:
                    op = dve.tensor_scalar(acc[r][:, :], row[:, :], x_slot[:, d:d + 1], None, ALU.add)
                else:
                    dve.wait_ge(dense_used, q + RING - 1)
                    op = dve.scalar_tensor_tensor(acc[r][:, :], row[:, :], x_slot[:, ds(k * P + d, 1)],
                                                  acc[r][:, :], ALU.add, ALU.max)
                op.then_inc(dense_used, 1)

            with dve.Fori(0, slots) as s:
                dve.wait_ge(slot_free, s + 1)
                dve.tensor_copy(from_now[:, :], v["from_all"][:, ds(s, 1)])
                dve.tensor_copy(to_now[:, :], v["to_all"][:, ds(s, 1)]).then_inc(slot_ready, 1)
                dve.wait_ge(rows_in, 16 * s + 16)
                for c in range(RUN):
                    use(s, 0, 0, c)
                with dve.Fori(1, P // RUN) as run:
                    for c in range(RUN):
                        use(s, 0, run, c)
                with dve.Fori(0, P // RUN) as run:
                    for c in range(RUN):
                        use(s, 1, run, c)
                dve.wait_ge(dense_used, s * D + D + RING)
                dve.tensor_tensor(t_out[0][:, :], acc[0][:, :], acc[1][:, :], ALU.max).then_inc(merged, 1)


def stage_ffn(nc, a, x3t_dram, xn3t_dram, t_dram, out):
    CB = 512
    BLOCKS = TOK // CB
    with ExitStack() as ctx:
        def sb(name, shape, dt=F32):
            return ctx.enter_context(nc.sbuf_tensor(name, shape, dt))

        def ps(name):
            return ctx.enter_context(nc.psum_tensor(name, [P, CB], F32))

        def sem(name):
            return ctx.enter_context(nc.semaphore(name))

        def sems(*names):
            return [sem("f_" + n) for n in names]

        w_c = sb("f_wc", [P, KD, FFN])
        w_g = sb("f_wg", [P, KD, FFN])
        w_d = sb("f_wd", [P, FT, D])
        slope = [sb(f"f_slope{s}", [P, FT, PIECES]) for s in range(2)]
        offset = [sb(f"f_offset{s}", [P, FT, PIECES]) for s in range(2)]
        shift = [sb(f"f_shift{s}", [P, FT, PIECES]) for s in range(2)]
        b_t, b_c, b_g = sb("f_bt", [P, FT]), sb("f_bc", [P, FT]), sb("f_bg", [P, FT])
        alpha = sb("f_alpha", [P, FT])
        b_d = sb("f_bd", [P, KD])
        half_bg = sb("f_half_bg", [P, FT])
        tanh_a = sb("f_tanh_a", [P, FT])
        share = [sb(f"f_share{s}", [P, FT]) for s in range(2)]
        x3 = [sb(f"f_x3{j}", [P, KD, CB]) for j in range(2)]
        x = [sb(f"f_x{j}", [P, KD, CB]) for j in range(2)]
        t = [sb(f"f_t{j}", [P, CB // P, FFN]) for j in range(2)]
        ident = sb("f_ident", [P, P])
        lines = [[sb(f"f_lines{v}{s}", [P, PIECES, CB]) for s in range(2)] for v in range(2)]
        cls = [sb(f"f_cls{v}", [P, CB]) for v in range(2)]
        th = [sb(f"f_th{v}", [P, CB]) for v in range(2)]
        convex = sb("f_convex", [P, CB])
        trop = [sb(f"f_trop{v}", [P, CB]) for v in range(2)]
        diff = [sb(f"f_diff{v}", [P, CB]) for v in range(2)]
        gated = [sb(f"f_gated{v}", [P, CB]) for v in range(2)]
        fused = [sb(f"f_fused{v}", [P, CB]) for v in range(2)]
        o_b = sb("f_ob", [P, KD, CB])
        o_x = [sb(f"f_ox{j}", [P, KD, CB]) for j in range(2)]
        ps_c = [ps(f"f_psc{v}") for v in range(2)]
        ps_g = [ps(f"f_psg{v}") for v in range(2)]
        ps_t = [ps(f"f_pst{v}") for v in range(2)]
        ps_o = [ps(f"f_pso{k}") for k in range(KD)]

        const_in, consts_ready = sems("const_in", "consts_ready")
        shift_ready, t_turned = sems("shift_ready", "t_turned")
        block_in = sems("block_in0", "block_in1")
        stored = sems("stored0", "stored1")
        c_done, g_done, cls_ready, th_ready = sems("c_done", "g_done", "cls_ready", "th_ready")
        lines_ready = sems("convex_lines_ready", "concave_lines_ready")
        trop_ready, diff_ready, gated_ready, fused_ready = sems("trop_ready", "diff_ready", "gated_ready", "fused_ready")
        fused_used, ob_ready, ox_ready = sems("fused_used", "ob_ready", "ox_ready")
        dve_steps = Steps(sem("f_dve_steps"), 7)

        block = ctx.enter_context(nc.Block())
        PIECE_CONSTS = ((slope[0], "sl_cvx"), (offset[0], "of_cvx"), (slope[1], "sl_ccv"), (offset[1], "of_ccv"))
        VECTORS = ((b_t, "bt"), (b_c, "bc"), (b_g, "bg"), (alpha, "alpha"), (b_d, "bd"))
        CONSTS = 4 + len(PIECE_CONSTS) + len(VECTORS)

        def rounds(eng, body):
            for j in range(2):
                body(0, j, j, True)
            with eng.Fori(1, BLOCKS // 2) as i:
                for j in range(2):
                    body(i, j, 2 * i + j, False)

        @block.sync
        def _(sp):
            sp.dma_start(w_c[:, :, :], a["Wc"].rearrange("(k p) f -> p k f", p=P)).then_inc(const_in, 16)
            sp.dma_start(w_g[:, :, :], a["Wg"].rearrange("(k p) f -> p k f", p=P)).then_inc(const_in, 16)
            sp.dma_start(w_d[:, :, :], a["Wd"].rearrange("(t p) d -> p t d", p=P)).then_inc(const_in, 16)
            sp.dma_start(ident[:, :], a["ident"]).then_inc(const_in, 16)
            for dst, name in PIECE_CONSTS:
                sp.dma_start(dst[:, :, :], a[name].rearrange("(t p) q -> p t q", p=P)).then_inc(const_in, 16)
            for dst, name in VECTORS:
                sp.dma_start(dst[:, :], a[name]).then_inc(const_in, 16)

            def load(m, j):
                sp.dma_start(x[j][:, :, :], xn3t_dram[:, :, ds(m * CB, CB)].rearrange("k p t -> p k t"))\
                  .then_inc(block_in[j], 16)
                sp.dma_start(x3[j][:, :, :], x3t_dram[:, :, ds(m * CB, CB)].rearrange("k p t -> p k t"))\
                  .then_inc(block_in[j], 16)
                sp.dma_start(t[j][:, :, :], t_dram[ds(m * CB, CB), :].rearrange("(g p) f -> p g f", p=P))\
                  .then_inc(block_in[j], 16)

            def store(m, j):
                sp.wait_ge(ox_ready, m + 1)
                sp.dma_start(out[:, :, ds(m * CB, CB)].rearrange("k p t -> p k t"), o_x[j][:, :, :])\
                  .then_inc(stored[j], 16)

            for j in range(2):
                load(j, j)
            with sp.Fori(0, BLOCKS // 2 - 1) as i:
                for j in range(2):
                    store(2 * i + j, j)
                    load(2 * i + j + 2, j)
            for j in range(2):
                store(BLOCKS - 2 + j, j)
            for j in range(2):
                sp.wait_ge(stored[j], 16 * (BLOCKS // 2) + 16)

        @block.gpsimd
        def _(pool):
            def body(i, j, m, first):
                for u in range(FT):
                    v, q = u % 2, m * FT + u
                    pool.wait_ge(cls_ready, q + 1)
                    pool.wait_ge(trop_ready, q + 1)
                    pool.tensor_tensor(diff[v][:, :], trop[v][:, :], cls[v][:, :], ALU.subtract).then_inc(diff_ready, 1)
                    if u == 3 and not (first and j == 0):
                        total(m - 1, 1 - j, i if j else i - 1)

            def total(m, j, i):
                pool.wait_ge(stored[j], 16 * i + 16)
                pool.wait_ge(ob_ready, m + 1)
                pool.tensor_tensor(o_x[j][:, :, :], o_b[:, :, :], x3[j][:, :, :], ALU.add).then_inc(ox_ready, 1)

            for j in range(2):
                pool.sem_inc(stored[j], 16)
            rounds(pool, body)
            total(BLOCKS - 1, 1, BLOCKS // 2 - 1)

        @block.scalar
        def _(act):
            act.wait_ge(const_in, 16 * CONSTS)
            act.activation(tanh_a[:, :], alpha[:, :], ACT.Tanh, scale=0.5).then_inc(consts_ready, 1)
            act.activation(half_bg[:, :], b_g[:, :], ACT.Copy, scale=0.5).then_inc(consts_ready, 1)
            act.wait_ge(consts_ready, 2)
            act.wait_ge(shift_ready, 4 * FT)

            def body(i, j, m, first):
                act.wait_ge(block_in[j], 48 * (i + 1))
                for u in range(FT):
                    v, q = u % 2, m * FT + u
                    if not (first and j == 0 and u < 2):
                        act.wait_ge(trop_ready, q - 1)
                    act.wait_ge(t_turned, q + 1)
                    for s in range(2):
                        for n in range(PIECES):
                            last = act.activation(lines[v][s][:, n, :], ps_t[v][:, :], ACT.Identity,
                                                  scale=slope[s][:, u, n:n + 1], bias=shift[s][:, u, n:n + 1])
                        last.then_inc(lines_ready[s], 1)
                    act.wait_ge(c_done, q + 1)
                    if not (first and j == 0 and u < 2):
                        act.wait_ge(fused_ready, q - 1)
                    act.activation(cls[v][:, :], ps_c[v][:, :], ACT.Gelu, bias=b_c[:, u:u + 1]).then_inc(cls_ready, 1)
                    act.wait_ge(g_done, q + 1)
                    act.activation(th[v][:, :], ps_g[v][:, :], ACT.Tanh, scale=0.5, bias=half_bg[:, u:u + 1])\
                       .then_inc(th_ready, 1)
                    if u == 1 and not (first and j == 0):
                        finish(m - 1)

            def finish(m):
                act.wait_ge(fused_used, (m + 1) * FT)
                wait_past(act, ox_ready, m)
                for k in range(KD):
                    last = act.activation(o_b[:, k, :], ps_o[k][:, :], ACT.Identity, bias=b_d[:, k:k + 1])
                last.then_inc(ob_ready, 1)

            rounds(act, body)
            finish(BLOCKS - 1)

        @block.tensor
        def _(pe):
            pe.wait_ge(const_in, 16 * CONSTS)

            def output_part(m, u, early):
                v, q = u % 2, m * FT + u
                if u == 0 and not early:
                    pe.wait_ge(ob_ready, m)
                pe.wait_ge(fused_ready, q + 1)
                for k in range(KD):
                    mm = pe.matmul(ps_o[k][:, :], w_d[:, u, k * P:(k + 1) * P], fused[v][:, :],
                                   start=(u == 0), stop=(u == FT - 1))
                mm.then_inc(fused_used, 1)

            def products(j, u, q, early):
                v = u % 2
                if not early:
                    pe.wait_ge(lines_ready[1], q - 1)
                for g in range(CB // P):
                    mm = pe.transpose(ps_t[v][:, g * P:(g + 1) * P], t[j][:, g, u * P:(u + 1) * P], ident[:, :])
                mm.then_inc(t_turned, 1)
                for ps_, w_, done, read in ((ps_c, w_c, c_done, cls_ready), (ps_g, w_g, g_done, th_ready)):
                    if not early:
                        pe.wait_ge(read, q - 1)
                    for k in range(KD):
                        mm = pe.matmul(ps_[v][:, :], w_[:, k, u * P:(u + 1) * P], x[j][:, k, :],
                                       start=(k == 0), stop=(k == KD - 1))
                    mm.then_inc(done, 1)

            def body(i, j, m, first, last=False):
                for u in range(FT):
                    q = m * FT + u
                    if u < FT - 1:
                        products(j, u + 1, q + 1, first and j == 0 and u == 0)
                    elif not last:
                        pe.wait_ge(block_in[1 - j], 48 * (i + j + 1))
                        products(1 - j, 0, q + 1, False)
                    if u > 0:
                        output_part(m, u - 1, first and j == 0)
                    elif not (first and j == 0):
                        output_part(m - 1, FT - 1, False)

            pe.wait_ge(block_in[0], 48)
            products(0, 0, 0, True)
            for j in range(2):
                body(0, j, j, True)
            with pe.Fori(1, BLOCKS // 2 - 1) as i:
                for j in range(2):
                    body(i, j, 2 * i + j, False)
            for j in range(2):
                body(BLOCKS // 2 - 1, j, BLOCKS - 2 + j, False, j == 1)
            output_part(BLOCKS - 1, FT - 1, False)

        @block.vector
        def _(dve):
            dve.wait_ge(const_in, 16 * CONSTS)
            for s in range(2):
                for u in range(FT):
                    dve.tensor_scalar(shift[s][:, u, :], slope[s][:, u, :], b_t[:, u:u + 1], None, ALU.mult)\
                       .then_inc(shift_ready, 1)
            dve.wait_ge(shift_ready, 2 * FT)
            for s in range(2):
                for u in range(FT):
                    dve.tensor_tensor(shift[s][:, u, :], shift[s][:, u, :], offset[s][:, u, :], ALU.add)\
                       .then_inc(shift_ready, 1)
            dve.wait_ge(consts_ready, 2)
            dve.tensor_scalar(share[0][:, :], tanh_a[:, :], 0.5, 0.5, ALU.mult, ALU.add).then_inc(consts_ready, 1)
            dve.tensor_scalar(share[1][:, :], tanh_a[:, :], -0.5, 0.5, ALU.mult, ALU.add).then_inc(consts_ready, 1)
            dve.wait_ge(consts_ready, 4)

            def fuse(m, u, peeled):
                v, q = u % 2, m * FT + u
                dve.wait_ge(diff_ready, q + 1)
                dve.wait_ge(th_ready, q + 1)
                dve.scalar_tensor_tensor(gated[v][:, :], th[v][:, :], 1.0, diff[v][:, :], ALU.add, ALU.mult)\
                   .then_inc(gated_ready, 1)
                dve.wait_ge(gated_ready, q + 1)
                if not peeled:
                    dve.wait_ge(fused_used, q - 1)
                dve.scalar_tensor_tensor(fused[v][:, :], gated[v][:, :], 0.5, cls[v][:, :], ALU.mult, ALU.add)\
                   .then_inc(fused_ready, 1)

            def body(i, j, m, first):
                for u in range(FT):
                    v, q = u % 2, m * FT + u
                    dve_steps.begin(q)
                    for s, op in ((0, ALU.max), (1, ALU.min)):
                        dve.wait_ge(lines_ready[s], q + 1)
                        l = lines[v][s]
                        for n in (4, 2, 1):
                            w = dve_steps.done(dve.tensor_tensor(l[:, 0:n, :], l[:, 0:n, :], l[:, n:2 * n, :], op))
                            dve.wait_ge(dve_steps.sem, w)
                    w = dve_steps.done(dve.tensor_scalar(convex[:, :], lines[v][0][:, 0, :], share[0][:, u:u + 1],
                                                         None, ALU.mult))
                    dve.wait_ge(dve_steps.sem, w)
                    dve.scalar_tensor_tensor(trop[v][:, :], lines[v][1][:, 0, :], share[1][:, u:u + 1], convex[:, :],
                                             ALU.mult, ALU.add).then_inc(trop_ready, 1)
                    dve_steps.end()
                    if u > 0:
                        fuse(m, u - 1, first and j == 0 and u < 3)
                    elif not (first and j == 0):
                        fuse(m - 1, FT - 1, False)

            rounds(dve, body)
            fuse(BLOCKS - 1, FT - 1, False)


def full_kernel(nc, a, out):
    x1_dram = nc.dram_tensor("x1_kept", [B, N, D], F32, kind="Internal").ap()
    x3t_dram = nc.dram_tensor("x3_transposed", [KD, P, TOK], F32, kind="Internal").ap()
    xn3t_dram = nc.dram_tensor("x3_normalised_transposed", [KD, P, TOK], F32, kind="Internal").ap()
    xn3_dram = nc.dram_tensor("x3_normalised", [TOK + P, D], F32, kind="Internal").ap()
    left_dram = nc.dram_tensor("x3_normalised_left", [TOK + 2 * P, D], F32, kind="Internal").ap()
    t_dram = nc.dram_tensor("t", [TOK + 2 * P, FFN], F32, kind="Internal").ap()
    wmax_dram = nc.dram_tensor("Wt_maxima", [1, D], F32, kind="Internal").ap()
    with ExitStack() as ctx:
        hx = ctx.enter_context(nc.sbuf_tensor("hx", [P, KD, 1 + N, B], F32))
        stage_gnn0(nc, a, hx, x1_dram)
        stage_lstm(nc, a, hx)
        stage_gnn1(nc, a, hx, x1_dram, x3t_dram, xn3t_dram, xn3_dram)
    stage_tropical(nc, a, xn3_dram, left_dram, t_dram, wmax_dram)
    stage_ffn(nc, a, x3t_dram, xn3t_dram, t_dram, out)


def kernel(**inputs):
    import concourse.bacc as bacc
    from concourse.bass_utils import run_bass_kernel_spmd

    given = {k: np.asarray(v) for k, v in inputs.items()}

    def gates_first_g(w):
        i, f, g, o = np.split(w, GATES, axis=0)
        return np.ascontiguousarray(np.concatenate([g, i, f, o], axis=0))

    def turned(w):
        return np.ascontiguousarray(w.T)

    def columns(v):
        return np.ascontiguousarray(v.reshape(-1, P).T)

    which = np.zeros((2, 2, 2, 4 * B), np.float32)
    which[:, 0, 0], which[:, 1, 1] = 1.0, 1.0
    ones = np.ones((P, P), np.float32)
    arrays = {
        "x": given["x"], "adj": given["adj"],
        "adjt": np.ascontiguousarray(given["adj"].transpose(0, 2, 1)),
        "theta": given["L0_gnn_theta"], "W_h": given["L0_gnn_W_h"], "W_t": given["L0_gnn_W_t"],
        "b_t": given["L0_gnn_b_t"].reshape(1, D),
        "w_ih_t": turned(gates_first_g(given["L0_ffn_W_ih"])),
        "w_hh_t": turned(gates_first_g(given["L0_ffn_W_hh"])),
        "b_ih": gates_first_g(given["L0_ffn_b_ih"]), "b_hh": gates_first_g(given["L0_ffn_b_hh"]),
        "w_lin_t": turned(given["L0_ffn_W_lin"]), "b_lin": given["L0_ffn_b_lin"].reshape(1, 2),
        "fw_att": given["L0_ffn_fw_att"], "bw_att": given["L0_ffn_bw_att"],
        "W1": given["L1_gnn_W"], "b1": given["L1_gnn_b"].reshape(1, D),
        "Wt_t": turned(given["L1_ffn_Wt"]), "Wc": given["L1_ffn_Wc"], "Wg": given["L1_ffn_Wg"], "Wd": given["L1_ffn_Wd"],
        "sl_cvx": given["L1_ffn_sl_cvx"], "of_cvx": given["L1_ffn_of_cvx"],
        "sl_ccv": given["L1_ffn_sl_ccv"], "of_ccv": given["L1_ffn_of_ccv"],
        "bt": columns(given["L1_ffn_bt"]), "bc": columns(given["L1_ffn_bc"]), "bg": columns(given["L1_ffn_bg"]),
        "alpha": columns(given["L1_ffn_alpha"]), "bd": columns(given["L1_ffn_bd"]),
        "ident": np.eye(P, dtype=np.float32),
        "before": np.triu(ones, 1), "after": np.tril(ones, -1), "which": which.reshape(4, 2 * 4 * B),
    }
    numbers = np.arange(P, dtype=np.float32)[:, None]
    tile_no = np.zeros((1, SLOTS), np.float32)
    tile_no[0, :TILES] = np.arange(1, TILES + 1)
    arrays |= {"p_plus": numbers, "p_minus": -numbers, "tile_no": tile_no}
    nc = bacc.Bacc("TRN2", target_bir_lowering=False, num_devices=1)
    a = {k: nc.dram_tensor(f"in_{k}", v.shape, mybir.dt.from_np(v.dtype), kind="ExternalInput").ap()
         for k, v in arrays.items()}
    out = nc.dram_tensor("out_t", [KD, P, TOK], F32, kind="ExternalOutput").ap()
    full_kernel(nc, a, out)
    r = run_bass_kernel_spmd(nc, [{f"in_{k}": v for k, v in arrays.items()}], core_ids=[0])
    out_t = np.asarray(r.results[0]["out_t"]).reshape(D, TOK)
    return np.ascontiguousarray(out_t.T).reshape(B, N, D)
```
